# Optimizing a Trainium2 kernel written in Bass

```python
import numpy as np
import jax
import jax.numpy as jnp

def _softmax(x, axis=-1):
    return jax.nn.softmax(x, axis=axis)

def _gelu(x):
    return jax.nn.gelu(x, approximate=True)

def _silu(x):
    return jax.nn.silu(x)

def _sigmoid(x):
    return jax.nn.sigmoid(x)

def _layernorm(x, axis=-1, eps=1e-05):
    m = jnp.mean(x, axis=axis, keepdims=True)
    v = jnp.var(x, axis=axis, keepdims=True)
    return (x - m) / jnp.sqrt(v + eps)

def _scatter_add(tgt, idx, src, axis=0):
    return tgt.at[idx].add(src)

def _segment_sum(src, seg, n):
    return jax.ops.segment_sum(src, seg, n)
kernel_name = 'mk_adj_seq_d4_adj_r2_3fea8d'

def setup_inputs(seed: int=0):
    np.random.seed(seed)
    _w = jnp.asarray

    def _rec_inputs():
        import jax
        import jax.numpy as jnp
        _gk = jax.random.key(seed)
        x = -0.0005207 + 1.001 * jax.random.normal(jax.random.fold_in(_gk, 1), (8, 1024, 256), jnp.float32)
        _a = jax.random.bernoulli(jax.random.fold_in(_gk, 2), 0.0078125, (8, 1024, 1024))
        _a = jnp.logical_or(_a, jnp.eye(1024, dtype=bool))
        adj = _a.astype(jnp.int32)
        return (x, adj)
    x, adj = _rec_inputs()

    def _L0_gnn_setup():
        import jax, jax.numpy as jnp
        import numpy as np
        B, S, D, H = (2, 1024, 256, 8)
        HD = D // H
        EPS = 1e-05

        def _ln(x, g, b):
            mu = jnp.mean(x, axis=-1, keepdims=True)
            var = jnp.mean((x - mu) ** 2, axis=-1, keepdims=True)
            return (x - mu) * jax.lax.rsqrt(var + EPS) * g + b
        key = jax.random.key(seed)
        ks = jax.random.split(key, 16)
        x = jax.random.normal(ks[0], (B, S, D), dtype=jnp.float32)
        adj = jax.random.randint(ks[1], (B, S, S), 0, 2, dtype=jnp.int32)
        adj = adj.at[:, jnp.arange(S), jnp.arange(S)].set(1)
        edge_attr = jax.random.normal(ks[2], (B, S, S), dtype=jnp.float32)
        sc = 1.0 / np.sqrt(D)
        p = lambda k, shp: jax.random.normal(k, shp, dtype=jnp.float32) * sc
        return {'x': x, 'adj_matrix': adj, 'edge_attr_matrix': edge_attr, 'ln1_g': jnp.ones((D,)), 'ln1_b': jnp.zeros((D,)), 'ln2_g': jnp.ones((D,)), 'ln2_b': jnp.zeros((D,)), 'wq': p(ks[3], (D, D)), 'bq': jnp.zeros((D,)), 'wk': p(ks[4], (D, D)), 'bk': jnp.zeros((D,)), 'wv': p(ks[5], (D, D)), 'bv': jnp.zeros((D,)), 'wo': p(ks[6], (D, D)), 'bo': jnp.zeros((D,)), 'w1': p(ks[7], (D, 4 * D)), 'b1': jnp.zeros((4 * D,)), 'w2': p(ks[8], (4 * D, D)), 'b2': jnp.zeros((D,))}
    _L0_gnn_all = _L0_gnn_setup()
    _L0_gnn_in = {k: v for k, v in _L0_gnn_all.items() if k in ('ln1_g', 'ln1_b', 'ln2_g', 'ln2_b', 'wq', 'bq', 'wk', 'bk', 'wv', 'bv', 'wo', 'bo', 'w1', 'b1', 'w2', 'b2')}
    del _L0_gnn_all

    def _L1_gnn_setup():
        import jax, jax.numpy as jnp
        import numpy as np
        EPSILON = 1e-13
        LN_EPS = 1e-05
        DIRECTIONS = 2
        HID = 256

        def _layer_norm(x, gamma, beta):
            mu = jnp.mean(x, axis=-1, keepdims=True)
            var = jnp.mean(jnp.square(x - mu), axis=-1, keepdims=True)
            return (x - mu) * jax.lax.rsqrt(var + LN_EPS) * gamma + beta
        key = jax.random.key(seed)
        k1, k2, k3, k4 = jax.random.split(key, 4)
        B, N, D = (16, 512, HID)
        adj = jax.random.randint(k1, (B, N, N), 0, 3, dtype=jnp.int32)
        hid = jax.random.normal(k2, (B, N, D), dtype=jnp.float32)
        W = jax.random.normal(k3, (DIRECTIONS * D, D), dtype=jnp.float32) * (1.0 / np.sqrt(DIRECTIONS * D))
        b = jnp.zeros((D,), dtype=jnp.float32)
        gamma = jnp.ones((D,), dtype=jnp.float32)
        beta = jnp.zeros((D,), dtype=jnp.float32)
        return {'adj': adj, 'hid': hid, 'W': W, 'b': b, 'gamma': gamma, 'beta': beta}
    _L1_gnn_all = _L1_gnn_setup()
    _L1_gnn_in = {k: v for k, v in _L1_gnn_all.items() if k in ('W', 'b', 'gamma', 'beta')}
    del _L1_gnn_all

    def _L2_gnn_setup():
        import jax, jax.numpy as jnp
        import numpy as np
        import math
        D = 256
        B, L = (8, 1024)
        EPS = 1e-05

        def layer_norm(y, gamma, beta):
            mu = jnp.mean(y, axis=-1, keepdims=True)
            var = jnp.mean(jnp.square(y - mu), axis=-1, keepdims=True)
            return (y - mu) * jax.lax.rsqrt(var + EPS) * gamma + beta
        key = jax.random.key(seed)
        ks = jax.random.split(key, 8)
        s = 1.0 / math.sqrt(D)
        x = jax.random.normal(ks[0], (B, L, D), dtype=jnp.float32)
        adj = jax.random.randint(ks[1], (B, L, L), 0, 2, dtype=jnp.int32)
        Wq = jax.random.normal(ks[2], (D, D), dtype=jnp.float32) * s
        Wk = jax.random.normal(ks[3], (D, D), dtype=jnp.float32) * s
        Wv = jax.random.normal(ks[4], (D, D), dtype=jnp.float32) * s
        Wo = jax.random.normal(ks[5], (D, D), dtype=jnp.float32) * s
        bo = jnp.zeros((D,), dtype=jnp.float32)
        gamma = jnp.ones((D,), dtype=jnp.float32)
        beta = jnp.zeros((D,), dtype=jnp.float32)
        return {'x': x, 'adj': adj, 'Wq': Wq, 'Wk': Wk, 'Wv': Wv, 'Wo': Wo, 'bo': bo, 'gamma': gamma, 'beta': beta}
    _L2_gnn_all = _L2_gnn_setup()
    _L2_gnn_in = {k: v for k, v in _L2_gnn_all.items() if k in ('Wq', 'Wk', 'Wv', 'Wo', 'bo', 'gamma', 'beta')}
    del _L2_gnn_all

    def _L3_gnn_setup():
        import jax, jax.numpy as jnp
        import numpy as np
        B, N, E, FF, L = (8, 1024, 256, 128, 2)
        LN_EPS = 1e-05
        SCALE = float(np.sqrt(FF))

        def layer_norm(x, g, b):
            m = jnp.mean(x, axis=-1, keepdims=True)
            v = jnp.mean(jnp.square(x - m), axis=-1, keepdims=True)
            return (x - m) * jax.lax.rsqrt(v + LN_EPS) * g + b
        key = jax.random.key(seed)
        ks = jax.random.split(key, 9)
        s = 0.02
        node_fts = jax.random.normal(ks[0], (B, N, E), jnp.float32)
        rel_edges = jax.random.randint(ks[1], (B, N, N), 0, 2, jnp.int32)
        Wq = jax.random.normal(ks[2], (L, FF, E), jnp.float32) * s
        bq = jnp.zeros((L, FF), jnp.float32)
        Wk = jax.random.normal(ks[3], (L, FF, E), jnp.float32) * s
        bk = jnp.zeros((L, FF), jnp.float32)
        Wc = jax.random.normal(ks[4], (L, E, E), jnp.float32) * s
        ln_g = jnp.ones((L, E), jnp.float32)
        ln_b = jnp.zeros((L, E), jnp.float32)
        return {'node_fts': node_fts, 'rel_edges': rel_edges, 'Wq': Wq, 'bq': bq, 'Wk': Wk, 'bk': bk, 'Wc': Wc, 'ln_g': ln_g, 'ln_b': ln_b}
    _L3_gnn_all = _L3_gnn_setup()
    _L3_gnn_in = {k: v for k, v in _L3_gnn_all.items() if k in ('Wq', 'bq', 'Wk', 'bk', 'Wc', 'ln_g', 'ln_b')}
    del _L3_gnn_all
    return {'x': x, 'adj': adj, 'L0_gnn_ln1_g': _L0_gnn_in['ln1_g'], 'L0_gnn_ln1_b': _L0_gnn_in['ln1_b'], 'L0_gnn_ln2_g': _L0_gnn_in['ln2_g'], 'L0_gnn_ln2_b': _L0_gnn_in['ln2_b'], 'L0_gnn_wq': _L0_gnn_in['wq'], 'L0_gnn_bq': _L0_gnn_in['bq'], 'L0_gnn_wk': _L0_gnn_in['wk'], 'L0_gnn_bk': _L0_gnn_in['bk'], 'L0_gnn_wv': _L0_gnn_in['wv'], 'L0_gnn_bv': _L0_gnn_in['bv'], 'L0_gnn_wo': _L0_gnn_in['wo'], 'L0_gnn_bo': _L0_gnn_in['bo'], 'L0_gnn_w1': _L0_gnn_in['w1'], 'L0_gnn_b1': _L0_gnn_in['b1'], 'L0_gnn_w2': _L0_gnn_in['w2'], 'L0_gnn_b2': _L0_gnn_in['b2'], 'L1_gnn_W': _L1_gnn_in['W'], 'L1_gnn_b': _L1_gnn_in['b'], 'L1_gnn_gamma': _L1_gnn_in['gamma'], 'L1_gnn_beta': _L1_gnn_in['beta'], 'L2_gnn_Wq': _L2_gnn_in['Wq'], 'L2_gnn_Wk': _L2_gnn_in['Wk'], 'L2_gnn_Wv': _L2_gnn_in['Wv'], 'L2_gnn_Wo': _L2_gnn_in['Wo'], 'L2_gnn_bo': _L2_gnn_in['bo'], 'L2_gnn_gamma': _L2_gnn_in['gamma'], 'L2_gnn_beta': _L2_gnn_in['beta'], 'L3_gnn_Wq': _L3_gnn_in['Wq'], 'L3_gnn_bq': _L3_gnn_in['bq'], 'L3_gnn_Wk': _L3_gnn_in['Wk'], 'L3_gnn_bk': _L3_gnn_in['bk'], 'L3_gnn_Wc': _L3_gnn_in['Wc'], 'L3_gnn_ln_g': _L3_gnn_in['ln_g'], 'L3_gnn_ln_b': _L3_gnn_in['ln_b']}

def reference(x, adj, L0_gnn_ln1_g, L0_gnn_ln1_b, L0_gnn_ln2_g, L0_gnn_ln2_b, L0_gnn_wq, L0_gnn_bq, L0_gnn_wk, L0_gnn_bk, L0_gnn_wv, L0_gnn_bv, L0_gnn_wo, L0_gnn_bo, L0_gnn_w1, L0_gnn_b1, L0_gnn_w2, L0_gnn_b2, L1_gnn_W, L1_gnn_b, L1_gnn_gamma, L1_gnn_beta, L2_gnn_Wq, L2_gnn_Wk, L2_gnn_Wv, L2_gnn_Wo, L2_gnn_bo, L2_gnn_gamma, L2_gnn_beta, L3_gnn_Wq, L3_gnn_bq, L3_gnn_Wk, L3_gnn_bk, L3_gnn_Wc, L3_gnn_ln_g, L3_gnn_ln_b):
    import jax
    import jax.numpy as jnp

    def _L0_gnn_ref(x, adj_matrix, edge_attr_matrix, ln1_g, ln1_b, ln2_g, ln2_b, wq, bq, wk, bk, wv, bv, wo, bo, w1, b1, w2, b2):
        import jax, jax.numpy as jnp
        import numpy as np
        B, S, D, H = (2, 1024, 256, 8)
        HD = D // H
        EPS = 1e-05

        def _ln(x, g, b):
            mu = jnp.mean(x, axis=-1, keepdims=True)
            var = jnp.mean((x - mu) ** 2, axis=-1, keepdims=True)
            return (x - mu) * jax.lax.rsqrt(var + EPS) * g + b
        b, s, d = x.shape
        residual = x
        nx = _ln(x, ln1_g, ln1_b)
        q = (nx @ wq + bq).reshape(b, s, H, HD).transpose(0, 2, 1, 3)
        k = (nx @ wk + bk).reshape(b, s, H, HD).transpose(0, 2, 1, 3)
        v = (nx @ wv + bv).reshape(b, s, H, HD).transpose(0, 2, 1, 3)
        adjf = adj_matrix.astype(jnp.float32)
        bias = jnp.where(adj_matrix > 0, 0.1 * edge_attr_matrix * adjf, -jnp.inf)[:, None]
        scores = jnp.einsum('bhqd,bhkd->bhqk', q, k) / np.sqrt(HD) + bias
        attn = jax.nn.softmax(scores, axis=-1)
        out = jnp.einsum('bhqk,bhkd->bhqd', attn, v)
        out = out.transpose(0, 2, 1, 3).reshape(b, s, d)
        x1 = residual + (out @ wo + bo)
        n2 = _ln(x1, ln2_g, ln2_b)
        mlp = jax.nn.gelu(n2 @ w1 + b1, approximate=False) @ w2 + b2
        return x1 + mlp

    def _L1_gnn_ref(adj, hid, W, b, gamma, beta):
        import jax, jax.numpy as jnp
        import numpy as np
        EPSILON = 1e-13
        LN_EPS = 1e-05
        DIRECTIONS = 2
        HID = 256

        def _layer_norm(x, gamma, beta):
            mu = jnp.mean(x, axis=-1, keepdims=True)
            var = jnp.mean(jnp.square(x - mu), axis=-1, keepdims=True)
            return (x - mu) * jax.lax.rsqrt(var + LN_EPS) * gamma + beta
        residual = hid
        direct_list = []
        for j in range(DIRECTIONS):
            mask = (adj == j + 1).astype(hid.dtype)
            weight = mask / (jnp.sum(mask, axis=-1, keepdims=True) + EPSILON)
            direct_list.append(jnp.einsum('bnm,bmd->bnd', weight, hid))
        out = jnp.concatenate(direct_list, axis=-1)
        out = out @ W + b
        out = jax.nn.relu(out)
        out = out + residual
        return _layer_norm(out, gamma, beta)

    def _L2_gnn_ref(x, adj, Wq, Wk, Wv, Wo, bo, gamma, beta):
        import jax, jax.numpy as jnp
        import numpy as np
        import math
        D = 256
        B, L = (8, 1024)
        EPS = 1e-05

        def layer_norm(y, gamma, beta):
            mu = jnp.mean(y, axis=-1, keepdims=True)
            var = jnp.mean(jnp.square(y - mu), axis=-1, keepdims=True)
            return (y - mu) * jax.lax.rsqrt(var + EPS) * gamma + beta
        d_out = Wq.shape[1]
        scale = 1.0 / math.sqrt(d_out)
        Q = x @ Wq
        K = x @ Wk
        V = x @ Wv
        sc = jnp.einsum('bld,bmd->blm', Q, K) * scale
        mask = adj == 0
        sc = jnp.where(mask, -jnp.inf, sc)
        all_inf = jnp.all(mask, axis=-1, keepdims=True)
        sc = jnp.where(all_inf, 0.0, sc)
        w = jax.nn.softmax(sc, axis=-1)
        out = jnp.einsum('blm,bmd->bld', w, V)
        y = x + out @ Wo + bo
        return layer_norm(y, gamma, beta)

    def _L3_gnn_ref(node_fts, rel_edges, Wq, bq, Wk, bk, Wc, ln_g, ln_b):
        import jax, jax.numpy as jnp
        import numpy as np
        B, N, E, FF, L = (8, 1024, 256, 128, 2)
        LN_EPS = 1e-05
        SCALE = float(np.sqrt(FF))

        def layer_norm(x, g, b):
            m = jnp.mean(x, axis=-1, keepdims=True)
            v = jnp.mean(jnp.square(x - m), axis=-1, keepdims=True)
            return (x - m) * jax.lax.rsqrt(v + LN_EPS) * g + b
        x = node_fts
        mask = rel_edges == 0
        for k in range(L):
            q = jnp.einsum('bnd,fd->bnf', x, Wq[k]) + bq[k]
            kk = jnp.einsum('bnd,fd->bnf', x, Wk[k]) + bk[k]
            scores = jnp.einsum('bof,bif->boi', q, kk) / SCALE
            scores = jnp.where(mask, -10000000000.0, scores)
            attn = jax.nn.softmax(scores, axis=2)
            attn = jnp.where(mask, 0.0, attn)
            ctx = jnp.einsum('boi,bid->bod', attn, x)
            ctx = jnp.einsum('bnd,ed->bne', ctx, Wc[k])
            x = layer_norm(x + ctx, ln_g[k], ln_b[k])
        return x
    x = _L0_gnn_ref(x, adj, adj, L0_gnn_ln1_g, L0_gnn_ln1_b, L0_gnn_ln2_g, L0_gnn_ln2_b, L0_gnn_wq, L0_gnn_bq, L0_gnn_wk, L0_gnn_bk, L0_gnn_wv, L0_gnn_bv, L0_gnn_wo, L0_gnn_bo, L0_gnn_w1, L0_gnn_b1, L0_gnn_w2, L0_gnn_b2)
    x = _L1_gnn_ref(adj, x, L1_gnn_W, L1_gnn_b, L1_gnn_gamma, L1_gnn_beta)
    x = _L2_gnn_ref(x, adj, L2_gnn_Wq, L2_gnn_Wk, L2_gnn_Wv, L2_gnn_Wo, L2_gnn_bo, L2_gnn_gamma, L2_gnn_beta)
    x = _L3_gnn_ref(x, adj, L3_gnn_Wq, L3_gnn_bq, L3_gnn_Wk, L3_gnn_bk, L3_gnn_Wc, L3_gnn_ln_g, L3_gnn_ln_b)
    return x

_drawn_inputs = setup_inputs


def setup_inputs(seed=0):
    import zlib

    import numpy as np

    out = dict(_drawn_inputs(seed))
    spreads = {'L0_gnn_ln1_g': (1.0, 0.2),
     'L0_gnn_ln1_b': (0.0, 0.1),
     'L0_gnn_ln2_g': (1.0, 0.2),
     'L0_gnn_ln2_b': (0.0, 0.1),
     'L0_gnn_bq': (0.0, 0.1),
     'L0_gnn_bk': (0.0, 0.8),
     'L0_gnn_bv': (0.0, 0.1),
     'L0_gnn_bo': (0.0, 0.1),
     'L0_gnn_b1': (0.0, 0.1),
     'L0_gnn_b2': (0.0, 0.1),
     'L1_gnn_b': (0.0, 0.1),
     'L1_gnn_gamma': (1.0, 0.2),
     'L1_gnn_beta': (0.0, 0.1),
     'L2_gnn_bo': (0.0, 0.1),
     'L2_gnn_gamma': (1.0, 0.2),
     'L2_gnn_beta': (0.0, 0.1),
     'L3_gnn_bq': (0.0, 0.8),
     'L3_gnn_bk': (0.0, 0.8),
     'L3_gnn_ln_g': (1.0, 0.2),
     'L3_gnn_ln_b': (0.0, 0.1)}
    factors = {'L3_gnn_Wq': 4.821, 'L3_gnn_Wk': 4.513}
    for name, (base, spread) in spreads.items():
        noise = np.random.default_rng([zlib.crc32(name.encode()), seed]).standard_normal(out[name].shape)
        drawn = base * np.exp(spread * noise) if base else spread * noise
        out[name] = jnp.asarray(drawn.astype(out[name].dtype))
    for name, factor in factors.items():
        out[name] = (out[name] * factor).astype(out[name].dtype)
    return out
```

```python
import concourse.bass as bass
from concourse import mybir
from contextlib import ExitStack

F32 = mybir.dt.float32
F32R = mybir.dt.float32r
I32 = mybir.dt.int32
ALU = mybir.AluOpType
ACT = mybir.ActivationFunctionType

P = 128
D = 256
DC = D // P
BIG = 1.0e30
EPS = 1.0e-5
DV = D + 2


def attention_layer(nc, tag, x_in, x_out, adj, wq_a, wk_a, wv_a, wo_a, bq, bk, bo, gamma, beta,
                    score_scale, B, N):
    folded = wo_a is not None
    T = N // P
    QC = DC if folded else 1
    KC = DC if folded else 1
    XB = T // 2
    KB = 0 if folded else N // 512
    VB = T // 2
    NP = XB + KB + VB
    HALF = 512

    with nc.cleanup_on_exit(), ExitStack() as ctx:
        def sb(name, shape, dt=F32):
            return ctx.enter_context(nc.sbuf_tensor(f"{tag}_{name}", shape, dt))

        def pb(name, shape):
            return ctx.enter_context(nc.psum_tensor(f"{tag}_{name}", shape, F32))

        def sem(name):
            return nc.alloc_semaphore(name=f"{tag}_{name}")

        w_raw = sb("w_raw", [P, 4 * DC * D])
        QW = D if folded else P
        wq_hi, wq_lo = sb("wq_hi", [P, DC, QW], F32R), sb("wq_lo", [P, DC, QW], F32R)
        wv_hi, wv_lo = sb("wv_hi", [P, DC, D], F32R), sb("wv_lo", [P, DC, D], F32R)
        if not folded:
            wk_hi, wk_lo = sb("wk_hi", [P, DC, P], F32R), sb("wk_lo", [P, DC, P], F32R)
            bqk = sb("bqk", [P, 2])
        else:
            bo_row = sb("bo_row", [P, D])
        w_fold = sb("w_fold", [P, 2, DC, D])
        gamma_row, beta_row = sb("gamma_row", [P, D]), sb("beta_row", [P, D])
        ident = sb("ident", [P, P])
        x_tok = sb("x_tok", [P, T, D])
        x_res = sb("x_res", [P, T, D])
        x_new = sb("x_new", [P, T, D])
        xT_hi, xT_lo = sb("xT_hi", [P, DC, N], F32R), sb("xT_lo", [P, DC, N], F32R)
        if folded:
            kT_hi, kT_lo = xT_hi, xT_lo
        else:
            kT_hi, kT_lo = sb("kT_hi", [P, 1, N], F32R), sb("kT_lo", [P, 1, N], F32R)
        v_hi, v_lo = sb("v_hi", [P, T, DV], F32R), sb("v_lo", [P, T, DV], F32R)
        qT_hi, qT_lo = sb("qT_hi", [P, QC, P], F32R), sb("qT_lo", [P, QC, P], F32R)
        adj_sb = sb("adj_sb", [P, T, N], I32)
        mask_bias = sb("mask_bias", [P, N])
        score = sb("score", [P, N])
        prob = sb("prob", [P, T, P])
        prob_hi, prob_lo = sb("prob_hi", [P, T, P], F32R), sb("prob_lo", [P, T, P], F32R)
        row_max = sb("row_max", [P, 1])
        has_key = sb("has_key", [P, 1])
        inv = sb("inv", [P, 2])
        y = sb("y", [P, D])
        stats = sb("stats", [P, 6])
        mean_var = sb("mean_var", [P, 2])
        ln_c = sb("ln_c", [P, 4])
        small = sb("small", [P, 3])

        ps_s = pb("ps_s", [P, N])
        ps_t = pb("ps_t", [P, N])
        ps_o = pb("ps_o", [P, HALF])
        ps_q = pb("ps_q", [P, HALF])
        ps_p = [pb(f"ps_p{i}", [P, HALF]) for i in range(2)]

        w_in, ready, w_ps, w_part = sem("w_in"), sem("ready"), sem("w_ps"), sem("w_part")
        x_in_s, res_in, adj_in, stored = sem("x_in"), sem("res_in"), sem("adj_in"), sem("stored")
        has_key_s, inv_s, stats_part, res_s = sem("has_key_s"), sem("inv_s"), sem("stats_part"), sem("res_s")
        proj_full, proj_hi, proj_lo = sem("proj_full"), sem("proj_hi"), sem("proj_lo")
        q_full, q_hi, q_lo = sem("q_full"), sem("q_hi"), sem("q_lo")
        score_full, shifted, turned = sem("score_full"), sem("shifted"), sem("turned")
        bias_made, bias_used = sem("bias_made"), sem("bias_used")
        exp_done, p_hi, p_lo, p_lo_b = sem("exp_done"), sem("p_hi"), sem("p_lo"), sem("p_lo_b")
        out_full, out_read, stats_done = sem("out_full"), sem("out_read"), sem("stats_done")
        rstd_part, rstd_done, normed, new_part, new_done = (sem("rstd_part"), sem("rstd_done"),
                                                            sem("normed"), sem("new_part"), sem("new_done"))
        step = sem("step")
        dve0 = sem("dve0")
        passed = sem("passed")

        x_in_t = x_in.rearrange("b (t p) d -> b p t d", p=P)
        x_out_t = x_out.rearrange("b (t p) d -> b p t d", p=P)
        adj_t = adj.rearrange("b (t p) m -> b t p m", p=P)
        raw = [w_raw[:, i * DC * D:(i + 1) * DC * D] for i in range(4)]

        def chunks(w):
            return w.rearrange("(c p) n -> p c n", p=P)

        block = ctx.enter_context(nc.Block())

        @block.sync
        def _(sp):
            weights = [wq_a, wk_a, wv_a] + ([wo_a] if folded else [])
            for i, w in enumerate(weights):
                n = w.shape[1]
                sp.dma_start(raw[i][:, 0:DC * n].rearrange("p (c n) -> p c n", c=DC), chunks(w)).then_inc(w_in, 16)
            sp.dma_start(gamma_row[:], gamma.partition_broadcast(P)).then_inc(w_in, 16)
            sp.dma_start(beta_row[:], beta.partition_broadcast(P)).then_inc(w_in, 16)
            if folded:
                sp.dma_start(bo_row[:], bo.partition_broadcast(P)).then_inc(w_in, 16)
            else:
                sp.dma_start(bqk[:, 0:1], bq.rearrange("(p o) -> p o", o=1)).then_inc(w_in, 16)
                sp.dma_start(bqk[:, 1:2], bk.rearrange("(p o) -> p o", o=1)).then_inc(w_in, 16)

            def load_tokens(b):
                sp.dma_start(x_tok[:], x_in_t[b]).then_inc(x_in_s, 16)

            def load_adj(b, t):
                sp.dma_start(adj_sb[:, t, :], adj_t[b, t]).then_inc(adj_in, 16)

            def load_residual(b):
                sp.dma_start(x_res[:], x_in_t[b]).then_inc(res_in, 16)

            def store(b, t):
                sp.wait_ge(new_done, b * T + t + 1)
                sp.dma_start(x_out_t[b][:, t, :], x_new[:, t, :]).then_inc(stored, 16)

            load_tokens(0)
            for t in range(T):
                load_adj(0, t)
            load_residual(0)
            sp.sem_inc(stored, 16 * T)
            with sp.Fori(0, B - 1) as b:
                sp.wait_ge(proj_full, b * NP + XB)
                load_tokens(b + 1)
                for t in range(T):
                    sp.wait_ge(bias_made, b * T + t + 1)
                    load_adj(b + 1, t)
                    if t == T - 1:
                        sp.wait_ge(out_read, (b + 1) * T + 1)
                        load_residual(b + 1)
                    store(b, t)
            for t in range(T):
                store(B - 1, t)
            sp.wait_ge(stored, 16 * T * (B + 1))

        @block.gpsimd
        def _(pool):
            pool.memset(ident[:], 0.0).then_inc(ready, 1)
            pool.memset(small[:, 0:1], -0.5).then_inc(ready, 1)
            pool.memset(small[:, 1:2], -1.0).then_inc(ready, 1)
            pool.memset(small[:, 2:3], EPS).then_inc(ready, 1)
            pool.wait_ge(ready, 4)
            pool.affine_select(out=ident[:], in_=ident[:], compare_op=ALU.not_equal, fill=1.0,
                               base=0, pattern=[[-1, P]], channel_multiplier=1).then_inc(ready, 1)
            pool.wait_ge(w_in, 16 * (7 if folded else 7))

            def p_low(g):
                pool.wait_ge(p_hi, 2 * g + 2)
                pool.tensor_tensor(prob_lo[:, T // 2:T, :], prob[:, T // 2:T, :], prob_hi[:, T // 2:T, :].bitcast(F32),
                                   ALU.subtract).then_inc(p_lo_b, 1)

            def norm_consts(g):
                pool.wait_ge(stats_done, g + 1)
                pool.tensor_tensor(ln_c[:, 0:1], mean_var[:, 1:2], small[:, 2:3], ALU.add).then_inc(rstd_part, 1)
                pool.wait_ge(rstd_part, 3 * g + 1)
                pool.tensor_tensor(ln_c[:, 1:2], ln_c[:, 0:1], small[:, 0:1], ALU.pow).then_inc(rstd_part, 1)
                pool.wait_ge(rstd_part, 3 * g + 2)
                pool.tensor_tensor(ln_c[:, 3:4], mean_var[:, 0:1], ln_c[:, 1:2], ALU.mult).then_inc(rstd_part, 1)
                pool.wait_ge(rstd_part, 3 * g + 3)
                pool.tensor_tensor(ln_c[:, 2:3], ln_c[:, 3:4], small[:, 1:2], ALU.mult).then_inc(rstd_done, 1)

            def affine(t, g):
                pool.wait_ge(normed, g + 2)
                pool.sem_inc(passed, 1)
                pool.tensor_tensor(x_new[:, t, :], x_new[:, t, :], gamma_row[:], ALU.mult).then_inc(new_part, 1)
                pool.wait_ge(new_part, g + 1)
                pool.sem_inc(passed, 1)
                pool.tensor_tensor(x_new[:, t, :], x_new[:, t, :], beta_row[:], ALU.add).then_inc(new_done, 1)

            with pool.Fori(0, B) as b:
                p_low(b * T)
                norm_consts(b * T)
                with pool.Fori(0, T - 1) as t:
                    g = b * T + t
                    p_low(g + 1)
                    affine(t, g)
                    norm_consts(g + 1)
                affine(T - 1, b * T + T - 1)

        @block.scalar
        def _(act):
            def split_hi(dst, ps, full, at, done, bias=0.0):
                act.wait_ge(full, at)
                act.activation(dst, ps, ACT.Identity, bias=bias).then_inc(done, 1)

            def q_evac(g):
                act.wait_ge(q_full, g + 1)
                act.activation(qT_hi[:], ps_q[:, 0:QC * P].rearrange("p (c n) -> p c n", c=QC), ACT.Identity,
                               bias=bqk[:, 0:1] if not folded else 0.0).then_inc(q_hi, 1)

            def exps(g):
                for h in range(2):
                    half = slice(h * T // 2, (h + 1) * T // 2)
                    act.wait_ge(turned, 2 * g + h + 1)
                    act.activation(prob[:, half, :], ps_t[:, h * HALF:(h + 1) * HALF].rearrange("p (t n) -> p t n", n=P),
                                   ACT.Exp).then_inc(exp_done, 1)
                    act.wait_ge(exp_done, 2 * g + h + 1)
                    act.activation(prob_hi[:, half, :], prob[:, half, :], ACT.Copy).then_inc(p_hi, 1)

            def normalise(t, g):
                act.wait_ge(rstd_done, g + 1)
                act.activation(x_new[:, t, :], y[:], ACT.Identity, bias=ln_c[:, 2:3], scale=ln_c[:, 1:2]).then_inc(normed, 1)

            act.wait_ge(w_in, 16 * 7)
            act.sem_inc(normed, 1)
            with act.Fori(0, B) as b:
                n = 0
                for i in range(XB):
                    split_hi(xT_hi[:, :, 2 * i * P:(2 * i + 2) * P], ps_p[n % 2][:].rearrange("p (c n) -> p c n", c=DC),
                             proj_full, b * NP + n + 1, proj_hi)
                    n += 1
                for i in range(KB):
                    split_hi(kT_hi[:, 0, i * HALF:(i + 1) * HALF], ps_p[n % 2][:], proj_full, b * NP + n + 1, proj_hi,
                             bias=bqk[:, 1:2])
                    n += 1
                for i in range(VB):
                    split_hi(v_hi[:, 2 * i:2 * i + 2, 0:D], ps_p[n % 2][:].rearrange("p (t n) -> p t n", n=D),
                             proj_full, b * NP + n + 1, proj_hi)
                    n += 1
                q_evac(b * T)
                q_evac(b * T + 1)
                exps(b * T)
                act.wait_ge(stored, 16 * T * (b + 1))
                q_evac(b * T + 2)
                with act.Fori(1, T - 2) as t:
                    g = b * T + t
                    exps(g)
                    normalise(t - 1, g - 1)
                    q_evac(g + 2)
                for t in (T - 2, T - 1):
                    exps(b * T + t)
                    normalise(t - 1, b * T + t - 1)
                normalise(T - 1, b * T + T - 1)

        @block.tensor
        def _(pe):
            pe.wait_ge(ready, 5)
            pe.wait_ge(w_in, 16 * 7)
            if folded:
                for j in range(2):
                    l = raw[2 * j].rearrange("p (c n) -> p c n", c=DC)
                    r = raw[2 * j + 1].rearrange("p (c n) -> p c n", c=DC)
                    for m in range(DC):
                        for c in range(DC):
                            mm = pe.matmul(ps_p[j][:, m * D:(m + 1) * D], l[:, c, m * P:(m + 1) * P], r[:, c, :],
                                           start=(c == 0), stop=(c == DC - 1))
                    mm.then_inc(w_ps, 1)
            pe.wait_ge(w_part, 1)

            def three(out, l_hi, l_lo, r_hi, r_lo, n, last):
                first = n == 0
                pe.matmul(out, l_hi, r_hi, start=first, stop=False)
                pe.matmul(out, l_hi, r_lo, start=False, stop=False)
                return pe.matmul(out, l_lo, r_hi, start=False, stop=(n == last))

            def q_tile(t, g):
                pe.wait_ge(q_lo, g + 1)
                for m in range(QC):
                    for c in range(DC):
                        mm = three(ps_q[:, m * P:(m + 1) * P], wq_hi[:, c, m * P:(m + 1) * P], wq_lo[:, c, m * P:(m + 1) * P],
                                   xT_hi[:, c, bass.ts(t, P)], xT_lo[:, c, bass.ts(t, P)], c, DC - 1)
                mm.then_inc(q_full, 1)

            def scores(g):
                pe.wait_ge(q_lo, g + 2)
                for h in range(2):
                    for c in range(KC):
                        mm = three(ps_s[:, h * HALF:(h + 1) * HALF], qT_hi[:, c, :], qT_lo[:, c, :],
                                   kT_hi[:, c, h * HALF:(h + 1) * HALF], kT_lo[:, c, h * HALF:(h + 1) * HALF], c, KC - 1)
                mm.then_inc(score_full, 1)

            def turn(g):
                pe.wait_ge(shifted, g + 1)
                for h in range(2):
                    for k in range(h * T // 2, (h + 1) * T // 2):
                        mm = pe.transpose(ps_t[:, k * P:(k + 1) * P], score[:, k * P:(k + 1) * P], ident[:])
                    mm.then_inc(turned, 1)

            def weigh(g):
                pe.wait_ge(out_read, g + 1)
                for k in range(T):
                    if k % (T // 2) == 0:
                        pe.wait_ge(p_lo if k == 0 else p_lo_b, g + 1)
                    mm = three(ps_o[:, 0:DV], prob_hi[:, k, :], prob_lo[:, k, :], v_hi[:, k, :], v_lo[:, k, :], k, T - 1)
                mm.then_inc(out_full, 1)

            with pe.Fori(0, B) as b:
                pe.wait_ge(x_in_s, (b + 1) * 16)
                n = 0

                def bank():
                    pe.wait_ge(proj_lo, b * NP + n + 1)
                    return ps_p[n % 2]

                for i in range(XB):
                    ps = bank()
                    for c in range(DC):
                        for j in range(2):
                            mm = pe.transpose(ps[:, (2 * c + j) * P:(2 * c + j + 1) * P],
                                              x_tok[:, 2 * i + j, c * P:(c + 1) * P], ident[:])
                    mm.then_inc(proj_full, 1)
                    n += 1
                pe.wait_ge(proj_lo, b * NP + XB + 2)
                for i in range(KB):
                    ps = bank()
                    for c in range(DC):
                        s = slice(i * HALF, (i + 1) * HALF)
                        mm = three(ps[:], wk_hi[:, c, :], wk_lo[:, c, :], xT_hi[:, c, s], xT_lo[:, c, s], c, DC - 1)
                    mm.then_inc(proj_full, 1)
                    n += 1
                for i in range(VB):
                    ps = bank()
                    for j in range(2):
                        s = slice((2 * i + j) * P, (2 * i + j + 1) * P)
                        for c in range(DC):
                            mm = three(ps[:, j * D:(j + 1) * D], xT_hi[:, c, s], xT_lo[:, c, s],
                                       wv_hi[:, c, :], wv_lo[:, c, :], c, DC - 1)
                    mm.then_inc(proj_full, 1)
                    n += 1
                q_tile(0, b * T)
                pe.wait_ge(proj_lo, b * NP + NP + 2)
                scores(b * T)
                q_tile(1, b * T + 1)
                with pe.Fori(0, T - 2) as t:
                    g = b * T + t
                    turn(g)
                    scores(g + 1)
                    q_tile(t + 2, g + 2)
                    weigh(g)
                g = b * T + T - 2
                turn(g)
                scores(g + 1)
                weigh(g)
                turn(g + 1)
                weigh(g + 1)

        @block.vector
        def _(dve):
            dve.memset(v_hi[:, :, D:D + 1].bitcast(F32), 1.0).then_inc(dve0, 1)
            dve.memset(v_hi[:, :, D + 1:DV].bitcast(F32), 0.0).then_inc(dve0, 1)
            dve.memset(v_lo[:, :, D:DV].bitcast(F32), 0.0).then_inc(dve0, 1)
            dve.sem_inc(proj_lo, 2)
            dve.sem_inc(q_lo, 1)
            dve.sem_inc(out_read, 1)
            dve.sem_inc(bias_used, 1)
            dve.wait_ge(w_in, 16 * 7)
            k = 0
            if folded:
                srcs = []
                for j in range(2):
                    dve.wait_ge(w_ps, j + 1)
                    dve.tensor_scalar(w_fold[:, j, :, :], ps_p[j][:].rearrange("p (c n) -> p c n", c=DC),
                                      score_scale if j == 0 else 1.0, None, ALU.mult).then_inc(step, 1)
                    k += 1
                dve.wait_ge(step, k)
                pairs = [(w_fold[:, 0, :, :], wq_hi, wq_lo), (w_fold[:, 1, :, :], wv_hi, wv_lo)]
            else:
                r = [raw[i][:, 0:DC * n].rearrange("p (c n) -> p c n", c=DC) for i, n in ((0, P), (1, P), (2, D))]
                dve.tensor_scalar(r[0], r[0], score_scale, None, ALU.mult).then_inc(step, 1)
                dve.tensor_scalar(bqk[:, 0:1], bqk[:, 0:1], score_scale, None, ALU.mult).then_inc(step, 1)
                k += 2
                dve.wait_ge(step, k)
                pairs = [(r[0], wq_hi, wq_lo), (r[1], wk_hi, wk_lo), (r[2], wv_hi, wv_lo)]
            for full, hi, lo in pairs:
                dve.tensor_copy(hi[:], full).then_inc(step, 1)
                k += 1
                dve.wait_ge(step, k)
                mm = dve.tensor_tensor(lo[:], full, hi[:].bitcast(F32), ALU.subtract)
            dve.wait_ge(dve0, 3)
            mm.then_inc(w_part, 1)
            dve.wait_ge(w_part, 1)

            def split_lo(dst, ps, hi, at, bias=None):
                dve.wait_ge(proj_hi, at)
                if bias is None:
                    dve.tensor_tensor(dst, ps, hi.bitcast(F32), ALU.subtract).then_inc(proj_lo, 1)
                else:
                    dve.scalar_tensor_tensor(dst, ps, bias, hi.bitcast(F32), ALU.add, ALU.subtract).then_inc(proj_lo, 1)

            def q_low(g):
                dve.wait_ge(q_hi, g + 1)
                src = ps_q[:, 0:QC * P].rearrange("p (c n) -> p c n", c=QC)
                if folded:
                    dve.tensor_tensor(qT_lo[:], src, qT_hi[:].bitcast(F32), ALU.subtract).then_inc(q_lo, 1)
                else:
                    dve.scalar_tensor_tensor(qT_lo[:, 0, :], ps_q[:, 0:P], bqk[:, 0:1], qT_hi[:, 0, :].bitcast(F32),
                                             ALU.add, ALU.subtract).then_inc(q_lo, 1)

            def make_bias(t, g):
                dve.tensor_scalar(mask_bias[:], adj_sb[:, t, :], 0.0, -BIG, ALU.is_equal, ALU.mult).then_inc(bias_made, 1)

            def shift(g):
                dve.wait_ge(bias_made, g + 1)
                dve.wait_ge(score_full, g + 1)
                dve.sem_inc(passed, 1)
                dve.tensor_tensor_reduce(score[:], ps_s[:], mask_bias[:], 1.0, -3.0e38, ALU.add, ALU.max,
                                         row_max[:]).then_inc(bias_used, 1)
                dve.wait_ge(bias_used, g + 2)
                dve.tensor_scalar(score[:], score[:], row_max[:], None, ALU.subtract).then_inc(shifted, 1)

            def flag(g):
                dve.tensor_scalar(has_key[:], row_max[:], -0.1 * BIG, None, ALU.is_gt).then_inc(has_key_s, 1)

            def p_low(g):
                half = slice(0, T // 2)
                dve.wait_ge(p_hi, 2 * g + 1)
                dve.tensor_tensor(prob_lo[:, half, :], prob[:, half, :], prob_hi[:, half, :].bitcast(F32),
                                  ALU.subtract).then_inc(p_lo, 1)

            def finish(t, g):
                dve.wait_ge(out_full, g + 1)
                dve.reciprocal(inv[:, 0:1], ps_o[:, D:D + 1]).then_inc(inv_s, 1)
                if folded:
                    dve.wait_ge(inv_s, g + 1)
                    iv = inv[:, 0:1]
                else:
                    dve.wait_ge(inv_s, 2 * g + 1)
                    dve.wait_ge(has_key_s, g + 1)
                    dve.tensor_tensor(inv[:, 1:2], inv[:, 0:1], has_key[:], ALU.mult).then_inc(inv_s, 1)
                    dve.wait_ge(inv_s, 2 * g + 2)
                    iv = inv[:, 1:2]
                dve.wait_ge(normed, g + 1)
                dve.scalar_tensor_tensor(y[:], ps_o[:, 0:D], iv, x_res[:, t, :], ALU.mult, ALU.add).then_inc(out_read, 1)
                dve.wait_ge(out_read, g + 2)
                dve.bn_stats(stats[:], y[:]).then_inc(stats_part, 1)
                dve.wait_ge(stats_part, g + 1)
                dve.sem_inc(passed, 1)
                dve.bn_aggr(mean_var[:], stats[:]).then_inc(stats_done, 1)

            with dve.Fori(0, B) as b:
                n = 0
                for i in range(XB):
                    s = slice(2 * i * P, (2 * i + 2) * P)
                    split_lo(xT_lo[:, :, s], ps_p[n % 2][:].rearrange("p (c n) -> p c n", c=DC), xT_hi[:, :, s],
                             b * NP + n + 1)
                    n += 1
                for i in range(KB):
                    s = slice(i * HALF, (i + 1) * HALF)
                    split_lo(kT_lo[:, 0, s], ps_p[n % 2][:], kT_hi[:, 0, s], b * NP + n + 1, bias=bqk[:, 1:2])
                    n += 1
                for i in range(VB):
                    s = slice(2 * i, 2 * i + 2)
                    split_lo(v_lo[:, s, 0:D], ps_p[n % 2][:].rearrange("p (t n) -> p t n", n=D), v_hi[:, s, 0:D],
                             b * NP + n + 1)
                    n += 1
                q_low(b * T)
                dve.wait_ge(adj_in, (b + 1) * 16 * T)
                make_bias(0, b * T)
                shift(b * T)
                q_low(b * T + 1)
                dve.wait_ge(res_in, (b + 1) * 16)
                if folded:
                    dve.tensor_tensor(x_res[:], x_res[:], bo_row[:].unsqueeze(1).to_broadcast([P, T, D]), ALU.add).then_inc(res_s, 1)
                    dve.wait_ge(res_s, b + 1)
                dve.sem_inc(passed, 1)
                def body(t, g, last):
                    if not folded:
                        flag(g)
                    p_low(g)
                    if last < 1:
                        make_bias(t + 1, g + 1)
                        shift(g + 1)
                    if last < 0:
                        q_low(g + 2)
                    finish(t, g)
                with dve.Fori(0, T - 2) as t:
                    body(t, b * T + t, -1)
                body(T - 2, b * T + T - 2, 0)
                body(T - 1, b * T + T - 1, 1)
    return nc


TINY = 1.0e-13


def direction_layer(nc, tag, x_in, x_out, adjT, w, bias, gamma, beta, B, N):
    T = N // P
    XB, YB = T // 2, T
    NP = XB + YB
    HALF = 512
    W2 = 2 * D

    with nc.cleanup_on_exit(), ExitStack() as ctx:
        def sb(name, shape, dt=F32):
            return ctx.enter_context(nc.sbuf_tensor(f"{tag}_{name}", shape, dt))

        def pb(name, shape):
            return ctx.enter_context(nc.psum_tensor(f"{tag}_{name}", shape, F32))

        def sem(name):
            return nc.alloc_semaphore(name=f"{tag}_{name}")

        w_raw = sb("w_raw", [P, DC, W2])
        w_hi, w_lo = sb("w_hi", [P, DC, W2], F32R), sb("w_lo", [P, DC, W2], F32R)
        bias_row, gamma_row, beta_row = sb("bias_row", [P, D]), sb("gamma_row", [P, D]), sb("beta_row", [P, D])
        ident, small = sb("ident", [P, P]), sb("small", [P, 3])
        small2 = sb("small2", [P, 2])
        x_tok, x_res, x_new = sb("x_tok", [P, T, D]), sb("x_res", [P, T, D]), sb("x_new", [P, T, D])
        xT_hi, xT_lo = sb("xT_hi", [P, DC, N], F32R), sb("xT_lo", [P, DC, N], F32R)
        y_hi, y_lo = sb("y_hi", [P, T, 2, DV], F32R), sb("y_lo", [P, T, 2, DV], F32R)
        adj_sb = [sb(f"adj_sb{j}", [P, T, P], I32) for j in range(2)]
        off = [sb(f"off{j}", [P, T, P]) for j in range(2)]
        kind1 = [sb(f"kind1_{j}", [P, T, P], F32R) for j in range(2)]
        kind2 = [sb(f"kind2_{j}", [P, T, P], F32R) for j in range(2)]
        cnt, inv = sb("cnt", [P, 2, 1]), sb("inv", [P, 2, 1])
        mean1, mean12, y = sb("mean1", [P, D]), sb("mean12", [P, D]), sb("y", [P, D])
        stats, mean_var, ln_c = sb("stats", [P, 6]), sb("mean_var", [P, 2]), sb("ln_c", [P, 4])

        ps_p = [pb(f"ps_p{i}", [P, HALF]) for i in range(2)]
        ps_o = [pb(f"ps_o{i}", [P, 2, HALF]) for i in range(2)]

        w_in, w_part, w_split, ready, ones_in = sem("w_in"), sem("w_part"), sem("w_split"), sem("ready"), sem("ones_in")
        x_in_s, res_in, stored = sem("x_in"), sem("res_in"), sem("stored")
        adj_in = [sem(f"adj_in{j}") for j in range(2)]
        proj_full, proj_hi, proj_lo = sem("proj_full"), sem("proj_hi"), sem("proj_lo")
        kind1_made, kind2_part, kind2_made = sem("kind1_made"), sem("kind2_part"), sem("kind2_made")
        out_full, out_read = sem("out_full"), sem("out_read")
        fin_part, stats_done = sem("fin_part"), sem("stats_done")
        rstd_part, rstd_done, normed, new_part, new_done = (sem("rstd_part"), sem("rstd_done"), sem("normed"),
                                                            sem("new_part"), sem("new_done"))
        passed, small2_in = sem("passed"), sem("small2_in")

        x_in_t = x_in.rearrange("b (t p) d -> b p t d", p=P)
        x_out_t = x_out.rearrange("b (t p) d -> b p t d", p=P)
        block = ctx.enter_context(nc.Block())
        H = T // 2

        @block.sync
        def _(sp):
            sp.dma_start(w_raw[:, :, 0:D], w[0:D, :].rearrange("(c p) n -> p c n", p=P)).then_inc(w_in, 16)
            sp.dma_start(w_raw[:, :, D:W2], w[D:W2, :].rearrange("(c p) n -> p c n", p=P)).then_inc(w_in, 16)
            for dst, src in ((bias_row, bias), (gamma_row, gamma), (beta_row, beta)):
                sp.dma_start(dst[:], src.partition_broadcast(P)).then_inc(w_in, 16)

            def load_tokens(b):
                sp.dma_start(x_tok[:], x_in_t[b]).then_inc(x_in_s, 16)

            def load_residual(b):
                sp.dma_start(x_res[:], x_in_t[b]).then_inc(res_in, 16)

            def load_adj(b, t, j):
                sp.dma_start(adj_sb[j][:], adjT[b, t]).then_inc(adj_in[j], 16)

            def store_last(b):
                t = T - 1
                sp.wait_ge(new_done, b * T + t + 1)
                sp.dma_start(x_out_t[b][:, t, :], x_new[:, t, :]).then_inc(stored, 16)

            load_tokens(0)
            load_adj(0, 0, 0)
            load_adj(0, 1, 1)
            load_residual(0)
            sp.sem_inc(stored, 16 * T)

            with sp.Fori(0, B - 1) as b:
                sp.wait_ge(proj_full, b * NP + XB)
                load_tokens(b + 1)
                with sp.Fori(0, H - 1) as i:
                    for j in range(2):
                        sp.wait_ge(kind1_made, b * T + 2 * i + j + 1)
                        sp.wait_ge(kind2_made, b * T + 2 * i + j + 1)
                        load_adj(b, 2 * i + 2 + j, j)
                for j in range(2):
                    sp.wait_ge(kind1_made, b * T + T - 1 + j)
                    sp.wait_ge(kind2_made, b * T + T - 1 + j)
                    load_adj(b + 1, j, j)
                sp.wait_ge(out_read, (b + 1) * T + 2)
                load_residual(b + 1)
                store_last(b)
            b = B - 1
            with sp.Fori(0, H - 1) as i:
                for j in range(2):
                    sp.wait_ge(kind1_made, b * T + 2 * i + j + 1)
                    sp.wait_ge(kind2_made, b * T + 2 * i + j + 1)
                    load_adj(b, 2 * i + 2 + j, j)
            store_last(b)
            sp.wait_ge(stored, 16 * T * (B + 1))

        @block.gpsimd
        def _(pool):
            pool.memset(ident[:], 0.0).then_inc(ready, 1)
            pool.memset(small[:, 0:1], -0.5).then_inc(ready, 1)
            pool.memset(small[:, 1:2], -1.0).then_inc(ready, 1)
            pool.memset(small[:, 2:3], EPS).then_inc(ready, 1)
            pool.wait_ge(ready, 4)
            pool.affine_select(out=ident[:], in_=ident[:], compare_op=ALU.not_equal, fill=1.0,
                               base=0, pattern=[[-1, P]], channel_multiplier=1).then_inc(ready, 1)
            pool.wait_ge(w_in, 16 * 5)

            def norm_consts(g):
                pool.wait_ge(stats_done, g + 1)
                pool.tensor_tensor(ln_c[:, 0:1], mean_var[:, 1:2], small[:, 2:3], ALU.add).then_inc(rstd_part, 1)
                pool.wait_ge(rstd_part, 3 * g + 1)
                pool.tensor_tensor(ln_c[:, 1:2], ln_c[:, 0:1], small[:, 0:1], ALU.pow).then_inc(rstd_part, 1)
                pool.wait_ge(rstd_part, 3 * g + 2)
                pool.tensor_tensor(ln_c[:, 3:4], mean_var[:, 0:1], ln_c[:, 1:2], ALU.mult).then_inc(rstd_part, 1)
                pool.wait_ge(rstd_part, 3 * g + 3)
                pool.tensor_tensor(ln_c[:, 2:3], ln_c[:, 3:4], small[:, 1:2], ALU.mult).then_inc(rstd_done, 1)

            def affine(t, g):
                pool.wait_ge(normed, g + 2)
                pool.sem_inc(passed, 1)
                pool.tensor_tensor(x_new[:, t, :], x_new[:, t, :], gamma_row[:], ALU.mult).then_inc(new_part, 1)
                pool.wait_ge(new_part, g + 1)
                pool.sem_inc(passed, 1)
                pool.tensor_tensor(x_new[:, t, :], x_new[:, t, :], beta_row[:], ALU.add).then_inc(new_done, 1)

            with pool.Fori(0, B) as b:
                with pool.Fori(0, T) as t:
                    g = b * T + t
                    norm_consts(g)
                    affine(t, g)

        @block.scalar
        def _(act):
            def split_hi(dst, ps, at):
                act.wait_ge(proj_full, at)
                act.activation(dst, ps, ACT.Identity).then_inc(proj_hi, 1)

            def make_kind2(g, j, seen):
                act.wait_ge(adj_in[j], 16 * seen)
                act.activation(off[j][:], adj_sb[j][:], ACT.Abs, bias=small2[:, 0:1]).then_inc(kind2_part, 1)
                act.wait_ge(kind2_part, g + 1)
                act.wait_ge(out_full, g + 1)
                act.activation(kind2[j][:], off[j][:], ACT.Relu, bias=small2[:, 1:2], scale=-1.0).then_inc(kind2_made, 1)

            def normalise(t, g):
                act.wait_ge(rstd_done, g + 1)
                act.activation(x_new[:, t, :], y[:], ACT.Identity, bias=ln_c[:, 2:3], scale=ln_c[:, 1:2]).then_inc(normed, 1)

            def store(b, t, g):
                act.wait_ge(new_done, g + 1)
                act.dma_start(x_out_t[b][:, t, :], x_new[:, t, :]).then_inc(stored, 16)

            act.sem_inc(normed, 1)
            act.wait_ge(small2_in, 2)
            with act.Fori(0, B) as b:
                n = 0
                for i in range(XB):
                    split_hi(xT_hi[:, :, 2 * i * P:(2 * i + 2) * P], ps_p[n % 2][:].rearrange("p (c n) -> p c n", c=DC),
                             b * NP + n + 1)
                    n += 1
                for t in range(YB):
                    split_hi(y_hi[:, t, :, 0:D], ps_p[n % 2][:].rearrange("p (j n) -> p j n", j=2), b * NP + n + 1)
                    n += 1
                make_kind2(b * T, 0, b * H + 1)
                make_kind2(b * T + 1, 1, b * H + 1)
                act.wait_ge(stored, 16 * T * (b + 1))
                act.sem_inc(passed, 1)
                g = b * T
                make_kind2(g + 2, 0, b * H + 2)
                normalise(0, g)
                make_kind2(g + 3, 1, b * H + 2)
                normalise(1, g + 1)
                store(b, 0, g)
                with act.Fori(1, H - 1) as i:
                    for j in range(2):
                        g = b * T + 2 * i + j
                        make_kind2(g + 2, j, b * H + i + 2)
                        normalise(2 * i + j, g)
                        store(b, 2 * i + j - 1, g - 1)
                for t in (T - 2, T - 1):
                    normalise(t, b * T + t)
                    store(b, t - 1, b * T + t - 1)

        @block.tensor
        def _(pe):
            pe.wait_ge(ready, 5)
            pe.wait_ge(w_split, 1)
            pe.wait_ge(ones_in, 3)
            pe.sem_inc(out_full, 2)

            def three(out, l_hi, l_lo, r_hi, r_lo, n, last):
                pe.matmul(out, l_hi, r_hi, start=(n == 0), stop=False)
                pe.matmul(out, l_hi, r_lo, start=False, stop=False)
                return pe.matmul(out, l_lo, r_hi, start=False, stop=(n == last))

            def aggregate(g, j):
                pe.wait_ge(kind1_made, g + 1)
                pe.wait_ge(out_read, g + 1)
                for d, kind in ((0, kind1), (1, kind2)):
                    if d == 1:
                        pe.wait_ge(kind2_made, g + 1)
                    for k in range(T):
                        pe.matmul(ps_o[j][:, d, 0:DV], kind[j][:, k, :], y_hi[:, k, d, :], start=(k == 0), stop=False)
                        mm = pe.matmul(ps_o[j][:, d, 0:DV], kind[j][:, k, :], y_lo[:, k, d, :], start=False,
                                       stop=(k == T - 1))
                mm.then_inc(out_full, 1)

            with pe.Fori(0, B) as b:
                pe.wait_ge(x_in_s, (b + 1) * 16)
                n = 0
                for i in range(XB):
                    pe.wait_ge(proj_lo, b * NP + n + 1)
                    for c in range(DC):
                        for j in range(2):
                            mm = pe.transpose(ps_p[n % 2][:, (2 * c + j) * P:(2 * c + j + 1) * P],
                                              x_tok[:, 2 * i + j, c * P:(c + 1) * P], ident[:])
                    mm.then_inc(proj_full, 1)
                    n += 1
                for t in range(YB):
                    pe.wait_ge(proj_lo, b * NP + max(n + 1, 2 + XB))
                    for c in range(DC):
                        s = slice(t * P, (t + 1) * P)
                        mm = three(ps_p[n % 2][:], xT_hi[:, c, s], xT_lo[:, c, s], w_hi[:, c, :], w_lo[:, c, :], c, DC - 1)
                    mm.then_inc(proj_full, 1)
                    n += 1
                pe.wait_ge(proj_lo, (b + 1) * NP + 2)
                pe.sem_inc(passed, 1)
                with pe.Fori(0, H) as i:
                    for j in range(2):
                        aggregate(b * T + 2 * i + j, j)

        @block.vector
        def _(dve):
            dve.memset(small2[:, 0:1], -2.0).then_inc(small2_in, 1)
            dve.memset(small2[:, 1:2], 1.0).then_inc(small2_in, 1)
            dve.memset(y_hi[:, :, :, D:D + 1].bitcast(F32), 1.0).then_inc(ones_in, 1)
            dve.memset(y_hi[:, :, :, D + 1:DV].bitcast(F32), 0.0).then_inc(ones_in, 1)
            dve.memset(y_lo[:, :, :, D:DV].bitcast(F32), 0.0).then_inc(ones_in, 1)
            dve.sem_inc(proj_lo, 2)
            dve.sem_inc(out_read, 2)
            dve.wait_ge(w_in, 16 * 5)
            dve.tensor_copy(w_hi[:], w_raw[:]).then_inc(w_part, 1)
            dve.wait_ge(w_part, 1)
            dve.tensor_tensor(w_lo[:], w_raw[:], w_hi[:].bitcast(F32), ALU.subtract).then_inc(w_split, 1)

            def split_lo(dst, ps, hi, at):
                dve.wait_ge(proj_hi, at)
                dve.tensor_tensor(dst, ps, hi.bitcast(F32), ALU.subtract).then_inc(proj_lo, 1)

            def make_kind1(g, j, seen):
                dve.wait_ge(adj_in[j], 16 * seen)
                dve.wait_ge(out_full, g + 1)
                dve.tensor_scalar(kind1[j][:], adj_sb[j][:], 1.0, None, ALU.is_equal).then_inc(kind1_made, 1)

            def finish(t, g, j):
                dve.wait_ge(out_full, g + 3)
                dve.tensor_scalar(cnt[:], ps_o[j][:, :, D:D + 1], TINY, None, ALU.add).then_inc(fin_part, 1)
                dve.wait_ge(fin_part, 5 * g + 1)
                dve.reciprocal(inv[:], cnt[:]).then_inc(fin_part, 1)
                dve.wait_ge(fin_part, 5 * g + 2)
                dve.scalar_tensor_tensor(mean1[:], ps_o[j][:, 0, 0:D], inv[:, 0, :], bias_row[:], ALU.mult, ALU.add)\
                   .then_inc(fin_part, 1)
                dve.wait_ge(fin_part, 5 * g + 3)
                dve.scalar_tensor_tensor(mean12[:], ps_o[j][:, 1, 0:D], inv[:, 1, :], mean1[:], ALU.mult, ALU.add)\
                   .then_inc(fin_part, 1)
                dve.wait_ge(fin_part, 5 * g + 4)
                dve.wait_ge(normed, g + 1)
                dve.scalar_tensor_tensor(y[:], mean12[:], 0.0, x_res[:, t, :], ALU.max, ALU.add).then_inc(out_read, 1)
                dve.wait_ge(out_read, g + 3)
                dve.bn_stats(stats[:], y[:]).then_inc(fin_part, 1)
                dve.wait_ge(fin_part, 5 * g + 5)
                dve.sem_inc(passed, 1)
                dve.bn_aggr(mean_var[:], stats[:]).then_inc(stats_done, 1)

            with dve.Fori(0, B) as b:
                n = 0
                for i in range(XB):
                    s = slice(2 * i * P, (2 * i + 2) * P)
                    split_lo(xT_lo[:, :, s], ps_p[n % 2][:].rearrange("p (c n) -> p c n", c=DC), xT_hi[:, :, s],
                             b * NP + n + 1)
                    n += 1
                for t in range(YB):
                    split_lo(y_lo[:, t, :, 0:D], ps_p[n % 2][:].rearrange("p (j n) -> p j n", j=2), y_hi[:, t, :, 0:D],
                             b * NP + n + 1)
                    n += 1
                make_kind1(b * T, 0, b * H + 1)
                make_kind1(b * T + 1, 1, b * H + 1)
                dve.wait_ge(res_in, (b + 1) * 16)
                dve.sem_inc(passed, 1)
                with dve.Fori(0, H - 1) as i:
                    for j in range(2):
                        g = b * T + 2 * i + j
                        make_kind1(g + 2, j, b * H + i + 2)
                        finish(2 * i + j, g, j)
                for t in (T - 2, T - 1):
                    finish(t, b * T + t, t % 2)


H = 8
HD = D // H
SHIFT_ON_ACT = (2, 4, 7)


def heads_layer(nc, tag, x_in, x_out, adj, g1, b1, wq, bq, wk, bk, wv, bv, wo, bo, B, N):
    T = N // P
    XB, KB, VB, QB = T // 2, DC * N // 512, T // 2, DC * N // 512
    NP = XB + KB + VB + QB
    HALF = 512
    SCALE = float(HD) ** -0.5
    HV = HD + 1
    nA = len(SHIFT_ON_ACT)
    nD = H - nA

    with nc.cleanup_on_exit(), ExitStack() as ctx:
        def sb(name, shape, dt=F32):
            return ctx.enter_context(nc.sbuf_tensor(f"{tag}_{name}", shape, dt))

        def pb(name, shape):
            return ctx.enter_context(nc.psum_tensor(f"{tag}_{name}", shape, F32))

        def sem(name):
            return nc.alloc_semaphore(name=f"{tag}_{name}")

        q_stack = sb("q_stack", [P, H, N], F32R)
        k_stack = sb("k_stack", [P, H, N], F32R)
        q_tile = [sb(f"q_tile{j}", [P, H, P], F32R) for j in range(2)]
        w_hi = [sb(f"w_hi{i}", [P, DC, D], F32R) for i in range(4)]
        w_lo = [sb(f"w_lo{i}", [P, DC, D], F32R) for i in range(4)]
        col = sb("col", [P, 6, DC])
        bcol = sb("bcol", [P, 3, DC])
        bo_row = sb("bo_row", [P, D])
        ident, small, tenth = sb("ident", [P, P]), sb("small", [P, 3]), sb("tenth", [P, 1])
        x_tok, x_res, x_new = sb("x_tok", [P, T, D]), sb("x_res", [P, T, D]), sb("x_new", [P, T, D])
        zT_hi, zT_lo = sb("zT_hi", [P, DC, N], F32R), sb("zT_lo", [P, DC, N], F32R)
        kT_hi, kT_lo = sb("kT_hi", [P, DC, N], F32R), sb("kT_lo", [P, DC, N], F32R)
        v = sb("v", [P, T, H, HV])
        adj_sb = [sb(f"adj_sb{j}", [P, N], I32) for j in range(2)]
        bias = [sb(f"bias{j}", [P, N]) for j in range(2)]
        adj_f, edge = sb("adj_f", [P, N]), sb("edge", [P, N])
        score = [sb(f"score{j}", [P, N]) for j in range(2)]
        prob = [sb(f"prob{j}", [P, T, P]) for j in range(2)]
        row_max = [sb(f"row_max{j}", [P, 1]) for j in range(2)]
        inv, att = sb("inv", [P, H, 1]), sb("att", [P, H, HD])
        attT_hi, attT_lo = sb("attT_hi", [P, DC, P], F32R), sb("attT_lo", [P, DC, P], F32R)
        stats, mean_var, ln_c = sb("stats", [P, T, 6]), sb("mean_var", [P, T, 2]), sb("ln_c", [P, 4, T])

        ps_s = [pb(f"ps_s{j}", [P, N]) for j in range(2)]
        ps_t = pb("ps_t", [P, N])
        ps_o = [pb(f"ps_o{j}", [P, HALF]) for j in range(2)]
        ps_p = [ps_t[:, 0:HALF], ps_t[:, HALF:N]]

        names = ("w_in ready w_part b_ps w_split ones_in x_in_s res_in stored proj_full proj_hi proj_lo "
                 "stat_part stats_done rstd_part rstd_done z_done stacked bias_part bias_made score_full taken "
                 "shifted_d shifted_a turned exp_done out_full inv_done att_done attT_full attT_hi_s attT_lo_s "
                 "wo_full x_done res_s passed")
        s = {n: sem(n) for n in names.split()}
        (w_in, ready, w_part, b_ps, w_split, ones_in, x_in_s, res_in, stored, proj_full, proj_hi, proj_lo,
         stat_part, stats_done, rstd_part, rstd_done, z_done, stacked, bias_part, bias_made, score_full, taken,
         shifted_d, shifted_a, turned, exp_done, out_full, inv_done, att_done, attT_full, attT_hi_s, attT_lo_s,
         wo_full, x_done, res_s, passed) = s.values()
        adj_in = [sem(f"adj_in{j}") for j in range(2)]
        q_in = [sem(f"q_in{j}") for j in range(2)]

        x_in_t = x_in.rearrange("b (t p) d -> b p t d", p=P)
        x_out_t = x_out.rearrange("b (t p) d -> b p t d", p=P)
        adj_t = adj.rearrange("b (t p) m -> b t p m", p=P)
        x_stage = [t[:].rearrange("p t n -> p (t n)")[:, k * DC * D:(k + 1) * DC * D].rearrange("p (c n) -> p c n", c=DC)
                   for t in prob for k in range(2)]
        block = ctx.enter_context(nc.Block())
        HT = T // 2
        NW = 4 + 5 + 1

        @block.sync
        def _(sp):
            for i, w in enumerate((wq, wk, wv, wo)):
                sp.dma_start(x_stage[i], w.rearrange("(c p) n -> p c n", p=P)).then_inc(w_in, 16)
            for i, c in enumerate((g1, b1, bq, bk, bv)):
                sp.dma_start(col[:, i, :].unsqueeze(2), c.rearrange("(c p o) -> p c o", p=P, o=1),
                             allow_slow_non_contiguous=True).then_inc(w_in, 16)
            sp.dma_start(bo_row[:], bo.partition_broadcast(P)).then_inc(w_in, 16)

            def load_tokens(b):
                sp.dma_start(x_tok[:], x_in_t[b]).then_inc(x_in_s, 16)

            def load_residual(b):
                sp.dma_start(x_res[:], x_in_t[b]).then_inc(res_in, 16)

            def load_adj(b, t, j):
                sp.dma_start(adj_sb[j][:], adj_t[b, t]).then_inc(adj_in[j], 16)

            def store(b, t):
                sp.wait_ge(x_done, b * T + t + 3)
                sp.dma_start(x_out_t[b][:, t, :], x_new[:, t, :]).then_inc(stored, 16)

            def stack(dst, parts):
                for r in range(4):
                    for q in range(4):
                        sp.dma_start(dst[32 * r:32 * r + 32, q:H:4, :].bitcast(F32),
                                     parts[r][32 * q:32 * q + 32, :, :].bitcast(F32))\
                          .then_inc(stacked, 16)

            def load_q(b, t, j):
                sp.dma_start(q_tile[j][:].bitcast(F32), q_stack[:, :, bass.ts(t, P)].bitcast(F32)).then_inc(q_in[j], 16)

            def batch(b, last):
                sp.wait_ge(proj_lo, b * NP + XB + KB + 2)
                stack(k_stack, (kT_hi, kT_lo, kT_hi, kT_lo))
                sp.wait_ge(proj_lo, (b + 1) * NP + 2)
                stack(q_stack, (kT_hi, kT_hi, kT_lo, kT_lo))
                if not last:
                    load_tokens(b + 1)
                sp.wait_ge(stacked, (b + 1) * 32 * 16)
                sp.sem_inc(passed, 1)
                load_q(b, 0, 0)
                load_q(b, 1, 1)
                for i in range(HT):
                    for j in range(2):
                        t = 2 * i + j
                        if t + 2 < T:
                            sp.wait_ge(bias_made, b * T + t + 1)
                            load_adj(b, t + 2, j)
                            sp.wait_ge(score_full, (b * T + t + 1) * H)
                            load_q(b, t + 2, j)
                        elif not last:
                            sp.wait_ge(bias_made, b * T + t + 1)
                            load_adj(b + 1, t + 2 - T, j)
                        if t > 0:
                            store(b, t - 1)
                store(b, T - 1)
                if not last:
                    load_residual(b + 1)

            load_tokens(0)
            load_adj(0, 0, 0)
            load_adj(0, 1, 1)
            load_residual(0)
            sp.sem_inc(stored, 16 * T)
            with sp.Fori(0, B - 1) as b:
                batch(b, False)
            batch(B - 1, True)
            sp.wait_ge(stored, 16 * T * (B + 1))

        @block.gpsimd
        def _(pool):
            pool.memset(ident[:], 0.0).then_inc(ready, 1)
            pool.memset(small[:, 0:1], -0.5).then_inc(ready, 1)
            pool.memset(small[:, 1:2], -1.0).then_inc(ready, 1)
            pool.memset(small[:, 2:3], EPS).then_inc(ready, 1)
            pool.memset(tenth[:], 0.1).then_inc(ready, 1)
            pool.wait_ge(ready, 5)
            pool.affine_select(out=ident[:], in_=ident[:], compare_op=ALU.not_equal, fill=1.0,
                               base=0, pattern=[[-1, P]], channel_multiplier=1).then_inc(ready, 1)

            def make_bias(g, j, seen):
                pool.wait_ge(adj_in[j], 16 * seen)
                pool.wait_ge(taken, (g + 1) * H)
                pool.sem_inc(passed, 1)
                pool.tensor_copy(adj_f[:], adj_sb[j][:]).then_inc(bias_part, 1)
                pool.wait_ge(bias_part, 4 * g + 1)
                pool.tensor_tensor(edge[:], adj_f[:], tenth[:].to_broadcast([P, N]), ALU.mult).then_inc(bias_part, 1)
                pool.tensor_scalar(bias[j][:], adj_f[:], 0.0, -BIG, ALU.is_le, ALU.mult).then_inc(bias_part, 1)
                pool.wait_ge(bias_part, 4 * g + 3)
                pool.tensor_tensor(edge[:], edge[:], adj_f[:], ALU.mult).then_inc(bias_part, 1)
                pool.wait_ge(bias_part, 4 * g + 4)
                pool.tensor_tensor(bias[j][:], edge[:], bias[j][:], ALU.add).then_inc(bias_made, 1)

            def norm_consts(b):
                e = [small[:, k:k + 1].to_broadcast([P, T]) for k in range(3)]
                pool.wait_ge(stats_done, (b + 1) * T)
                pool.tensor_tensor(ln_c[:, 0, :], mean_var[:, :, 1], e[2], ALU.add).then_inc(rstd_part, 1)
                pool.wait_ge(rstd_part, 3 * b + 1)
                pool.tensor_tensor(ln_c[:, 1, :], ln_c[:, 0, :], e[0], ALU.pow).then_inc(rstd_part, 1)
                pool.wait_ge(rstd_part, 3 * b + 2)
                pool.tensor_tensor(ln_c[:, 3, :], mean_var[:, :, 0], ln_c[:, 1, :], ALU.mult).then_inc(rstd_part, 1)
                pool.wait_ge(rstd_part, 3 * b + 3)
                pool.tensor_tensor(ln_c[:, 2, :], ln_c[:, 3, :], e[1], ALU.mult).then_inc(rstd_done, 1)

            with pool.Fori(0, B) as b:
                norm_consts(b)
                with pool.Fori(0, HT) as i:
                    for j in range(2):
                        make_bias(b * T + 2 * i + j, j, b * HT + i + 1)

        @block.scalar
        def _(act):
            def shift(g, h, k):
                act.wait_ge(taken, g * H + h + 1 + 2 * H)
                act.activation(score[h % 2][:], score[h % 2][:], ACT.Identity, bias=row_max[h % 2][:], scale=-1.0)\
                   .then_inc(shifted_a, 1)

            def exps(g, h):
                sign = -1.0 if h in SHIFT_ON_ACT else 1.0
                for k in range(2):
                    half = slice(k * T // 2, (k + 1) * T // 2)
                    act.wait_ge(turned, 2 * (g * H + h) + k + 1)
                    act.activation(prob[h % 2][:, half, :], ps_t[:, k * HALF:(k + 1) * HALF].rearrange("p (t n) -> p t n", n=P),
                                   ACT.Exp, scale=sign).then_inc(exp_done, 1)

            def att_high(g, j):
                act.wait_ge(attT_full, g + 1)
                for c in range(DC):
                    act.activation(attT_hi[:, c, :], ps_o[j][:, c * P:(c + 1) * P], ACT.Identity, bias=bcol[:, 2, c:c + 1])\
                       .then_inc(attT_hi_s, 1)

            def tile(b, t, j, first, last):
                g = b * T + t
                for h in range(H):
                    exps(g, h)
                    if h + 1 in SHIFT_ON_ACT:
                        shift(g, h + 1, 0)
                    if h == 3 and not first:
                        att_high(g - 1, 1 - j)
                if last:
                    att_high(g, j)

            def split_hi(dst, ps, at, bias=0.0):
                act.wait_ge(proj_full, at)
                act.activation(dst, ps, ACT.Identity, bias=bias).then_inc(proj_hi, 1)

            act.wait_ge(w_split, 1)
            act.sem_inc(exp_done, 2)
            with act.Fori(0, B) as b:
                act.wait_ge(rstd_done, b + 1)
                act.sem_inc(passed, 1)
                for t in range(T):
                    act.activation(x_tok[:, t, :], x_tok[:, t, :], ACT.Identity, bias=ln_c[:, 2, t:t + 1],
                                   scale=ln_c[:, 1, t:t + 1]).then_inc(z_done, 1)
                n = 0
                for i in range(XB):
                    split_hi(zT_hi[:, :, 2 * i * P:(2 * i + 2) * P], ps_p[n % 2].rearrange("p (c n) -> p c n", c=DC),
                             b * NP + n + 1)
                    n += 1
                for which in (1, 0):
                    for m in range(DC):
                        for i in range(2):
                            if which == 0 and m == 0 and i == 0:
                                act.wait_ge(stacked, (2 * b + 1) * 16 * 16)
                                act.sem_inc(passed, 1)
                            split_hi(kT_hi[:, m, i * HALF:(i + 1) * HALF], ps_p[n % 2], b * NP + n + 1,
                                     bias=bcol[:, which, m:m + 1])
                            n += 1
                    if which == 1:
                        n += VB
                tile(b, 0, 0, True, False)
                tile(b, 1, 1, False, False)
                with act.Fori(1, HT - 1) as i:
                    for j in range(2):
                        tile(b, 2 * i + j, j, False, False)
                tile(b, T - 2, 0, False, False)
                tile(b, T - 1, 1, False, True)

        @block.tensor
        def _(pe):
            def three(out, l_hi, l_lo, r_hi, r_lo, n, last):
                pe.matmul(out, l_hi, r_hi, start=(n == 0), stop=False)
                pe.matmul(out, l_hi, r_lo, start=False, stop=False)
                return pe.matmul(out, l_lo, r_hi, start=False, stop=(n == last))

            pe.wait_ge(w_in, 16 * NW)
            for i in range(3):
                for m in range(DC):
                    for c in range(DC):
                        mm = pe.matmul(ps_o[0][:, i * DC + m:i * DC + m + 1], x_stage[i][:, c, m * P:(m + 1) * P],
                                       col[:, 1, c:c + 1], start=(c == 0), stop=(c == DC - 1))
            mm.then_inc(b_ps, 1)
            pe.wait_ge(ready, 6)
            pe.wait_ge(w_split, 1)
            pe.wait_ge(ones_in, 1)

            def scores(g, h, j):
                for k in range(2):
                    mm = pe.matmul(ps_s[h % 2][:, k * HALF:(k + 1) * HALF], q_tile[j][:, h, :],
                                   k_stack[:, h, k * HALF:(k + 1) * HALF], start=True, stop=True)
                mm.then_inc(score_full, 1)

            def turn(g, h):
                if h in SHIFT_ON_ACT:
                    pe.wait_ge(shifted_a, g * nA + SHIFT_ON_ACT.index(h) + 1)
                else:
                    pe.wait_ge(shifted_d, g * nD + [x for x in range(H) if x not in SHIFT_ON_ACT].index(h) + 1)
                for k in range(2):
                    pe.wait_ge(exp_done, 2 * (g * H + h) + k + 1)
                    for c in range(k * T // 2, (k + 1) * T // 2):
                        mm = pe.transpose(ps_t[:, c * P:(c + 1) * P], score[h % 2][:, c * P:(c + 1) * P], ident[:])
                    mm.then_inc(turned, 1)

            def weigh(g, h, j):
                if h == 0:
                    pe.wait_ge(x_done, g + 1)
                for c in range(T):
                    if c % (T // 2) == 0:
                        pe.wait_ge(exp_done, 2 * (g * H + h) + 2 * c // T + 1 + 2)
                    mm = pe.matmul(ps_o[j][:, h * HV:(h + 1) * HV], prob[h % 2][:, c, :], v[:, c, h, :],
                                   start=(c == 0), stop=(c == T - 1))
                if h == H - 1:
                    mm.then_inc(out_full, 1)

            def turn_att(g, j):
                pe.wait_ge(att_done, g + 1)
                for c in range(DC):
                    mm = pe.transpose(ps_o[j][:, c * P:(c + 1) * P], att[:].rearrange("p h d -> p (h d)")[:, c * P:(c + 1) * P],
                                      ident[:])
                mm.then_inc(attT_full, 1)

            def project_att(g, j):
                pe.wait_ge(attT_lo_s, DC * (g + 1))
                for c in range(DC):
                    mm = three(ps_o[j][:, D:2 * D], attT_hi[:, c, :], attT_lo[:, c, :], w_hi[3][:, c, :], w_lo[3][:, c, :],
                               c, DC - 1)
                mm.then_inc(wo_full, 1)

            def tile(b, i, j, first, last):
                g = b * T + 2 * i + j
                for h in range(H):
                    turn(g, h)
                    if h + 2 < H:
                        scores(g, h + 2, j)
                    elif not last:
                        if h + 2 == H:
                            pe.wait_ge(q_in[1 - j], 16 * (b * HT + i + j + 1))
                        scores(g + 1, h + 2 - H, 1 - j)
                    if h > 0:
                        weigh(g, h - 1, j)
                    elif not first:
                        weigh(g - 1, H - 1, 1 - j)
                    if not first:
                        if h == 2:
                            turn_att(g - 1, 1 - j)
                        if h == 5:
                            project_att(g - 1, 1 - j)
                if last:
                    weigh(g, H - 1, j)
                    turn_att(g, j)
                    project_att(g, j)

            with pe.Fori(0, B) as b:
                n = 0
                for i in range(XB):
                    pe.wait_ge(proj_lo, b * NP + n + 1)
                    pe.wait_ge(z_done, b * T + 2 * i + 2)
                    for c in range(DC):
                        for j in range(2):
                            mm = pe.transpose(ps_p[n % 2][:, (2 * c + j) * P:(2 * c + j + 1) * P],
                                              x_tok[:, 2 * i + j, c * P:(c + 1) * P], ident[:])
                    mm.then_inc(proj_full, 1)
                    n += 1
                pe.wait_ge(proj_lo, b * NP + XB + 2)

                def project_T(which):
                    nonlocal n
                    for m in range(DC):
                        for i in range(2):
                            pe.wait_ge(proj_lo, b * NP + n + 1)
                            for c in range(DC):
                                ws, ts = slice(m * P, (m + 1) * P), slice(i * HALF, (i + 1) * HALF)
                                mm = three(ps_p[n % 2], w_hi[which][:, c, ws], w_lo[which][:, c, ws],
                                           zT_hi[:, c, ts], zT_lo[:, c, ts], c, DC - 1)
                            mm.then_inc(proj_full, 1)
                            n += 1

                project_T(1)
                for i in range(VB):
                    pe.wait_ge(proj_lo, b * NP + n + 1)
                    for j in range(2):
                        ts = slice((2 * i + j) * P, (2 * i + j + 1) * P)
                        for c in range(DC):
                            mm = three(ps_p[n % 2][:, j * D:(j + 1) * D], zT_hi[:, c, ts], zT_lo[:, c, ts],
                                       w_hi[2][:, c, :], w_lo[2][:, c, :], c, DC - 1)
                    mm.then_inc(proj_full, 1)
                    n += 1
                project_T(0)
                pe.wait_ge(proj_lo, (b + 1) * NP + 2)
                pe.wait_ge(q_in[0], 16 * (b * HT + 1))
                scores(b * T, 0, 0)
                scores(b * T, 1, 0)
                tile(b, 0, 0, True, False)
                tile(b, 0, 1, False, False)
                with pe.Fori(1, HT - 1) as i:
                    for j in range(2):
                        tile(b, i, j, False, False)
                tile(b, HT - 1, 0, False, False)
                tile(b, HT - 1, 1, False, True)

        @block.vector
        def _(dve):
            k = 0

            def stepped(ins):
                nonlocal k
                ins.then_inc(w_part, 1)
                k += 1
                dve.wait_ge(w_part, k)

            dve.memset(v[:, :, :, HD:HV], 1.0).then_inc(ones_in, 1)
            dve.sem_inc(proj_lo, 2)
            dve.sem_inc(taken, 2 * H)
            dve.sem_inc(x_done, 2)
            dve.wait_ge(w_in, 16 * NW)
            dve.wait_ge(b_ps, 1)
            stepped(dve.tensor_tensor(bcol[:], ps_o[0][:, 0:3 * DC].rearrange("p (i c) -> p i c", i=3), col[:, 2:5, :], ALU.add))
            stepped(dve.tensor_scalar(bcol[:, 0, :], bcol[:, 0, :], SCALE, None, ALU.mult))
            for i in range(4):
                if i < 3:
                    for c in range(DC):
                        ins = dve.tensor_scalar(x_stage[i][:, c, :], x_stage[i][:, c, :], col[:, 0, c:c + 1],
                                                SCALE if i == 0 else 1.0, ALU.mult, ALU.mult)
                        stepped(ins)
                stepped(dve.tensor_copy(w_hi[i][:], x_stage[i]))
                stepped(dve.tensor_tensor(w_lo[i][:], x_stage[i], w_hi[i][:].bitcast(F32), ALU.subtract))
            dve.sem_inc(w_split, 1)

            def split_lo(dst, ps, hi, at, bias=None):
                dve.wait_ge(proj_hi, at)
                if bias is None:
                    dve.tensor_tensor(dst, ps, hi.bitcast(F32), ALU.subtract).then_inc(proj_lo, 1)
                else:
                    dve.scalar_tensor_tensor(dst, ps, bias, hi.bitcast(F32), ALU.add, ALU.subtract).then_inc(proj_lo, 1)

            def take(g, h, j):
                dve.wait_ge(score_full, g * H + h + 1)
                if h == 0:
                    dve.wait_ge(bias_made, g + 1)
                dve.sem_inc(passed, 1)
                dve.tensor_tensor_reduce(score[h % 2][:], ps_s[h % 2][:], bias[j][:], 1.0, -3.0e38, ALU.add, ALU.max,
                                         row_max[h % 2][:]).then_inc(taken, 1)
                if h not in SHIFT_ON_ACT:
                    dve.wait_ge(taken, g * H + h + 1 + 2 * H)
                    dve.tensor_scalar(score[h % 2][:], score[h % 2][:], row_max[h % 2][:], None, ALU.subtract)\
                       .then_inc(shifted_d, 1)

            def average(g, j):
                dve.wait_ge(out_full, g + 1)
                o = ps_o[j][:, 0:H * HV].rearrange("p (h d) -> p h d", h=H)
                dve.reciprocal(inv[:], o[:, :, HD:HV]).then_inc(inv_done, 1)
                dve.wait_ge(inv_done, g + 1)
                dve.tensor_tensor(att[:], o[:, :, 0:HD], inv[:].to_broadcast([P, H, HD]), ALU.mult).then_inc(att_done, 1)

            def att_low(g, j):
                dve.wait_ge(attT_hi_s, DC * (g + 1))
                for c in range(DC):
                    dve.scalar_tensor_tensor(attT_lo[:, c, :], ps_o[j][:, c * P:(c + 1) * P], bcol[:, 2, c:c + 1],
                                             attT_hi[:, c, :].bitcast(F32), ALU.add, ALU.subtract).then_inc(attT_lo_s, 1)

            def add_residual(t, g, j):
                dve.wait_ge(wo_full, g + 1)
                dve.tensor_tensor(x_new[:, t, :], ps_o[j][:, D:2 * D], x_res[:, t, :], ALU.add).then_inc(x_done, 1)

            def tile(b, t, j, first, last):
                g = b * T + t
                for h in range(H):
                    take(g, h, j)
                    if not first:
                        if h == 2:
                            average(g - 1, 1 - j)
                        if h == 4:
                            att_low(g - 1, 1 - j)
                        if h == 7:
                            add_residual(t - 1, g - 1, 1 - j)
                if last:
                    average(g, j)
                    att_low(g, j)
                    add_residual(t, g, j)

            with dve.Fori(0, B) as b:
                dve.wait_ge(x_in_s, 16 * (b + 1))
                dve.sem_inc(passed, 1)
                for t in range(T):
                    dve.bn_stats(stats[:, t, :], x_tok[:, t, :]).then_inc(stat_part, 1)
                dve.wait_ge(stat_part, (b + 1) * T)
                dve.sem_inc(passed, 1)
                for t in range(T):
                    dve.bn_aggr(mean_var[:, t, :], stats[:, t, :]).then_inc(stats_done, 1)
                dve.wait_ge(res_in, 16 * (b + 1))
                dve.tensor_tensor(x_res[:], x_res[:], bo_row[:].unsqueeze(1).to_broadcast([P, T, D]), ALU.add).then_inc(res_s, 1)
                n = 0
                for i in range(XB):
                    ts = slice(2 * i * P, (2 * i + 2) * P)
                    split_lo(zT_lo[:, :, ts], ps_p[n % 2].rearrange("p (c n) -> p c n", c=DC), zT_hi[:, :, ts],
                             b * (NP - VB) + i + 1)
                    n += 1
                for which in (1, 0):
                    for m in range(DC):
                        for i in range(2):
                            ts = slice(i * HALF, (i + 1) * HALF)
                            at = b * (NP - VB) + XB + (1 - which) * KB + 2 * m + i + 1
                            split_lo(kT_lo[:, m, ts], ps_p[n % 2], kT_hi[:, m, ts], at, bias=bcol[:, which, m:m + 1])
                            n += 1
                    if which == 1:
                        for i in range(VB):
                            dve.wait_ge(proj_full, b * NP + n + 1)
                            dve.tensor_copy(v[:, 2 * i:2 * i + 2, :, 0:HD],
                                            ps_p[n % 2].rearrange("p (t h d) -> p t h d", t=2, h=H)).then_inc(proj_lo, 1)
                            n += 1
                dve.wait_ge(res_s, b + 1)
                dve.wait_ge(stored, 16 * T * (b + 1))
                dve.sem_inc(passed, 1)
                tile(b, 0, 0, True, False)
                tile(b, 1, 1, False, False)
                with dve.Fori(1, HT - 1) as i:
                    for j in range(2):
                        tile(b, 2 * i + j, j, False, False)
                tile(b, T - 2, 0, False, False)
                tile(b, T - 1, 1, False, True)


FW = 4 * D
FT = FW // P


def mlp_layer(nc, tag, x_in, x_out, g2, b2n, w1, b1, w2, b2, B, N):
    HALF = 512
    CT = HALF // P
    NC = B * N // HALF

    with nc.cleanup_on_exit(), ExitStack() as ctx:
        def sb(name, shape, dt=F32):
            return ctx.enter_context(nc.sbuf_tensor(f"{tag}_{name}", shape, dt))

        def pb(name, shape):
            return ctx.enter_context(nc.psum_tensor(f"{tag}_{name}", shape, F32))

        def sem(name):
            return nc.alloc_semaphore(name=f"{tag}_{name}")

        w1_raw, w2_raw = sb("w1_raw", [P, DC, FW]), sb("w2_raw", [P, FT, D])
        w1_hi, w1_lo = sb("w1_hi", [P, DC, FW], F32R), sb("w1_lo", [P, DC, FW], F32R)
        w2_hi, w2_lo = sb("w2_hi", [P, FT, D], F32R), sb("w2_lo", [P, FT, D], F32R)
        col = sb("col", [P, 2, DC])
        b1_col, b1_all = sb("b1_col", [P, FT]), sb("b1_all", [P, FT])
        b2_row = sb("b2_row", [P, D])
        ident, small = sb("ident", [P, P]), sb("small", [P, 3])
        x_c = [sb(f"x_c{j}", [P, CT, D]) for j in range(2)]
        x_new = [sb(f"x_new{j}", [P, CT, D]) for j in range(2)]
        z = sb("z", [P, CT, D])
        zT_hi, zT_lo = sb("zT_hi", [P, DC, HALF], F32R), sb("zT_lo", [P, DC, HALF], F32R)
        h = [sb(f"h{i}", [P, HALF]) for i in range(2)]
        h_hi, h_lo = sb("h_hi", [P, FT, HALF], F32R), sb("h_lo", [P, FT, HALF], F32R)
        stats, mean_var, ln_c = sb("stats", [P, CT, 6]), sb("mean_var", [P, CT, 2]), sb("ln_c", [P, 4, CT])

        ps_z = pb("ps_z", [P, DC, HALF])
        ps_h = [pb(f"ps_h{i}", [P, HALF]) for i in range(2)]
        ps_o = [pb(f"ps_o{i}", [P, HALF]) for i in range(2)]

        names = ("w_in ready w_part b_ps w_split stored z_full zT_high zT_low h_full h_gelu h_high h_low_d h_low_p "
                 "stat_part stats_done rstd_part rstd_done z_done res_done out_full x_done passed")
        (w_in, ready, w_part, b_ps, w_split, stored, z_full, zT_high, zT_low, h_full, h_gelu, h_high, h_low_d, h_low_p,
         stat_part, stats_done, rstd_part, rstd_done, z_done, res_done, out_full, x_done, passed) = (
            sem(n) for n in names.split())
        x_in_s = [sem(f"x_in{j}") for j in range(2)]

        xi = x_in.rearrange("b (c t p) d -> (b c) p t d", p=P, t=CT)
        xo = x_out.rearrange("b (c t p) d -> (b c) p t d", p=P, t=CT)
        block = ctx.enter_context(nc.Block())
        NP2 = NC // 2

        @block.sync
        def _(sp):
            sp.dma_start(w1_raw[:], w1.rearrange("(c p) n -> p c n", p=P)).then_inc(w_in, 16)
            sp.dma_start(w2_raw[:], w2.rearrange("(c p) n -> p c n", p=P)).then_inc(w_in, 16)
            for i, c in enumerate((g2, b2n)):
                sp.dma_start(col[:, i, :].unsqueeze(2), c.rearrange("(c p o) -> p c o", p=P, o=1),
                             allow_slow_non_contiguous=True).then_inc(w_in, 16)
            sp.dma_start(b1_col[:].unsqueeze(2), b1.rearrange("(c p o) -> p c o", p=P, o=1),
                         allow_slow_non_contiguous=True).then_inc(w_in, 16)
            sp.dma_start(b2_row[:], b2.partition_broadcast(P)).then_inc(w_in, 16)
            for j in range(2):
                sp.dma_start(x_c[j][:], xi[j]).then_inc(x_in_s[j], 16)
            sp.sem_inc(stored, 16 * 2)

            def store(c, j):
                sp.wait_ge(x_done, CT * (c + 1) + 2)
                sp.dma_start(xo[c], x_new[j][:]).then_inc(stored, 16)

            with sp.Fori(0, NP2 - 1) as i:
                for j in range(2):
                    store(2 * i + j, j)
                    sp.dma_start(x_c[j][:], xi[2 * i + 2 + j]).then_inc(x_in_s[j], 16)
            for j in range(2):
                store(NC - 2 + j, j)
            sp.wait_ge(stored, 16 * (NC + 2))

        @block.gpsimd
        def _(pool):
            pool.memset(ident[:], 0.0).then_inc(ready, 1)
            pool.memset(small[:, 0:1], -0.5).then_inc(ready, 1)
            pool.memset(small[:, 1:2], -1.0).then_inc(ready, 1)
            pool.memset(small[:, 2:3], EPS).then_inc(ready, 1)
            pool.wait_ge(ready, 4)
            pool.affine_select(out=ident[:], in_=ident[:], compare_op=ALU.not_equal, fill=1.0,
                               base=0, pattern=[[-1, P]], channel_multiplier=1).then_inc(ready, 1)
            pool.wait_ge(w_in, 16 * 6)
            pool.sem_inc(h_low_p, 1)
            e = [small[:, k:k + 1].to_broadcast([P, CT]) for k in range(3)]

            def norm_consts(c):
                pool.wait_ge(stats_done, (c + 1) * CT)
                pool.tensor_tensor(ln_c[:, 0, :], mean_var[:, :, 1], e[2], ALU.add).then_inc(rstd_part, 1)
                pool.wait_ge(rstd_part, 3 * c + 1)
                pool.tensor_tensor(ln_c[:, 1, :], ln_c[:, 0, :], e[0], ALU.pow).then_inc(rstd_part, 1)
                pool.wait_ge(rstd_part, 3 * c + 2)
                pool.tensor_tensor(ln_c[:, 3, :], mean_var[:, :, 0], ln_c[:, 1, :], ALU.mult).then_inc(rstd_part, 1)
                pool.wait_ge(rstd_part, 3 * c + 3)
                pool.tensor_tensor(ln_c[:, 2, :], ln_c[:, 3, :], e[1], ALU.mult).then_inc(rstd_done, 1)

            def residual(c, j):
                pool.wait_ge(z_done, CT * (c + 1))
                pool.tensor_tensor(x_c[j][:], x_c[j][:], b2_row[:].unsqueeze(1).to_broadcast([P, CT, D]), ALU.add)\
                    .then_inc(res_done, 1)

            def chunk(c, j, last):
                if not last:
                    norm_consts(c + 1)
                for f in range(1, FT, 2):
                    pool.wait_ge(h_high, FT * c + f + 1)
                    pool.tensor_tensor(h_lo[:, f, :], h[f % 2][:], h_hi[:, f, :].bitcast(F32), ALU.subtract).then_inc(h_low_p, 1)
                    if f == 3 and not last:
                        residual(c + 1, 1 - j)

            norm_consts(0)
            residual(0, 0)
            with pool.Fori(0, NP2 - 1) as i:
                for j in range(2):
                    chunk(2 * i + j, j, False)
            chunk(NC - 2, 0, False)
            chunk(NC - 1, 1, True)

        @block.scalar
        def _(act):
            def normalise(c, j):
                act.wait_ge(rstd_done, c + 1)
                act.sem_inc(passed, 1)
                for t in range(CT):
                    act.activation(z[:, t, :], x_c[j][:, t, :], ACT.Identity, bias=ln_c[:, 2, t:t + 1],
                                   scale=ln_c[:, 1, t:t + 1]).then_inc(z_done, 1)

            def split_high(c):
                for d in range(DC):
                    act.wait_ge(z_full, DC * c + d + 1)
                    act.activation(zT_hi[:, d, :], ps_z[:, d, :], ACT.Identity).then_inc(zT_high, 1)

            def chunk(c, j, last):
                for f in range(FT):
                    act.wait_ge(h_full, FT * c + f + 1)
                    act.wait_ge(h_low_p if f % 2 else h_low_d, FT // 2 * c + f // 2 + 1)
                    act.activation(h[f % 2][:], ps_h[f % 2][:], ACT.Gelu, bias=b1_all[:, f:f + 1]).then_inc(h_gelu, 1)
                    if f == 1 and not last:
                        normalise(c + 1, 1 - j)
                if not last:
                    split_high(c + 1)

            act.wait_ge(w_split, 1)
            act.sem_inc(h_gelu, 2)
            normalise(0, 0)
            split_high(0)
            with act.Fori(0, NP2 - 1) as i:
                for j in range(2):
                    chunk(2 * i + j, j, False)
            chunk(NC - 2, 0, False)
            chunk(NC - 1, 1, True)

        @block.tensor
        def _(pe):
            def three(out, l_hi, l_lo, r_hi, r_lo, n, last):
                pe.matmul(out, l_hi, r_hi, start=(n == 0), stop=False)
                pe.matmul(out, l_hi, r_lo, start=False, stop=False)
                return pe.matmul(out, l_lo, r_hi, start=False, stop=(n == last))

            pe.wait_ge(w_in, 16 * 6)
            for f in range(FT):
                for c in range(DC):
                    mm = pe.matmul(ps_h[0][:, f:f + 1], w1_raw[:, c, f * P:(f + 1) * P], col[:, 1, c:c + 1],
                                   start=(c == 0), stop=(c == DC - 1))
            mm.then_inc(b_ps, 1)
            pe.wait_ge(ready, 5)
            pe.wait_ge(w_split, 1)

            def turn(c):
                pe.wait_ge(z_done, CT * (c + 1))
                for d in range(DC):
                    for t in range(CT):
                        mm = pe.transpose(ps_z[:, d, t * P:(t + 1) * P], z[:, t, d * P:(d + 1) * P], ident[:])
                    mm.then_inc(z_full, 1)

            def chunk(c, j, last):
                pe.wait_ge(zT_low, DC * (c + 1))
                for f in range(FT):
                    pe.wait_ge(h_gelu, FT * c + f + 1)
                    for d in range(DC):
                        s = slice(f * P, (f + 1) * P)
                        mm = three(ps_h[f % 2][:], w1_hi[:, d, s], w1_lo[:, d, s], zT_hi[:, d, :], zT_lo[:, d, :], d, DC - 1)
                    mm.then_inc(h_full, 1)
                if not last:
                    turn(c + 1)
                pe.wait_ge(h_low_d, FT // 2 * (c + 1) + 1)
                pe.wait_ge(h_low_p, FT // 2 * (c + 1) + 1)
                for t in range(CT):
                    pe.wait_ge(x_done, CT * c + t + 1)
                    s = slice(t * P, (t + 1) * P)
                    for f in range(FT):
                        mm = three(ps_o[t % 2][:, 0:D], h_hi[:, f, s], h_lo[:, f, s], w2_hi[:, f, :], w2_lo[:, f, :], f, FT - 1)
                    mm.then_inc(out_full, 1)

            turn(0)
            with pe.Fori(0, NP2 - 1) as i:
                for j in range(2):
                    chunk(2 * i + j, j, False)
            chunk(NC - 2, 0, False)
            chunk(NC - 1, 1, True)

        @block.vector
        def _(dve):
            k = 0

            def stepped(ins):
                nonlocal k
                ins.then_inc(w_part, 1)
                k += 1
                dve.wait_ge(w_part, k)

            dve.wait_ge(w_in, 16 * 6)
            dve.wait_ge(b_ps, 1)
            stepped(dve.tensor_tensor(b1_all[:], ps_h[0][:, 0:FT], b1_col[:], ALU.add))
            for c in range(DC):
                stepped(dve.tensor_scalar(w1_raw[:, c, :], w1_raw[:, c, :], col[:, 0, c:c + 1], None, ALU.mult))
            stepped(dve.tensor_copy(w1_hi[:], w1_raw[:]))
            stepped(dve.tensor_tensor(w1_lo[:], w1_raw[:], w1_hi[:].bitcast(F32), ALU.subtract))
            stepped(dve.tensor_copy(w2_hi[:], w2_raw[:]))
            stepped(dve.tensor_tensor(w2_lo[:], w2_raw[:], w2_hi[:].bitcast(F32), ALU.subtract))
            dve.sem_inc(w_split, 1)
            dve.sem_inc(x_done, 2)
            dve.sem_inc(h_low_d, 1)

            def statistics(c, j, seen):
                dve.wait_ge(x_in_s[j], 16 * seen)
                dve.sem_inc(passed, 1)
                for t in range(CT):
                    dve.bn_stats(stats[:, t, :], x_c[j][:, t, :]).then_inc(stat_part, 1)
                dve.wait_ge(stat_part, (c + 1) * CT)
                dve.sem_inc(passed, 1)
                for t in range(CT):
                    dve.bn_aggr(mean_var[:, t, :], stats[:, t, :]).then_inc(stats_done, 1)

            def split_low(c):
                for d in range(DC):
                    dve.wait_ge(zT_high, DC * c + d + 1)
                    dve.tensor_tensor(zT_lo[:, d, :], ps_z[:, d, :], zT_hi[:, d, :].bitcast(F32), ALU.subtract)\
                       .then_inc(zT_low, 1)

            def chunk(c, j, last, seen):
                if not last:
                    statistics(c + 1, 1 - j, seen)
                for f in range(FT):
                    dve.wait_ge(h_gelu, FT * c + f + 1 + 2)
                    dve.tensor_copy(h_hi[:, f, :], h[f % 2][:]).then_inc(h_high, 1)
                    if f % 2 == 0:
                        dve.wait_ge(h_high, FT * c + f + 1)
                        dve.tensor_tensor(h_lo[:, f, :], h[f % 2][:], h_hi[:, f, :].bitcast(F32), ALU.subtract)\
                           .then_inc(h_low_d, 1)
                if not last:
                    split_low(c + 1)
                dve.wait_ge(stored, 16 * (c + 1))
                dve.wait_ge(res_done, c + 1)
                dve.sem_inc(passed, 1)
                for t in range(CT):
                    dve.wait_ge(out_full, CT * c + t + 1)
                    dve.tensor_tensor(x_new[j][:, t, :], ps_o[t % 2][:, 0:D], x_c[j][:, t, :], ALU.add).then_inc(x_done, 1)

            statistics(0, 0, 1)
            split_low(0)
            with dve.Fori(0, NP2 - 1) as i:
                chunk(2 * i, 0, False, i + 1)
                chunk(2 * i + 1, 1, False, i + 2)
            chunk(NC - 2, 0, False, NP2)
            chunk(NC - 1, 1, True, NP2 + 1)


def graph_net(nc, x, adj, adj_turned, ln1_g, ln1_b, ln2_g, ln2_b, wq0, bq0, wk0, bk0, wv0, bv0, wo0, bo0, w1, b1, w2, b2,
              w_dir, b_dir, gamma1, beta1, wq2, wk2, wv2, wo2, bo2, gamma2, beta2, wq3, bq3, wk3, bk3, wc3, gamma3, beta3,
              out):
    B, N, _ = x.shape
    mid = [nc.dram_tensor(f"x_layer{i}", [B, N, D], F32).ap() for i in range(5)]
    heads_layer(nc, "heads", x, mid[0], adj, ln1_g, ln1_b, wq0, bq0, wk0, bk0, wv0, bv0, wo0, bo0, B, N)
    mlp_layer(nc, "mlp", mid[0], mid[1], ln2_g, ln2_b, w1, b1, w2, b2, B, N)
    direction_layer(nc, "dir", mid[1], mid[2], adj_turned, w_dir, b_dir, gamma1, beta1, B, N)
    attention_layer(nc, "fold", mid[2], mid[3], adj, wq2, wk2, wv2, wo2, None, None, bo2, gamma2, beta2,
                    float(D) ** -0.5, B, N)
    L, _, F = wq3.shape
    for k in range(L):
        attention_layer(nc, f"att{k}", mid[3 + k], out if k == L - 1 else mid[4 + k], adj, wq3[k], wk3[k], wc3[k], None,
                        bq3[k], bk3[k], None, gamma3[k], beta3[k], float(F) ** -0.5, B, N)


_INS = ["x", "adj", "adj_turned", "L0_gnn_ln1_g", "L0_gnn_ln1_b", "L0_gnn_ln2_g", "L0_gnn_ln2_b",
        "L0_gnn_wq", "L0_gnn_bq", "L0_gnn_wk", "L0_gnn_bk", "L0_gnn_wv", "L0_gnn_bv", "L0_gnn_wo", "L0_gnn_bo",
        "L0_gnn_w1", "L0_gnn_b1", "L0_gnn_w2", "L0_gnn_b2", "L1_gnn_W", "L1_gnn_b", "L1_gnn_gamma", "L1_gnn_beta",
        "L2_gnn_Wq", "L2_gnn_Wk", "L2_gnn_Wv", "L2_gnn_Wo", "L2_gnn_bo", "L2_gnn_gamma", "L2_gnn_beta",
        "L3_gnn_Wq", "L3_gnn_bq", "L3_gnn_Wk", "L3_gnn_bk", "L3_gnn_Wc", "L3_gnn_ln_g", "L3_gnn_ln_b"]


def kernel(**inputs):
    import numpy as _np
    import concourse.bacc as _bacc
    from concourse import mybir as _mybir
    from concourse.bass_utils import run_bass_kernel_spmd as _run

    data = dict(inputs)
    adj = _np.asarray(data["adj"])
    B, N, _ = adj.shape
    data["adj_turned"] = adj.reshape(B, N // 128, 128, N // 128, 128).transpose(0, 1, 4, 3, 2)
    for name in ("L2_gnn_Wq", "L2_gnn_Wk", "L2_gnn_Wv"):
        data[name] = _np.asarray(data[name]).T
    for name in ("L3_gnn_Wq", "L3_gnn_Wk", "L3_gnn_Wc"):
        data[name] = _np.asarray(data[name]).transpose(0, 2, 1)

    nc = _bacc.Bacc("TRN2", target_bir_lowering=False, num_devices=1)
    arrays, args = {}, []
    for name in _INS:
        a = _np.ascontiguousarray(data[name])
        arrays[f"in_{name}_dram"] = a
        args.append(nc.dram_tensor(f"in_{name}_dram", a.shape, _mybir.dt.from_np(a.dtype), kind="ExternalInput").ap())
    args.append(nc.dram_tensor("out_0_dram", data["x"].shape, _mybir.dt.float32, kind="ExternalOutput").ap())
    graph_net(nc, *args)
    r = _run(nc, [arrays], core_ids=[0])
    return r.results[0]["out_0_dram"]
```

```python
import concourse.bass as bass
from concourse import mybir
from contextlib import ExitStack

F32 = mybir.dt.float32
F32R = mybir.dt.float32r
I32 = mybir.dt.int32
ALU = mybir.AluOpType
ACT = mybir.ActivationFunctionType

P = 128
D = 256
DC = D // P
BIG = 1.0e30
EPS = 1.0e-5
DV = D + 2


def attention_layer(nc, tag, x_in, x_out, adj, wq_a, wk_a, wv_a, wo_a, bq, bk, bo, gamma, beta,
                    score_scale, B, N):
    folded = wo_a is not None
    T = N // P
    QC = DC if folded else 1
    KC = DC if folded else 1
    XB = T // 2
    KB = 0 if folded else N // 512
    VB = T // 2
    NP = XB + KB + VB
    HALF = 512

    with nc.cleanup_on_exit(), ExitStack() as ctx:
        def sb(name, shape, dt=F32):
            return ctx.enter_context(nc.sbuf_tensor(f"{tag}_{name}", shape, dt))

        def pb(name, shape):
            return ctx.enter_context(nc.psum_tensor(f"{tag}_{name}", shape, F32))

        def sem(name):
            return nc.alloc_semaphore(name=f"{tag}_{name}")

        w_raw = sb("w_raw", [P, 4 * DC * D])
        QW = D if folded else P
        wq_hi, wq_lo = sb("wq_hi", [P, DC, QW], F32R), sb("wq_lo", [P, DC, QW], F32R)
        wv_hi, wv_lo = sb("wv_hi", [P, DC, D], F32R), sb("wv_lo", [P, DC, D], F32R)
        if not folded:
            wk_hi, wk_lo = sb("wk_hi", [P, DC, P], F32R), sb("wk_lo", [P, DC, P], F32R)
            bqk = sb("bqk", [P, 2])
        else:
            bo_row = sb("bo_row", [P, D])
        w_fold = sb("w_fold", [P, 2, DC, D])
        gamma_row, beta_row = sb("gamma_row", [P, D]), sb("beta_row", [P, D])
        ident = sb("ident", [P, P])
        x_tok = sb("x_tok", [P, T, D])
        x_res = sb("x_res", [P, T, D])
        x_new = sb("x_new", [P, T, D])
        xT_hi, xT_lo = sb("xT_hi", [P, DC, N], F32R), sb("xT_lo", [P, DC, N], F32R)
        if folded:
            kT_hi, kT_lo = xT_hi, xT_lo
        else:
            kT_hi, kT_lo = sb("kT_hi", [P, 1, N], F32R), sb("kT_lo", [P, 1, N], F32R)
        v_hi, v_lo = sb("v_hi", [P, T, DV], F32R), sb("v_lo", [P, T, DV], F32R)
        qT_hi, qT_lo = sb("qT_hi", [P, QC, P], F32R), sb("qT_lo", [P, QC, P], F32R)
        adj_sb = sb("adj_sb", [P, T, N], I32)
        mask_bias = sb("mask_bias", [P, N])
        score = sb("score", [P, N])
        prob = sb("prob", [P, T, P])
        prob_hi, prob_lo = sb("prob_hi", [P, T, P], F32R), sb("prob_lo", [P, T, P], F32R)
        row_max = sb("row_max", [P, 1])
        has_key = sb("has_key", [P, 1])
        inv = sb("inv", [P, 2])
        y = sb("y", [P, D])
        stats = sb("stats", [P, 6])
        mean_var = sb("mean_var", [P, 2])
        ln_c = sb("ln_c", [P, 4])
        small = sb("small", [P, 3])

        ps_s = pb("ps_s", [P, N])
        ps_t = pb("ps_t", [P, N])
        ps_o = pb("ps_o", [P, HALF])
        ps_q = pb("ps_q", [P, HALF])
        ps_p = [pb(f"ps_p{i}", [P, HALF]) for i in range(2)]

        w_in, ready, w_ps, w_part = sem("w_in"), sem("ready"), sem("w_ps"), sem("w_part")
        x_in_s, res_in, adj_in, stored = sem("x_in"), sem("res_in"), sem("adj_in"), sem("stored")
        has_key_s, inv_s, stats_part, res_s = sem("has_key_s"), sem("inv_s"), sem("stats_part"), sem("res_s")
        proj_full, proj_hi, proj_lo = sem("proj_full"), sem("proj_hi"), sem("proj_lo")
        q_full, q_hi, q_lo = sem("q_full"), sem("q_hi"), sem("q_lo")
        score_full, shifted, turned = sem("score_full"), sem("shifted"), sem("turned")
        bias_made, bias_used = sem("bias_made"), sem("bias_used")
        exp_done, p_hi, p_lo, p_lo_b = sem("exp_done"), sem("p_hi"), sem("p_lo"), sem("p_lo_b")
        out_full, out_read, stats_done = sem("out_full"), sem("out_read"), sem("stats_done")
        rstd_part, rstd_done, normed, new_part, new_done = (sem("rstd_part"), sem("rstd_done"),
                                                            sem("normed"), sem("new_part"), sem("new_done"))
        step = sem("step")
        dve0 = sem("dve0")
        passed = sem("passed")

        x_in_t = x_in.rearrange("b (t p) d -> b p t d", p=P)
        x_out_t = x_out.rearrange("b (t p) d -> b p t d", p=P)
        adj_t = adj.rearrange("b (t p) m -> b t p m", p=P)
        raw = [w_raw[:, i * DC * D:(i + 1) * DC * D] for i in range(4)]

        def chunks(w):
            return w.rearrange("(c p) n -> p c n", p=P)

        block = ctx.enter_context(nc.Block())

        @block.sync
        def _(sp):
            weights = [wq_a, wk_a, wv_a] + ([wo_a] if folded else [])
            for i, w in enumerate(weights):
                n = w.shape[1]
                sp.dma_start(raw[i][:, 0:DC * n].rearrange("p (c n) -> p c n", c=DC), chunks(w)).then_inc(w_in, 16)
            sp.dma_start(gamma_row[:], gamma.partition_broadcast(P)).then_inc(w_in, 16)
            sp.dma_start(beta_row[:], beta.partition_broadcast(P)).then_inc(w_in, 16)
            if folded:
                sp.dma_start(bo_row[:], bo.partition_broadcast(P)).then_inc(w_in, 16)
            else:
                sp.dma_start(bqk[:, 0:1], bq.rearrange("(p o) -> p o", o=1)).then_inc(w_in, 16)
                sp.dma_start(bqk[:, 1:2], bk.rearrange("(p o) -> p o", o=1)).then_inc(w_in, 16)

            def load_tokens(b):
                sp.dma_start(x_tok[:], x_in_t[b]).then_inc(x_in_s, 16)

            def load_adj(b, t):
                sp.dma_start(adj_sb[:, t, :], adj_t[b, t]).then_inc(adj_in, 16)

            def load_residual(b):
                sp.dma_start(x_res[:], x_in_t[b]).then_inc(res_in, 16)

            def store(b, t):
                sp.wait_ge(new_done, b * T + t + 1)
                sp.dma_start(x_out_t[b][:, t, :], x_new[:, t, :]).then_inc(stored, 16)

            load_tokens(0)
            for t in range(T):
                load_adj(0, t)
            load_residual(0)
            sp.sem_inc(stored, 16 * T)
            with sp.Fori(0, B - 1) as b:
                sp.wait_ge(proj_full, b * NP + XB)
                load_tokens(b + 1)
                for t in range(T):
                    sp.wait_ge(bias_made, b * T + t + 1)
                    load_adj(b + 1, t)
                    if t == T - 1:
                        sp.wait_ge(out_read, (b + 1) * T + 1)
                        load_residual(b + 1)
                    store(b, t)
            for t in range(T):
                store(B - 1, t)
            sp.wait_ge(stored, 16 * T * (B + 1))

        @block.gpsimd
        def _(pool):
            pool.memset(ident[:], 0.0).then_inc(ready, 1)
            pool.memset(small[:, 0:1], -0.5).then_inc(ready, 1)
            pool.memset(small[:, 1:2], -1.0).then_inc(ready, 1)
            pool.memset(small[:, 2:3], EPS).then_inc(ready, 1)
            pool.wait_ge(ready, 4)
            pool.affine_select(out=ident[:], in_=ident[:], compare_op=ALU.not_equal, fill=1.0,
                               base=0, pattern=[[-1, P]], channel_multiplier=1).then_inc(ready, 1)
            pool.wait_ge(w_in, 16 * (7 if folded else 7))

            def p_low(g):
                pool.wait_ge(p_hi, 2 * g + 2)
                pool.tensor_tensor(prob_lo[:, T // 2:T, :], prob[:, T // 2:T, :], prob_hi[:, T // 2:T, :].bitcast(F32),
                                   ALU.subtract).then_inc(p_lo_b, 1)

            def norm_consts(g):
                pool.wait_ge(stats_done, g + 1)
                pool.tensor_tensor(ln_c[:, 0:1], mean_var[:, 1:2], small[:, 2:3], ALU.add).then_inc(rstd_part, 1)
                pool.wait_ge(rstd_part, 3 * g + 1)
                pool.tensor_tensor(ln_c[:, 1:2], ln_c[:, 0:1], small[:, 0:1], ALU.pow).then_inc(rstd_part, 1)
                pool.wait_ge(rstd_part, 3 * g + 2)
                pool.tensor_tensor(ln_c[:, 3:4], mean_var[:, 0:1], ln_c[:, 1:2], ALU.mult).then_inc(rstd_part, 1)
                pool.wait_ge(rstd_part, 3 * g + 3)
                pool.tensor_tensor(ln_c[:, 2:3], ln_c[:, 3:4], small[:, 1:2], ALU.mult).then_inc(rstd_done, 1)

            def affine(t, g):
                pool.wait_ge(normed, g + 2)
                pool.sem_inc(passed, 1)
                pool.tensor_tensor(x_new[:, t, :], x_new[:, t, :], gamma_row[:], ALU.mult).then_inc(new_part, 1)
                pool.wait_ge(new_part, g + 1)
                pool.sem_inc(passed, 1)
                pool.tensor_tensor(x_new[:, t, :], x_new[:, t, :], beta_row[:], ALU.add).then_inc(new_done, 1)

            with pool.Fori(0, B) as b:
                p_low(b * T)
                norm_consts(b * T)
                with pool.Fori(0, T - 1) as t:
                    g = b * T + t
                    p_low(g + 1)
                    affine(t, g)
                    norm_consts(g + 1)
                affine(T - 1, b * T + T - 1)

        @block.scalar
        def _(act):
            def split_hi(dst, ps, full, at, done, bias=0.0):
                act.wait_ge(full, at)
                act.activation(dst, ps, ACT.Identity, bias=bias).then_inc(done, 1)

            def q_evac(g):
                act.wait_ge(q_full, g + 1)
                act.activation(qT_hi[:], ps_q[:, 0:QC * P].rearrange("p (c n) -> p c n", c=QC), ACT.Identity,
                               bias=bqk[:, 0:1] if not folded else 0.0).then_inc(q_hi, 1)

            def exps(g):
                for h in range(2):
                    half = slice(h * T // 2, (h + 1) * T // 2)
                    act.wait_ge(turned, 2 * g + h + 1)
                    act.activation(prob[:, half, :], ps_t[:, h * HALF:(h + 1) * HALF].rearrange("p (t n) -> p t n", n=P),
                                   ACT.Exp).then_inc(exp_done, 1)
                    act.wait_ge(exp_done, 2 * g + h + 1)
                    act.activation(prob_hi[:, half, :], prob[:, half, :], ACT.Copy).then_inc(p_hi, 1)

            def normalise(t, g):
                act.wait_ge(rstd_done, g + 1)
                act.activation(x_new[:, t, :], y[:], ACT.Identity, bias=ln_c[:, 2:3], scale=ln_c[:, 1:2]).then_inc(normed, 1)

            act.wait_ge(w_in, 16 * 7)
            act.sem_inc(normed, 1)
            with act.Fori(0, B) as b:
                n = 0
                for i in range(XB):
                    split_hi(xT_hi[:, :, 2 * i * P:(2 * i + 2) * P], ps_p[n % 2][:].rearrange("p (c n) -> p c n", c=DC),
                             proj_full, b * NP + n + 1, proj_hi)
                    n += 1
                for i in range(KB):
                    split_hi(kT_hi[:, 0, i * HALF:(i + 1) * HALF], ps_p[n % 2][:], proj_full, b * NP + n + 1, proj_hi,
                             bias=bqk[:, 1:2])
                    n += 1
                for i in range(VB):
                    split_hi(v_hi[:, 2 * i:2 * i + 2, 0:D], ps_p[n % 2][:].rearrange("p (t n) -> p t n", n=D),
                             proj_full, b * NP + n + 1, proj_hi)
                    n += 1
                q_evac(b * T)
                q_evac(b * T + 1)
                exps(b * T)
                act.wait_ge(stored, 16 * T * (b + 1))
                q_evac(b * T + 2)
                with act.Fori(1, T - 2) as t:
                    g = b * T + t
                    exps(g)
                    normalise(t - 1, g - 1)
                    q_evac(g + 2)
                for t in (T - 2, T - 1):
                    exps(b * T + t)
                    normalise(t - 1, b * T + t - 1)
                normalise(T - 1, b * T + T - 1)

        @block.tensor
        def _(pe):
            pe.wait_ge(ready, 5)
            pe.wait_ge(w_in, 16 * 7)
            if folded:
                for j in range(2):
                    l = raw[2 * j].rearrange("p (c n) -> p c n", c=DC)
                    r = raw[2 * j + 1].rearrange("p (c n) -> p c n", c=DC)
                    for m in range(DC):
                        for c in range(DC):
                            mm = pe.matmul(ps_p[j][:, m * D:(m + 1) * D], l[:, c, m * P:(m + 1) * P], r[:, c, :],
                                           start=(c == 0), stop=(c == DC - 1))
                    mm.then_inc(w_ps, 1)
            pe.wait_ge(w_part, 1)

            def three(out, l_hi, l_lo, r_hi, r_lo, n, last):
                first = n == 0
                pe.matmul(out, l_hi, r_hi, start=first, stop=False)
                pe.matmul(out, l_hi, r_lo, start=False, stop=False)
                return pe.matmul(out, l_lo, r_hi, start=False, stop=(n == last))

            def q_tile(t, g):
                pe.wait_ge(q_lo, g + 1)
                for m in range(QC):
                    for c in range(DC):
                        mm = three(ps_q[:, m * P:(m + 1) * P], wq_hi[:, c, m * P:(m + 1) * P], wq_lo[:, c, m * P:(m + 1) * P],
                                   xT_hi[:, c, bass.ts(t, P)], xT_lo[:, c, bass.ts(t, P)], c, DC - 1)
                mm.then_inc(q_full, 1)

            def scores(g):
                pe.wait_ge(q_lo, g + 2)
                for h in range(2):
                    for c in range(KC):
                        mm = three(ps_s[:, h * HALF:(h + 1) * HALF], qT_hi[:, c, :], qT_lo[:, c, :],
                                   kT_hi[:, c, h * HALF:(h + 1) * HALF], kT_lo[:, c, h * HALF:(h + 1) * HALF], c, KC - 1)
                mm.then_inc(score_full, 1)

            def turn(g):
                pe.wait_ge(shifted, g + 1)
                for h in range(2):
                    for k in range(h * T // 2, (h + 1) * T // 2):
                        mm = pe.transpose(ps_t[:, k * P:(k + 1) * P], score[:, k * P:(k + 1) * P], ident[:])
                    mm.then_inc(turned, 1)

            def weigh(g):
                pe.wait_ge(out_read, g + 1)
                for k in range(T):
                    if k % (T // 2) == 0:
                        pe.wait_ge(p_lo if k == 0 else p_lo_b, g + 1)
                    mm = three(ps_o[:, 0:DV], prob_hi[:, k, :], prob_lo[:, k, :], v_hi[:, k, :], v_lo[:, k, :], k, T - 1)
                mm.then_inc(out_full, 1)

            with pe.Fori(0, B) as b:
                pe.wait_ge(x_in_s, (b + 1) * 16)
                n = 0

                def bank():
                    pe.wait_ge(proj_lo, b * NP + n + 1)
                    return ps_p[n % 2]

                for i in range(XB):
                    ps = bank()
                    for c in range(DC):
                        for j in range(2):
                            mm = pe.transpose(ps[:, (2 * c + j) * P:(2 * c + j + 1) * P],
                                              x_tok[:, 2 * i + j, c * P:(c + 1) * P], ident[:])
                    mm.then_inc(proj_full, 1)
                    n += 1
                pe.wait_ge(proj_lo, b * NP + XB + 2)
                for i in range(KB):
                    ps = bank()
                    for c in range(DC):
                        s = slice(i * HALF, (i + 1) * HALF)
                        mm = three(ps[:], wk_hi[:, c, :], wk_lo[:, c, :], xT_hi[:, c, s], xT_lo[:, c, s], c, DC - 1)
                    mm.then_inc(proj_full, 1)
                    n += 1
                for i in range(VB):
                    ps = bank()
                    for j in range(2):
                        s = slice((2 * i + j) * P, (2 * i + j + 1) * P)
                        for c in range(DC):
                            mm = three(ps[:, j * D:(j + 1) * D], xT_hi[:, c, s], xT_lo[:, c, s],
                                       wv_hi[:, c, :], wv_lo[:, c, :], c, DC - 1)
                    mm.then_inc(proj_full, 1)
                    n += 1
                q_tile(0, b * T)
                pe.wait_ge(proj_lo, b * NP + NP + 2)
                scores(b * T)
                q_tile(1, b * T + 1)
                with pe.Fori(0, T - 2) as t:
                    g = b * T + t
                    turn(g)
                    scores(g + 1)
                    q_tile(t + 2, g + 2)
                    weigh(g)
                g = b * T + T - 2
                turn(g)
                scores(g + 1)
                weigh(g)
                turn(g + 1)
                weigh(g + 1)

        @block.vector
        def _(dve):
            dve.memset(v_hi[:, :, D:D + 1].bitcast(F32), 1.0).then_inc(dve0, 1)
            dve.memset(v_hi[:, :, D + 1:DV].bitcast(F32), 0.0).then_inc(dve0, 1)
            dve.memset(v_lo[:, :, D:DV].bitcast(F32), 0.0).then_inc(dve0, 1)
            dve.sem_inc(proj_lo, 2)
            dve.sem_inc(q_lo, 1)
            dve.sem_inc(out_read, 1)
            dve.sem_inc(bias_used, 1)
            dve.wait_ge(w_in, 16 * 7)
            k = 0
            if folded:
                srcs = []
                for j in range(2):
                    dve.wait_ge(w_ps, j + 1)
                    dve.tensor_scalar(w_fold[:, j, :, :], ps_p[j][:].rearrange("p (c n) -> p c n", c=DC),
                                      score_scale if j == 0 else 1.0, None, ALU.mult).then_inc(step, 1)
                    k += 1
                dve.wait_ge(step, k)
                pairs = [(w_fold[:, 0, :, :], wq_hi, wq_lo), (w_fold[:, 1, :, :], wv_hi, wv_lo)]
            else:
                r = [raw[i][:, 0:DC * n].rearrange("p (c n) -> p c n", c=DC) for i, n in ((0, P), (1, P), (2, D))]
                dve.tensor_scalar(r[0], r[0], score_scale, None, ALU.mult).then_inc(step, 1)
                dve.tensor_scalar(bqk[:, 0:1], bqk[:, 0:1], score_scale, None, ALU.mult).then_inc(step, 1)
                k += 2
                dve.wait_ge(step, k)
                pairs = [(r[0], wq_hi, wq_lo), (r[1], wk_hi, wk_lo), (r[2], wv_hi, wv_lo)]
            for full, hi, lo in pairs:
                dve.tensor_copy(hi[:], full).then_inc(step, 1)
                k += 1
                dve.wait_ge(step, k)
                mm = dve.tensor_tensor(lo[:], full, hi[:].bitcast(F32), ALU.subtract)
            dve.wait_ge(dve0, 3)
            mm.then_inc(w_part, 1)
            dve.wait_ge(w_part, 1)

            def split_lo(dst, ps, hi, at, bias=None):
                dve.wait_ge(proj_hi, at)
                if bias is None:
                    dve.tensor_tensor(dst, ps, hi.bitcast(F32), ALU.subtract).then_inc(proj_lo, 1)
                else:
                    dve.scalar_tensor_tensor(dst, ps, bias, hi.bitcast(F32), ALU.add, ALU.subtract).then_inc(proj_lo, 1)

            def q_low(g):
                dve.wait_ge(q_hi, g + 1)
                src = ps_q[:, 0:QC * P].rearrange("p (c n) -> p c n", c=QC)
                if folded:
                    dve.tensor_tensor(qT_lo[:], src, qT_hi[:].bitcast(F32), ALU.subtract).then_inc(q_lo, 1)
                else:
                    dve.scalar_tensor_tensor(qT_lo[:, 0, :], ps_q[:, 0:P], bqk[:, 0:1], qT_hi[:, 0, :].bitcast(F32),
                                             ALU.add, ALU.subtract).then_inc(q_lo, 1)

            def make_bias(t, g):
                dve.tensor_scalar(mask_bias[:], adj_sb[:, t, :], 0.0, -BIG, ALU.is_equal, ALU.mult).then_inc(bias_made, 1)

            def shift(g):
                dve.wait_ge(bias_made, g + 1)
                dve.wait_ge(score_full, g + 1)
                dve.sem_inc(passed, 1)
                dve.tensor_tensor_reduce(score[:], ps_s[:], mask_bias[:], 1.0, -3.0e38, ALU.add, ALU.max,
                                         row_max[:]).then_inc(bias_used, 1)
                dve.wait_ge(bias_used, g + 2)
                dve.tensor_scalar(score[:], score[:], row_max[:], None, ALU.subtract).then_inc(shifted, 1)

            def flag(g):
                dve.tensor_scalar(has_key[:], row_max[:], -0.1 * BIG, None, ALU.is_gt).then_inc(has_key_s, 1)

            def p_low(g):
                half = slice(0, T // 2)
                dve.wait_ge(p_hi, 2 * g + 1)
                dve.tensor_tensor(prob_lo[:, half, :], prob[:, half, :], prob_hi[:, half, :].bitcast(F32),
                                  ALU.subtract).then_inc(p_lo, 1)

            def finish(t, g):
                dve.wait_ge(out_full, g + 1)
                dve.reciprocal(inv[:, 0:1], ps_o[:, D:D + 1]).then_inc(inv_s, 1)
                if folded:
                    dve.wait_ge(inv_s, g + 1)
                    iv = inv[:, 0:1]
                else:
                    dve.wait_ge(inv_s, 2 * g + 1)
                    dve.wait_ge(has_key_s, g + 1)
                    dve.tensor_tensor(inv[:, 1:2], inv[:, 0:1], has_key[:], ALU.mult).then_inc(inv_s, 1)
                    dve.wait_ge(inv_s, 2 * g + 2)
                    iv = inv[:, 1:2]
                dve.wait_ge(normed, g + 1)
                dve.scalar_tensor_tensor(y[:], ps_o[:, 0:D], iv, x_res[:, t, :], ALU.mult, ALU.add).then_inc(out_read, 1)
                dve.wait_ge(out_read, g + 2)
                dve.bn_stats(stats[:], y[:]).then_inc(stats_part, 1)
                dve.wait_ge(stats_part, g + 1)
                dve.sem_inc(passed, 1)
                dve.bn_aggr(mean_var[:], stats[:]).then_inc(stats_done, 1)

            with dve.Fori(0, B) as b:
                n = 0
                for i in range(XB):
                    s = slice(2 * i * P, (2 * i + 2) * P)
                    split_lo(xT_lo[:, :, s], ps_p[n % 2][:].rearrange("p (c n) -> p c n", c=DC), xT_hi[:, :, s],
                             b * NP + n + 1)
                    n += 1
                for i in range(KB):
                    s = slice(i * HALF, (i + 1) * HALF)
                    split_lo(kT_lo[:, 0, s], ps_p[n % 2][:], kT_hi[:, 0, s], b * NP + n + 1, bias=bqk[:, 1:2])
                    n += 1
                for i in range(VB):
                    s = slice(2 * i, 2 * i + 2)
                    split_lo(v_lo[:, s, 0:D], ps_p[n % 2][:].rearrange("p (t n) -> p t n", n=D), v_hi[:, s, 0:D],
                             b * NP + n + 1)
                    n += 1
                q_low(b * T)
                dve.wait_ge(adj_in, (b + 1) * 16 * T)
                make_bias(0, b * T)
                shift(b * T)
                q_low(b * T + 1)
                dve.wait_ge(res_in, (b + 1) * 16)
                if folded:
                    dve.tensor_tensor(x_res[:], x_res[:], bo_row[:].unsqueeze(1).to_broadcast([P, T, D]), ALU.add).then_inc(res_s, 1)
                    dve.wait_ge(res_s, b + 1)
                dve.sem_inc(passed, 1)
                def body(t, g, last):
                    if not folded:
                        flag(g)
                    p_low(g)
                    if last < 1:
                        make_bias(t + 1, g + 1)
                        shift(g + 1)
                    if last < 0:
                        q_low(g + 2)
                    finish(t, g)
                with dve.Fori(0, T - 2) as t:
                    body(t, b * T + t, -1)
                body(T - 2, b * T + T - 2, 0)
                body(T - 1, b * T + T - 1, 1)
    return nc


TINY = 1.0e-13


def direction_layer(nc, tag, x_in, x_out, adjT, w, bias, gamma, beta, B, N):
    T = N // P
    XB, YB = T // 2, T
    NP = XB + YB
    HALF = 512
    W2 = 2 * D

    with nc.cleanup_on_exit(), ExitStack() as ctx:
        def sb(name, shape, dt=F32):
            return ctx.enter_context(nc.sbuf_tensor(f"{tag}_{name}", shape, dt))

        def pb(name, shape):
            return ctx.enter_context(nc.psum_tensor(f"{tag}_{name}", shape, F32))

        def sem(name):
            return nc.alloc_semaphore(name=f"{tag}_{name}")

        w_raw = sb("w_raw", [P, DC, W2])
        w_hi, w_lo = sb("w_hi", [P, DC, W2], F32R), sb("w_lo", [P, DC, W2], F32R)
        bias_row, gamma_row, beta_row = sb("bias_row", [P, D]), sb("gamma_row", [P, D]), sb("beta_row", [P, D])
        ident, small = sb("ident", [P, P]), sb("small", [P, 3])
        small2 = sb("small2", [P, 2])
        x_tok, x_res, x_new = sb("x_tok", [P, T, D]), sb("x_res", [P, T, D]), sb("x_new", [P, T, D])
        xT_hi, xT_lo = sb("xT_hi", [P, DC, N], F32R), sb("xT_lo", [P, DC, N], F32R)
        y_hi, y_lo = sb("y_hi", [P, T, 2, DV], F32R), sb("y_lo", [P, T, 2, DV], F32R)
        adj_sb = [sb(f"adj_sb{j}", [P, T, P], I32) for j in range(2)]
        off = [sb(f"off{j}", [P, T, P]) for j in range(2)]
        kind1 = [sb(f"kind1_{j}", [P, T, P], F32R) for j in range(2)]
        kind2 = [sb(f"kind2_{j}", [P, T, P], F32R) for j in range(2)]
        cnt, inv = sb("cnt", [P, 2, 1]), sb("inv", [P, 2, 1])
        mean1, mean12, y = sb("mean1", [P, D]), sb("mean12", [P, D]), sb("y", [P, D])
        stats, mean_var, ln_c = sb("stats", [P, 6]), sb("mean_var", [P, 2]), sb("ln_c", [P, 4])

        ps_p = [pb(f"ps_p{i}", [P, HALF]) for i in range(2)]
        ps_o = [pb(f"ps_o{i}", [P, 2, HALF]) for i in range(2)]

        w_in, w_part, w_split, ready, ones_in = sem("w_in"), sem("w_part"), sem("w_split"), sem("ready"), sem("ones_in")
        x_in_s, res_in, stored = sem("x_in"), sem("res_in"), sem("stored")
        adj_in = [sem(f"adj_in{j}") for j in range(2)]
        proj_full, proj_hi, proj_lo = sem("proj_full"), sem("proj_hi"), sem("proj_lo")
        kind1_made, kind2_part, kind2_made = sem("kind1_made"), sem("kind2_part"), sem("kind2_made")
        out_full, out_read = sem("out_full"), sem("out_read")
        fin_part, stats_done = sem("fin_part"), sem("stats_done")
        rstd_part, rstd_done, normed, new_part, new_done = (sem("rstd_part"), sem("rstd_done"), sem("normed"),
                                                            sem("new_part"), sem("new_done"))
        passed, small2_in = sem("passed"), sem("small2_in")

        x_in_t = x_in.rearrange("b (t p) d -> b p t d", p=P)
        x_out_t = x_out.rearrange("b (t p) d -> b p t d", p=P)
        block = ctx.enter_context(nc.Block())
        H = T // 2

        @block.sync
        def _(sp):
            sp.dma_start(w_raw[:, :, 0:D], w[0:D, :].rearrange("(c p) n -> p c n", p=P)).then_inc(w_in, 16)
            sp.dma_start(w_raw[:, :, D:W2], w[D:W2, :].rearrange("(c p) n -> p c n", p=P)).then_inc(w_in, 16)
            for dst, src in ((bias_row, bias), (gamma_row, gamma), (beta_row, beta)):
                sp.dma_start(dst[:], src.partition_broadcast(P)).then_inc(w_in, 16)

            def load_tokens(b):
                sp.dma_start(x_tok[:], x_in_t[b]).then_inc(x_in_s, 16)

            def load_residual(b):
                sp.dma_start(x_res[:], x_in_t[b]).then_inc(res_in, 16)

            def load_adj(b, t, j):
                sp.dma_start(adj_sb[j][:], adjT[b, t]).then_inc(adj_in[j], 16)

            def store_last(b):
                t = T - 1
                sp.wait_ge(new_done, b * T + t + 1)
                sp.dma_start(x_out_t[b][:, t, :], x_new[:, t, :]).then_inc(stored, 16)

            load_tokens(0)
            load_adj(0, 0, 0)
            load_adj(0, 1, 1)
            load_residual(0)
            sp.sem_inc(stored, 16 * T)

            with sp.Fori(0, B - 1) as b:
                sp.wait_ge(proj_full, b * NP + XB)
                load_tokens(b + 1)
                with sp.Fori(0, H - 1) as i:
                    for j in range(2):
                        sp.wait_ge(kind1_made, b * T + 2 * i + j + 1)
                        sp.wait_ge(kind2_made, b * T + 2 * i + j + 1)
                        load_adj(b, 2 * i + 2 + j, j)
                for j in range(2):
                    sp.wait_ge(kind1_made, b * T + T - 1 + j)
                    sp.wait_ge(kind2_made, b * T + T - 1 + j)
                    load_adj(b + 1, j, j)
                sp.wait_ge(out_read, (b + 1) * T + 2)
                load_residual(b + 1)
                store_last(b)
            b = B - 1
            with sp.Fori(0, H - 1) as i:
                for j in range(2):
                    sp.wait_ge(kind1_made, b * T + 2 * i + j + 1)
                    sp.wait_ge(kind2_made, b * T + 2 * i + j + 1)
                    load_adj(b, 2 * i + 2 + j, j)
            store_last(b)
            sp.wait_ge(stored, 16 * T * (B + 1))

        @block.gpsimd
        def _(pool):
            pool.memset(ident[:], 0.0).then_inc(ready, 1)
            pool.memset(small[:, 0:1], -0.5).then_inc(ready, 1)
            pool.memset(small[:, 1:2], -1.0).then_inc(ready, 1)
            pool.memset(small[:, 2:3], EPS).then_inc(ready, 1)
            pool.wait_ge(ready, 4)
            pool.affine_select(out=ident[:], in_=ident[:], compare_op=ALU.not_equal, fill=1.0,
                               base=0, pattern=[[-1, P]], channel_multiplier=1).then_inc(ready, 1)
            pool.wait_ge(w_in, 16 * 5)

            def norm_consts(g):
                pool.wait_ge(stats_done, g + 1)
                pool.tensor_tensor(ln_c[:, 0:1], mean_var[:, 1:2], small[:, 2:3], ALU.add).then_inc(rstd_part, 1)
                pool.wait_ge(rstd_part, 3 * g + 1)
                pool.tensor_tensor(ln_c[:, 1:2], ln_c[:, 0:1], small[:, 0:1], ALU.pow).then_inc(rstd_part, 1)
                pool.wait_ge(rstd_part, 3 * g + 2)
                pool.tensor_tensor(ln_c[:, 3:4], mean_var[:, 0:1], ln_c[:, 1:2], ALU.mult).then_inc(rstd_part, 1)
                pool.wait_ge(rstd_part, 3 * g + 3)
                pool.tensor_tensor(ln_c[:, 2:3], ln_c[:, 3:4], small[:, 1:2], ALU.mult).then_inc(rstd_done, 1)

            def affine(t, g):
                pool.wait_ge(normed, g + 2)
                pool.sem_inc(passed, 1)
                pool.tensor_tensor(x_new[:, t, :], x_new[:, t, :], gamma_row[:], ALU.mult).then_inc(new_part, 1)
                pool.wait_ge(new_part, g + 1)
                pool.sem_inc(passed, 1)
                pool.tensor_tensor(x_new[:, t, :], x_new[:, t, :], beta_row[:], ALU.add).then_inc(new_done, 1)

            with pool.Fori(0, B) as b:
                with pool.Fori(0, T) as t:
                    g = b * T + t
                    norm_consts(g)
                    affine(t, g)

        @block.scalar
        def _(act):
            def split_hi(dst, ps, at):
                act.wait_ge(proj_full, at)
                act.activation(dst, ps, ACT.Identity).then_inc(proj_hi, 1)

            def make_kind2(g, j, seen):
                act.wait_ge(adj_in[j], 16 * seen)
                act.activation(off[j][:], adj_sb[j][:], ACT.Abs, bias=small2[:, 0:1]).then_inc(kind2_part, 1)
                act.wait_ge(kind2_part, g + 1)
                act.wait_ge(out_full, g + 1)
                act.activation(kind2[j][:], off[j][:], ACT.Relu, bias=small2[:, 1:2], scale=-1.0).then_inc(kind2_made, 1)

            def normalise(t, g):
                act.wait_ge(rstd_done, g + 1)
                act.activation(x_new[:, t, :], y[:], ACT.Identity, bias=ln_c[:, 2:3], scale=ln_c[:, 1:2]).then_inc(normed, 1)

            def store(b, t, g):
                act.wait_ge(new_done, g + 1)
                act.dma_start(x_out_t[b][:, t, :], x_new[:, t, :]).then_inc(stored, 16)

            act.sem_inc(normed, 1)
            act.wait_ge(small2_in, 2)
            with act.Fori(0, B) as b:
                n = 0
                for i in range(XB):
                    split_hi(xT_hi[:, :, 2 * i * P:(2 * i + 2) * P], ps_p[n % 2][:].rearrange("p (c n) -> p c n", c=DC),
                             b * NP + n + 1)
                    n += 1
                for t in range(YB):
                    split_hi(y_hi[:, t, :, 0:D], ps_p[n % 2][:].rearrange("p (j n) -> p j n", j=2), b * NP + n + 1)
                    n += 1
                make_kind2(b * T, 0, b * H + 1)
                make_kind2(b * T + 1, 1, b * H + 1)
                act.wait_ge(stored, 16 * T * (b + 1))
                act.sem_inc(passed, 1)
                g = b * T
                make_kind2(g + 2, 0, b * H + 2)
                normalise(0, g)
                make_kind2(g + 3, 1, b * H + 2)
                normalise(1, g + 1)
                store(b, 0, g)
                with act.Fori(1, H - 1) as i:
                    for j in range(2):
                        g = b * T + 2 * i + j
                        make_kind2(g + 2, j, b * H + i + 2)
                        normalise(2 * i + j, g)
                        store(b, 2 * i + j - 1, g - 1)
                for t in (T - 2, T - 1):
                    normalise(t, b * T + t)
                    store(b, t - 1, b * T + t - 1)

        @block.tensor
        def _(pe):
            pe.wait_ge(ready, 5)
            pe.wait_ge(w_split, 1)
            pe.wait_ge(ones_in, 3)
            pe.sem_inc(out_full, 2)

            def three(out, l_hi, l_lo, r_hi, r_lo, n, last):
                pe.matmul(out, l_hi, r_hi, start=(n == 0), stop=False)
                pe.matmul(out, l_hi, r_lo, start=False, stop=False)
                return pe.matmul(out, l_lo, r_hi, start=False, stop=(n == last))

            def aggregate(g, j):
                pe.wait_ge(kind1_made, g + 1)
                pe.wait_ge(out_read, g + 1)
                for d, kind in ((0, kind1), (1, kind2)):
                    if d == 1:
                        pe.wait_ge(kind2_made, g + 1)
                    for k in range(T):
                        pe.matmul(ps_o[j][:, d, 0:DV], kind[j][:, k, :], y_hi[:, k, d, :], start=(k == 0), stop=False)
                        mm = pe.matmul(ps_o[j][:, d, 0:DV], kind[j][:, k, :], y_lo[:, k, d, :], start=False,
                                       stop=(k == T - 1))
                mm.then_inc(out_full, 1)

            with pe.Fori(0, B) as b:
                pe.wait_ge(x_in_s, (b + 1) * 16)
                n = 0
                for i in range(XB):
                    pe.wait_ge(proj_lo, b * NP + n + 1)
                    for c in range(DC):
                        for j in range(2):
                            mm = pe.transpose(ps_p[n % 2][:, (2 * c + j) * P:(2 * c + j + 1) * P],
                                              x_tok[:, 2 * i + j, c * P:(c + 1) * P], ident[:])
                    mm.then_inc(proj_full, 1)
                    n += 1
                for t in range(YB):
                    pe.wait_ge(proj_lo, b * NP + max(n + 1, 2 + XB))
                    for c in range(DC):
                        s = slice(t * P, (t + 1) * P)
                        mm = three(ps_p[n % 2][:], xT_hi[:, c, s], xT_lo[:, c, s], w_hi[:, c, :], w_lo[:, c, :], c, DC - 1)
                    mm.then_inc(proj_full, 1)
                    n += 1
                pe.wait_ge(proj_lo, (b + 1) * NP + 2)
                pe.sem_inc(passed, 1)
                with pe.Fori(0, H) as i:
                    for j in range(2):
                        aggregate(b * T + 2 * i + j, j)

        @block.vector
        def _(dve):
            dve.memset(small2[:, 0:1], -2.0).then_inc(small2_in, 1)
            dve.memset(small2[:, 1:2], 1.0).then_inc(small2_in, 1)
            dve.memset(y_hi[:, :, :, D:D + 1].bitcast(F32), 1.0).then_inc(ones_in, 1)
            dve.memset(y_hi[:, :, :, D + 1:DV].bitcast(F32), 0.0).then_inc(ones_in, 1)
            dve.memset(y_lo[:, :, :, D:DV].bitcast(F32), 0.0).then_inc(ones_in, 1)
            dve.sem_inc(proj_lo, 2)
            dve.sem_inc(out_read, 2)
            dve.wait_ge(w_in, 16 * 5)
            dve.tensor_copy(w_hi[:], w_raw[:]).then_inc(w_part, 1)
            dve.wait_ge(w_part, 1)
            dve.tensor_tensor(w_lo[:], w_raw[:], w_hi[:].bitcast(F32), ALU.subtract).then_inc(w_split, 1)

            def split_lo(dst, ps, hi, at):
                dve.wait_ge(proj_hi, at)
                dve.tensor_tensor(dst, ps, hi.bitcast(F32), ALU.subtract).then_inc(proj_lo, 1)

            def make_kind1(g, j, seen):
                dve.wait_ge(adj_in[j], 16 * seen)
                dve.wait_ge(out_full, g + 1)
                dve.tensor_scalar(kind1[j][:], adj_sb[j][:], 1.0, None, ALU.is_equal).then_inc(kind1_made, 1)

            def finish(t, g, j):
                dve.wait_ge(out_full, g + 3)
                dve.tensor_scalar(cnt[:], ps_o[j][:, :, D:D + 1], TINY, None, ALU.add).then_inc(fin_part, 1)
                dve.wait_ge(fin_part, 5 * g + 1)
                dve.reciprocal(inv[:], cnt[:]).then_inc(fin_part, 1)
                dve.wait_ge(fin_part, 5 * g + 2)
                dve.scalar_tensor_tensor(mean1[:], ps_o[j][:, 0, 0:D], inv[:, 0, :], bias_row[:], ALU.mult, ALU.add)\
                   .then_inc(fin_part, 1)
                dve.wait_ge(fin_part, 5 * g + 3)
                dve.scalar_tensor_tensor(mean12[:], ps_o[j][:, 1, 0:D], inv[:, 1, :], mean1[:], ALU.mult, ALU.add)\
                   .then_inc(fin_part, 1)
                dve.wait_ge(fin_part, 5 * g + 4)
                dve.wait_ge(normed, g + 1)
                dve.scalar_tensor_tensor(y[:], mean12[:], 0.0, x_res[:, t, :], ALU.max, ALU.add).then_inc(out_read, 1)
                dve.wait_ge(out_read, g + 3)
                dve.bn_stats(stats[:], y[:]).then_inc(fin_part, 1)
                dve.wait_ge(fin_part, 5 * g + 5)
                dve.sem_inc(passed, 1)
                dve.bn_aggr(mean_var[:], stats[:]).then_inc(stats_done, 1)

            with dve.Fori(0, B) as b:
                n = 0
                for i in range(XB):
                    s = slice(2 * i * P, (2 * i + 2) * P)
                    split_lo(xT_lo[:, :, s], ps_p[n % 2][:].rearrange("p (c n) -> p c n", c=DC), xT_hi[:, :, s],
                             b * NP + n + 1)
                    n += 1
                for t in range(YB):
                    split_lo(y_lo[:, t, :, 0:D], ps_p[n % 2][:].rearrange("p (j n) -> p j n", j=2), y_hi[:, t, :, 0:D],
                             b * NP + n + 1)
                    n += 1
                make_kind1(b * T, 0, b * H + 1)
                make_kind1(b * T + 1, 1, b * H + 1)
                dve.wait_ge(res_in, (b + 1) * 16)
                dve.sem_inc(passed, 1)
                with dve.Fori(0, H - 1) as i:
                    for j in range(2):
                        g = b * T + 2 * i + j
                        make_kind1(g + 2, j, b * H + i + 2)
                        finish(2 * i + j, g, j)
                for t in (T - 2, T - 1):
                    finish(t, b * T + t, t % 2)


H = 8
HD = D // H
HV = HD + 1


def heads_project(nc, tag, x_in, q_parts, k_parts, v_out, g1, b1, wq, bq, wk, bk, wv, bv, B, N):
    T = N // P
    HALF = 512
    RING = 8
    X, KQ, V = T // 2, DC * N // HALF, T // 2
    NF = X + 2 * KQ + V
    NH = X + 2 * KQ
    SCALE = float(HD) ** -0.5

    with nc.cleanup_on_exit(), ExitStack() as ctx:
        def sb(name, shape, dt=F32):
            return ctx.enter_context(nc.sbuf_tensor(f"{tag}_{name}", shape, dt))

        def sem(name):
            return nc.alloc_semaphore(name=f"{tag}_{name}")

        w_raw = [sb(f"w_raw{i}", [P, DC, D]) for i in range(3)]
        w_hi = [sb(f"w_hi{i}", [P, DC, D], F32R) for i in range(3)]
        w_lo = [sb(f"w_lo{i}", [P, DC, D], F32R) for i in range(3)]
        col = sb("col", [P, 4, DC])
        bcol = sb("bcol", [P, 2, DC])
        b1_wide = sb("b1_wide", [P, DC, P])
        bv_row = sb("bv_row", [P, D])
        ident, small = sb("ident", [P, P]), sb("small", [P, 3])
        x_tok = [sb(f"x_tok{j}", [P, T, D]) for j in range(2)]
        zT_hi = [sb(f"zT_hi{j}", [P, DC, N], F32R) for j in range(2)]
        zT_lo = [sb(f"zT_lo{j}", [P, DC, N], F32R) for j in range(2)]
        kT = [[sb(f"kT_{part}{j}", [P, DC, N], F32R) for part in ("hi", "lo")] for j in range(2)]
        qT = [[sb(f"qT_{part}{j}", [P, DC, N], F32R) for part in ("hi", "lo")] for j in range(2)]
        v = [sb(f"v{j}", [P, T, H, HV]) for j in range(2)]
        stats, mean_var, ln_c = sb("stats", [P, T, 6]), sb("mean_var", [P, T, 2]), sb("ln_c", [P, 4, T])
        ring = [ctx.enter_context(nc.psum_tensor(f"{tag}_ring{i}", [P, HALF], F32)) for i in range(RING)]

        names = ("w_in ready w_part b_ps w_split full high low stat_part stats_done rstd_part rstd_done z_done passed")
        (w_in, ready, w_part, b_ps, w_split, full, high, low, stat_part, stats_done, rstd_part, rstd_done, z_done,
         passed) = (sem(n) for n in names.split())
        x_loaded = [sem(f"x_loaded{j}") for j in range(2)]
        stored = [sem(f"stored{j}") for j in range(2)]

        x_in_t = x_in.rearrange("b (t p) d -> b p t d", p=P)
        q_t = q_parts.rearrange("(b t) s (c p) n -> b s c p t n", t=T, p=P)
        k_t = k_parts.rearrange("b s (c p) n -> b s p c n", p=P)
        NW = 3 + 4 + 1
        NS = 2 * DC + 2 + 1
        block = ctx.enter_context(nc.Block())

        def fill(b, n, has_x):
            return X + NF * b + n - (0 if has_x else X)

        def bank(n, has_x):
            return ring[(X + n - (0 if has_x else X)) % RING]

        def split(b, n, has_x):
            return X + NH * b + n - (0 if has_x else X)

        @block.sync
        def _(sp):
            for i, w in enumerate((wq, wk, wv)):
                sp.dma_start(w_raw[i][:], w.rearrange("(c p) n -> p c n", p=P)).then_inc(w_in, 16)
            for i, c in enumerate((g1, b1, bq, bk)):
                sp.dma_start(col[:, i, :].unsqueeze(2), c.rearrange("(c p o) -> p c o", p=P, o=1),
                             allow_slow_non_contiguous=True).then_inc(w_in, 16)
            sp.dma_start(bv_row[:], bv.partition_broadcast(P)).then_inc(w_in, 16)
            for j in range(2):
                sp.dma_start(x_tok[j][:], x_in_t[j]).then_inc(x_loaded[j], 16)
                sp.sem_inc(stored[j], 16 * NS)

            def batch(b, j, has_x, has_load):
                if has_load:
                    sp.wait_ge(full, NF * b + X)
                    sp.dma_start(x_tok[j][:], x_in_t[b + 2]).then_inc(x_loaded[j], 16)
                sp.wait_ge(low, fill(b, X + KQ - 1, has_x) + 1 + RING)
                for s in range(2):
                    sp.dma_start(k_t[b, s], kT[j][s][:].bitcast(F32)).then_inc(stored[j], 16)
                sp.wait_ge(low, fill(b, X + 2 * KQ - 1, has_x) + 1 + RING)
                for s in range(2):
                    for c in range(DC):
                        sp.dma_start(q_t[b, s, c], qT[j][s][:, c, :].rearrange("p (t n) -> p t n", n=P).bitcast(F32))\
                          .then_inc(stored[j], 16)
                sp.wait_ge(low, fill(b, NF - 1, has_x) + 1 + RING)
                sp.dma_start(v_out[b], v[j][:].rearrange("p t h d -> p (t h d)")).then_inc(stored[j], 16)

            with sp.Fori(0, (B - 2) // 2) as i:
                for j in range(2):
                    batch(2 * i + j, j, True, True)
            batch(B - 2, 0, True, False)
            batch(B - 1, 1, False, False)
            for j in range(2):
                sp.wait_ge(stored[j], 16 * NS * (B // 2 + 1))

        @block.gpsimd
        def _(pool):
            pool.memset(ident[:], 0.0).then_inc(ready, 1)
            pool.memset(small[:, 0:1], -0.5).then_inc(ready, 1)
            pool.memset(small[:, 1:2], -1.0).then_inc(ready, 1)
            pool.memset(small[:, 2:3], EPS).then_inc(ready, 1)
            pool.wait_ge(ready, 4)
            pool.affine_select(out=ident[:], in_=ident[:], compare_op=ALU.not_equal, fill=1.0,
                               base=0, pattern=[[-1, P]], channel_multiplier=1).then_inc(ready, 1)
            half, minus, eps = (small[:, k:k + 1].to_broadcast([P, T]) for k in range(3))

            def norm_consts(b):
                pool.wait_ge(stats_done, (b + 1) * T)
                pool.tensor_tensor(ln_c[:, 0, :], mean_var[:, :, 1], eps, ALU.add).then_inc(rstd_part, 1)
                pool.wait_ge(rstd_part, 3 * b + 1)
                pool.tensor_tensor(ln_c[:, 1, :], ln_c[:, 0, :], half, ALU.pow).then_inc(rstd_part, 1)
                pool.wait_ge(rstd_part, 3 * b + 2)
                pool.tensor_tensor(ln_c[:, 3, :], mean_var[:, :, 0], ln_c[:, 1, :], ALU.mult).then_inc(rstd_part, 1)
                pool.wait_ge(rstd_part, 3 * b + 3)
                pool.tensor_tensor(ln_c[:, 2, :], ln_c[:, 3, :], minus, ALU.mult).then_inc(rstd_done, 1)

            with pool.Fori(0, B) as b:
                norm_consts(b)

        @block.scalar
        def _(act):
            def normalise(b, j):
                act.wait_ge(rstd_done, b + 1)
                act.sem_inc(passed, 1)
                for t in range(T):
                    act.activation(x_tok[j][:, t, :], x_tok[j][:, t, :], ACT.Identity, bias=ln_c[:, 2, t:t + 1],
                                   scale=ln_c[:, 1, t:t + 1]).then_inc(z_done, 1)

            def high_x(dst, ps, i, at):
                act.wait_ge(full, at + 1)
                act.activation(dst[:, :, 2 * i * P:(2 * i + 2) * P], ps[:].rearrange("p (c n) -> p c n", c=DC),
                               ACT.Identity).then_inc(high, 1)

            def batch(b, j, has_x, has_load, seen):
                if has_x:
                    for n in range(X):
                        high_x(zT_hi[1 - j], bank(n, True), n, fill(b, n, True))
                act.wait_ge(stored[j], 16 * NS * seen)
                for which, dst in ((1, kT[j][0]), (0, qT[j][0])):
                    for k in range(KQ):
                        n = X + (1 - which) * KQ + k
                        m, s = k // 2, slice(k % 2 * HALF, (k % 2 + 1) * HALF)
                        act.wait_ge(full, fill(b, n, has_x) + 1)
                        act.activation(dst[:, m, s], bank(n, has_x)[:], ACT.Identity, bias=bcol[:, which, m:m + 1])\
                           .then_inc(high, 1)
                    if which == 1 and has_load:
                        normalise(b + 2, j)

            act.wait_ge(w_split, 1)
            normalise(0, 0)
            for n in range(X):
                high_x(zT_hi[0], ring[n], n, n)
            normalise(1, 1)
            with act.Fori(0, (B - 2) // 2) as i:
                for j in range(2):
                    batch(2 * i + j, j, True, True, i + 1)
            batch(B - 2, 0, True, False, B // 2)
            batch(B - 1, 1, False, False, B // 2)

        @block.tensor
        def _(pe):
            def three(out, l_hi, l_lo, r_hi, r_lo, n, last):
                pe.matmul(out, l_hi, r_hi, start=(n == 0), stop=False)
                pe.matmul(out, l_hi, r_lo, start=False, stop=False)
                return pe.matmul(out, l_lo, r_hi, start=False, stop=(n == last))

            pe.wait_ge(w_in, 16 * NW)
            for i in range(2):
                for m in range(DC):
                    for c in range(DC):
                        mm = pe.matmul(ring[0][:, i * DC + m:i * DC + m + 1], w_raw[i][:, c, m * P:(m + 1) * P],
                                       col[:, 1, c:c + 1], start=(c == 0), stop=(c == DC - 1))
            mm.then_inc(b_ps, 1)
            pe.wait_ge(w_part, 1)
            for c in range(DC):
                mm = pe.matmul(ring[1][:, 0:D], b1_wide[:, c, :], w_raw[2][:, c, :], start=(c == 0), stop=(c == DC - 1))
            mm.then_inc(b_ps, 1)
            pe.wait_ge(ready, 5)
            pe.wait_ge(w_split, 1)

            def turn(b, j, at):
                for n in range(X):
                    k, ps = at(n)
                    pe.wait_ge(low, k + 1)
                    pe.wait_ge(z_done, b * T + 2 * n + 2)
                    for c in range(DC):
                        for r in range(2):
                            mm = pe.transpose(ps[:, (2 * c + r) * P:(2 * c + r + 1) * P],
                                              x_tok[j][:, 2 * n + r, c * P:(c + 1) * P], ident[:])
                    mm.then_inc(full, 1)

            def batch(b, j, has_x):
                if has_x:
                    turn(b + 1, 1 - j, lambda n: (fill(b, n, True), bank(n, True)))
                pe.wait_ge(low, NF * b + X + RING)
                for which in (1, 0):
                    for k in range(KQ):
                        n = X + (1 - which) * KQ + k
                        ws, ts = slice(k // 2 * P, (k // 2 + 1) * P), slice(k % 2 * HALF, (k % 2 + 1) * HALF)
                        pe.wait_ge(low, fill(b, n, has_x) + 1)
                        for c in range(DC):
                            mm = three(bank(n, has_x)[:], w_hi[which][:, c, ws], w_lo[which][:, c, ws],
                                       zT_hi[j][:, c, ts], zT_lo[j][:, c, ts], c, DC - 1)
                        mm.then_inc(full, 1)
                for k in range(V):
                    n = X + 2 * KQ + k
                    pe.wait_ge(low, fill(b, n, has_x) + 1)
                    for r in range(2):
                        ts = slice((2 * k + r) * P, (2 * k + r + 1) * P)
                        for c in range(DC):
                            mm = three(bank(n, has_x)[:, r * D:(r + 1) * D], zT_hi[j][:, c, ts], zT_lo[j][:, c, ts],
                                       w_hi[2][:, c, :], w_lo[2][:, c, :], c, DC - 1)
                    mm.then_inc(full, 1)

            turn(0, 0, lambda n: (n, ring[n]))
            with pe.Fori(0, (B - 2) // 2) as i:
                for j in range(2):
                    batch(2 * i + j, j, True)
            batch(B - 2, 0, True)
            batch(B - 1, 1, False)

        @block.vector
        def _(dve):
            done = 0

            def stepped(ins):
                nonlocal done
                ins.then_inc(w_part, 1)
                done += 1
                dve.wait_ge(w_part, done)

            dve.wait_ge(w_in, 16 * NW)
            stepped(dve.tensor_copy(b1_wide[:], col[:, 1, :].unsqueeze(2).to_broadcast([P, DC, P])))
            for j in range(2):
                stepped(dve.memset(v[j][:, :, :, HD:HV], 1.0))
            dve.wait_ge(b_ps, 2)
            stepped(dve.tensor_tensor(bcol[:], ring[0][:, 0:2 * DC].rearrange("p (i c) -> p i c", i=2), col[:, 2:4, :], ALU.add))
            stepped(dve.tensor_scalar(bcol[:, 0, :], bcol[:, 0, :], SCALE, None, ALU.mult))
            stepped(dve.tensor_tensor(bv_row[:], ring[1][:, 0:D], bv_row[:], ALU.add))
            for i in range(3):
                for c in range(DC):
                    stepped(dve.tensor_scalar(w_raw[i][:, c, :], w_raw[i][:, c, :], col[:, 0, c:c + 1],
                                              SCALE if i == 0 else 1.0, ALU.mult, ALU.mult))
                stepped(dve.tensor_copy(w_hi[i][:], w_raw[i][:]))
                stepped(dve.tensor_tensor(w_lo[i][:], w_raw[i][:], w_hi[i][:].bitcast(F32), ALU.subtract))
            dve.sem_inc(w_split, 1)
            dve.sem_inc(low, RING)

            def statistics(b, j, seen):
                dve.wait_ge(x_loaded[j], 16 * seen)
                dve.sem_inc(passed, 1)
                for t in range(T):
                    dve.bn_stats(stats[:, t, :], x_tok[j][:, t, :]).then_inc(stat_part, 1)
                dve.wait_ge(stat_part, (b + 1) * T)
                dve.sem_inc(passed, 1)
                for t in range(T):
                    dve.bn_aggr(mean_var[:, t, :], stats[:, t, :]).then_inc(stats_done, 1)

            def low_x(j, ps, i, at):
                ts = slice(2 * i * P, (2 * i + 2) * P)
                dve.wait_ge(high, at + 1)
                dve.tensor_tensor(zT_lo[j][:, :, ts], ps[:].rearrange("p (c n) -> p c n", c=DC),
                                  zT_hi[j][:, :, ts].bitcast(F32), ALU.subtract).then_inc(low, 1)

            def batch(b, j, has_x, has_load, seen):
                if has_x:
                    for n in range(X):
                        low_x(1 - j, bank(n, True), n, split(b, n, True))
                if has_load:
                    statistics(b + 2, j, seen + 1)
                dve.wait_ge(stored[j], 16 * NS * seen)
                for which, (hi, lo) in ((1, kT[j]), (0, qT[j])):
                    for k in range(KQ):
                        n = X + (1 - which) * KQ + k
                        m, s = k // 2, slice(k % 2 * HALF, (k % 2 + 1) * HALF)
                        dve.wait_ge(high, split(b, n, has_x) + 1)
                        dve.scalar_tensor_tensor(lo[:, m, s], bank(n, has_x)[:], bcol[:, which, m:m + 1],
                                                 hi[:, m, s].bitcast(F32), ALU.add, ALU.subtract).then_inc(low, 1)
                for k in range(V):
                    n = X + 2 * KQ + k
                    dve.wait_ge(full, fill(b, n, has_x) + 1)
                    dve.tensor_tensor(v[j][:, 2 * k:2 * k + 2, :, 0:HD],
                                      bank(n, has_x)[:].rearrange("p (t h d) -> p t h d", t=2, h=H),
                                      bv_row[:].rearrange("p (h d) -> p h d", h=H).unsqueeze(1).to_broadcast([P, 2, H, HD]),
                                      ALU.add).then_inc(low, 1)

            statistics(0, 0, 1)
            for n in range(X):
                low_x(0, ring[n], n, n)
            statistics(1, 1, 1)
            with dve.Fori(0, (B - 2) // 2) as i:
                for j in range(2):
                    batch(2 * i + j, j, True, True, i + 1)
            batch(B - 2, 0, True, False, B // 2)
            batch(B - 1, 1, False, False, B // 2)


SHIFT_ON_ACT = (2, 4, 7)
SHIFT_ON_DVE = tuple(h for h in range(H) if h not in SHIFT_ON_ACT)


def heads_attend(nc, tag, x_in, x_out, adj, q_parts, k_parts, v_in, wo, bo, B, N):
    T = N // P
    G = B * T
    HALF = 512
    nA, nD = len(SHIFT_ON_ACT), len(SHIFT_ON_DVE)

    with nc.cleanup_on_exit(), ExitStack() as ctx:
        def sb(name, shape, dt=F32):
            return ctx.enter_context(nc.sbuf_tensor(f"{tag}_{name}", shape, dt))

        def pb(name, shape):
            return ctx.enter_context(nc.psum_tensor(f"{tag}_{name}", shape, F32))

        def sem(name):
            return nc.alloc_semaphore(name=f"{tag}_{name}")

        q_tile = [sb(f"q_tile{j}", [P, H, P], F32R) for j in range(2)]
        k_stack = sb("k_stack", [P, 2, H, N], F32R)
        v = sb("v", [P, 2, T, H, HV])
        wo_raw, wo_hi, wo_lo = sb("wo_raw", [P, DC, D]), sb("wo_hi", [P, DC, D], F32R), sb("wo_lo", [P, DC, D], F32R)
        bo_row = sb("bo_row", [P, D])
        ident, tenth = sb("ident", [P, P]), sb("tenth", [P, 1])
        x_res = [sb(f"x_res{j}", [P, D]) for j in range(2)]
        x_new = [sb(f"x_new{j}", [P, D]) for j in range(2)]
        adj_sb = [sb(f"adj_sb{j}", [P, N], I32) for j in range(2)]
        bias = [sb(f"bias{j}", [P, N]) for j in range(2)]
        adj_f, edge, masked = sb("adj_f", [P, N]), sb("edge", [P, N]), sb("masked", [P, N])
        score = [sb(f"score{j}", [P, N]) for j in range(2)]
        prob = [sb(f"prob{j}", [P, T, P]) for j in range(2)]
        row_max = [sb(f"row_max{j}", [P, 1]) for j in range(2)]
        inv, att = sb("inv", [P, H, 1]), sb("att", [P, H, HD])
        attT_hi, attT_lo = sb("attT_hi", [P, DC, P], F32R), sb("attT_lo", [P, DC, P], F32R)

        ps_s = [pb(f"ps_s{j}", [P, N]) for j in range(2)]
        ps_t = pb("ps_t", [P, N])
        ps_o = [pb(f"ps_o{j}", [P, HALF]) for j in range(2)]

        names = ("w_in ready w_part w_split bias_part bias_made score_full taken shifted_d shifted_a turned exp_done "
                 "out_full inv_done att_done attT_full attT_high attT_low wo_full x_done res_ready kv_in passed")
        (w_in, ready, w_part, w_split, bias_part, bias_made, score_full, taken, shifted_d, shifted_a, turned, exp_done,
         out_full, inv_done, att_done, attT_full, attT_high, attT_low, wo_full, x_done, res_ready, kv_in, passed) = (
            sem(n) for n in names.split())
        adj_in, q_in, res_in, stored = ([sem(f"{n}{j}") for j in range(2)] for n in ("adj_in", "q_in", "res_in", "stored"))

        x_in_g = x_in.rearrange("b (t p) d -> (b t) p d", p=P)
        x_out_g = x_out.rearrange("b (t p) d -> (b t) p d", p=P)
        adj_g = adj.rearrange("b (t p) m -> (b t) p m", p=P)
        q_g = q_parts.rearrange("g s (h p) n -> g s p h n", h=H)
        k_b = k_parts.rearrange("b s (h p) n -> b s p h n", h=H)
        HT = T // 2
        GT = G // 2
        KV = 16 * 5 * HT
        block = ctx.enter_context(nc.Block())

        @block.sync
        def _(sp):
            def load_q(g, j):
                for r, part in enumerate((0, 0, 1, 1)):
                    sp.dma_start(q_tile[j][32 * r:32 * r + 32, :, :].bitcast(F32), q_g[g, part]).then_inc(q_in[j], 16)

            def load_kv(b, slot, c):
                for r, part in enumerate((0, 1, 0, 1)):
                    sp.dma_start(k_stack[32 * r:32 * r + 32, slot, bass.ts(c, 2), :].bitcast(F32),
                                 k_b[b, part][:, bass.ts(c, 2), :]).then_inc(kv_in, 16)
                sp.dma_start(v[:, slot, bass.ts(c, 2)].rearrange("p t h d -> p (t h d)"),
                             v_in[b][:, bass.ts(c, 2 * H * HV)]).then_inc(kv_in, 16)

            def load_adj(g, j):
                sp.dma_start(adj_sb[j][:], adj_g[g]).then_inc(adj_in[j], 16)

            def load_residual(g, j):
                sp.dma_start(x_res[j][:], x_in_g[g]).then_inc(res_in[j], 16)

            def pair(i, last, kv=None):
                if kv is not None:
                    b, slot, c = kv
                    sp.wait_ge(out_full, b * T)
                    sp.wait_ge(kv_in, KV * (b + 1))
                    sp.sem_inc(passed, 1)
                    load_kv(b + 1, slot, c)
                if not last:
                    for j in range(2):
                        sp.wait_ge(bias_part, 4 * (2 * i + j) + 1)
                        load_adj(2 * i + j + 2, j)
                        sp.wait_ge(score_full, (2 * i + j + 1) * H)
                        load_q(2 * i + j + 2, j)
                for j in range(2):
                    sp.wait_ge(x_done, 2 * i + j + 1 + 2)
                    sp.dma_start(x_out_g[2 * i + j], x_new[j][:]).then_inc(stored[j], 16)
                    if not last:
                        load_residual(2 * i + j + 2, j)

            load_q(0, 0)
            sp.dma_start(wo_raw[:], wo.rearrange("(c p) n -> p c n", p=P)).then_inc(w_in, 16)
            sp.dma_start(bo_row[:], bo.partition_broadcast(P)).then_inc(w_in, 16)
            load_adj(0, 0)
            for c in range(HT):
                load_kv(0, 0, c)
            load_adj(1, 1)
            load_q(1, 1)
            for j in range(2):
                load_residual(j, j)
                sp.sem_inc(stored[j], 16)
            sp.wait_ge(kv_in, KV)
            sp.sem_inc(passed, 1)
            for c in range(HT):
                load_kv(1, 1, c)
            with sp.Fori(0, HT) as i:
                pair(i, False)
            with sp.Fori(0, (B - 2) // 2) as bb:
                for k in range(2):
                    b = 2 * bb + 1 + k
                    with sp.Fori(0, HT) as i:
                        pair(b * HT + i, False, (b, k, i))
            with sp.Fori(0, HT - 1) as i:
                pair((B - 1) * HT + i, False)
            pair(GT - 1, True)
            for j in range(2):
                sp.wait_ge(stored[j], 16 * (GT + 1))

        @block.gpsimd
        def _(pool):
            pool.memset(ident[:], 0.0).then_inc(ready, 1)
            pool.memset(tenth[:], 0.1).then_inc(ready, 1)
            pool.wait_ge(ready, 2)
            pool.affine_select(out=ident[:], in_=ident[:], compare_op=ALU.not_equal, fill=1.0,
                               base=0, pattern=[[-1, P]], channel_multiplier=1).then_inc(ready, 1)
            pool.wait_ge(w_in, 16 * 2)

            def make_bias(g, j, seen):
                pool.wait_ge(adj_in[j], 16 * seen)
                pool.sem_inc(passed, 1)
                pool.tensor_copy(adj_f[:], adj_sb[j][:]).then_inc(bias_part, 1)
                pool.wait_ge(bias_part, 4 * g + 1)
                pool.tensor_tensor(edge[:], adj_f[:], tenth[:].to_broadcast([P, N]), ALU.mult).then_inc(bias_part, 1)
                pool.tensor_scalar(masked[:], adj_f[:], 0.0, -BIG, ALU.is_le, ALU.mult).then_inc(bias_part, 1)
                pool.wait_ge(bias_part, 4 * g + 3)
                pool.tensor_tensor(edge[:], edge[:], adj_f[:], ALU.mult).then_inc(bias_part, 1)
                pool.wait_ge(bias_part, 4 * g + 4)
                pool.wait_ge(taken, (g + 1) * H)
                pool.tensor_tensor(bias[j][:], edge[:], masked[:], ALU.add).then_inc(bias_made, 1)

            def residual(j, seen):
                pool.wait_ge(res_in[j], 16 * seen)
                pool.tensor_tensor(x_res[j][:], x_res[j][:], bo_row[:], ALU.add).then_inc(res_ready, 1)

            with pool.Fori(0, GT) as i:
                for j in range(2):
                    make_bias(2 * i + j, j, i + 1)
                    residual(j, i + 1)

        @block.scalar
        def _(act):
            def shift(g, h):
                act.wait_ge(taken, g * H + h + 1 + 2 * H)
                act.activation(score[h % 2][:], score[h % 2][:], ACT.Identity, bias=row_max[h % 2][:], scale=-1.0)\
                   .then_inc(shifted_a, 1)

            def exps(g, h):
                sign = -1.0 if h in SHIFT_ON_ACT else 1.0
                for k in range(2):
                    half = slice(k * T // 2, (k + 1) * T // 2)
                    act.wait_ge(turned, 2 * (g * H + h) + k + 1)
                    act.activation(prob[h % 2][:, half, :], ps_t[:, k * HALF:(k + 1) * HALF].rearrange("p (t n) -> p t n", n=P),
                                   ACT.Exp, scale=sign).then_inc(exp_done, 1)

            def att_split(g, j):
                act.wait_ge(attT_full, g + 1)
                act.activation(attT_hi[:], ps_o[j][:, 0:D].rearrange("p (c n) -> p c n", c=DC), ACT.Identity)\
                   .then_inc(attT_high, 1)

            def tile(g, j, first):
                for h in range(H):
                    exps(g, h)
                    if h + 1 in SHIFT_ON_ACT:
                        shift(g, h + 1)
                    if h == 3 and not first:
                        att_split(g - 1, 1 - j)

            act.sem_inc(exp_done, 2)
            tile(0, 0, True)
            tile(1, 1, False)
            with act.Fori(1, GT) as i:
                for j in range(2):
                    tile(2 * i + j, j, False)
            att_split(G - 1, 1)

        @block.tensor
        def _(pe):
            def three(out, l_hi, l_lo, r_hi, r_lo, n, last):
                pe.matmul(out, l_hi, r_hi, start=(n == 0), stop=False)
                pe.matmul(out, l_hi, r_lo, start=False, stop=False)
                return pe.matmul(out, l_lo, r_hi, start=False, stop=(n == last))

            def scores(h, j, slot):
                for k in range(2):
                    mm = pe.matmul(ps_s[h % 2][:, k * HALF:(k + 1) * HALF], q_tile[j][:, h, :],
                                   k_stack[:, slot, h, k * HALF:(k + 1) * HALF], start=True, stop=True)
                mm.then_inc(score_full, 1)

            def turn(g, h):
                if h in SHIFT_ON_ACT:
                    pe.wait_ge(shifted_a, g * nA + SHIFT_ON_ACT.index(h) + 1)
                else:
                    pe.wait_ge(shifted_d, g * nD + SHIFT_ON_DVE.index(h) + 1)
                for k in range(2):
                    pe.wait_ge(exp_done, 2 * (g * H + h) + k + 1)
                    for c in range(k * T // 2, (k + 1) * T // 2):
                        mm = pe.transpose(ps_t[:, c * P:(c + 1) * P], score[h % 2][:, c * P:(c + 1) * P], ident[:])
                    mm.then_inc(turned, 1)

            def weigh(g, h, j, slot):
                if h == 0:
                    pe.wait_ge(x_done, g + 1)
                for c in range(T):
                    if c % (T // 2) == 0:
                        pe.wait_ge(exp_done, 2 * (g * H + h) + 2 * c // T + 1 + 2)
                    mm = pe.matmul(ps_o[j][:, h * HV:(h + 1) * HV], prob[h % 2][:, c, :], v[:, slot, c, h, :],
                                   start=(c == 0), stop=(c == T - 1))
                if h == H - 1:
                    mm.then_inc(out_full, 1)

            def turn_att(g, j):
                pe.wait_ge(att_done, g + 1)
                for c in range(DC):
                    mm = pe.transpose(ps_o[j][:, c * P:(c + 1) * P], att[:].rearrange("p h d -> p (h d)")[:, c * P:(c + 1) * P],
                                      ident[:])
                mm.then_inc(attT_full, 1)

            def project_att(g, j):
                pe.wait_ge(attT_low, g + 1)
                for c in range(DC):
                    mm = three(ps_o[j][:, D:2 * D], attT_hi[:, c, :], attT_lo[:, c, :], wo_hi[:, c, :], wo_lo[:, c, :],
                               c, DC - 1)
                mm.then_inc(wo_full, 1)

            def tile(b, i, j, slot, prev, then):
                g = b * T + 2 * i + j
                for h in range(H):
                    turn(g, h)
                    if h + 2 < H:
                        scores(h + 2, j, slot)
                    elif then is not None:
                        if h + 2 == H:
                            pe.wait_ge(q_in[1 - j], 16 * 4 * (b * HT + i + j + 1))
                        scores(h + 2 - H, 1 - j, then)
                    if h > 0:
                        weigh(g, h - 1, j, slot)
                    elif prev is not None:
                        weigh(g - 1, H - 1, 1 - j, prev)
                    if prev is not None:
                        if h == 2:
                            turn_att(g - 1, 1 - j)
                        if h == 5:
                            project_att(g - 1, 1 - j)

            def batch(b, slot, first, last):
                tile(b, 0, 0, slot, None if first else 1 - slot, slot)
                with pe.Fori(0, HT - 1) as i:
                    tile(b, i, 1, slot, slot, slot)
                    tile(b, i + 1, 0, slot, slot, slot)
                if not last:
                    pe.wait_ge(kv_in, KV * (b + 2))
                tile(b, HT - 1, 1, slot, slot, None if last else 1 - slot)

            pe.wait_ge(ready, 3)
            pe.wait_ge(w_split, 1)
            pe.wait_ge(q_in[0], 16 * 4)
            pe.wait_ge(kv_in, KV)
            scores(0, 0, 0)
            scores(1, 0, 0)
            batch(0, 0, True, False)
            if B > 2:
                with pe.Fori(0, (B - 2) // 2) as i:
                    batch(2 * i + 1, 1, False, False)
                    batch(2 * i + 2, 0, False, False)
            batch(B - 1, 1, False, True)
            weigh(G - 1, H - 1, 1, 1)
            turn_att(G - 1, 1)
            project_att(G - 1, 1)

        @block.vector
        def _(dve):
            dve.wait_ge(w_in, 16 * 2)
            dve.tensor_copy(wo_hi[:], wo_raw[:]).then_inc(w_part, 1)
            dve.wait_ge(w_part, 1)
            dve.tensor_tensor(wo_lo[:], wo_raw[:], wo_hi[:].bitcast(F32), ALU.subtract).then_inc(w_split, 1)
            dve.sem_inc(taken, 2 * H)
            dve.sem_inc(x_done, 2)

            def take(g, h, j):
                dve.wait_ge(score_full, g * H + h + 1)
                if h == 0:
                    dve.wait_ge(bias_made, g + 1)
                dve.sem_inc(passed, 1)
                dve.tensor_tensor_reduce(score[h % 2][:], ps_s[h % 2][:], bias[j][:], 1.0, -3.0e38, ALU.add, ALU.max,
                                         row_max[h % 2][:]).then_inc(taken, 1)
                if h not in SHIFT_ON_ACT:
                    dve.wait_ge(taken, g * H + h + 1 + 2 * H)
                    dve.tensor_scalar(score[h % 2][:], score[h % 2][:], row_max[h % 2][:], None, ALU.subtract)\
                       .then_inc(shifted_d, 1)

            def average(g, j):
                dve.wait_ge(out_full, g + 1)
                o = ps_o[j][:, 0:H * HV].rearrange("p (h d) -> p h d", h=H)
                dve.reciprocal(inv[:], o[:, :, HD:HV]).then_inc(inv_done, 1)
                dve.wait_ge(inv_done, g + 1)
                dve.tensor_tensor(att[:], o[:, :, 0:HD], inv[:].to_broadcast([P, H, HD]), ALU.mult).then_inc(att_done, 1)

            def att_low(g, j):
                dve.wait_ge(attT_high, g + 1)
                dve.tensor_tensor(attT_lo[:], ps_o[j][:, 0:D].rearrange("p (c n) -> p c n", c=DC),
                                  attT_hi[:].bitcast(F32), ALU.subtract).then_inc(attT_low, 1)

            def add_residual(g, j, seen):
                dve.wait_ge(stored[j], 16 * seen)
                dve.wait_ge(res_ready, g + 1)
                dve.wait_ge(wo_full, g + 1)
                dve.tensor_tensor(x_new[j][:], ps_o[j][:, D:2 * D], x_res[j][:], ALU.add).then_inc(x_done, 1)

            def tile(g, j, first, seen):
                for h in range(H):
                    take(g, h, j)
                    if not first:
                        if h == 2:
                            average(g - 1, 1 - j)
                        if h == 4:
                            att_low(g - 1, 1 - j)
                        if h == 7:
                            add_residual(g - 1, 1 - j, seen)

            tile(0, 0, True, 0)
            tile(1, 1, False, 1)
            with dve.Fori(1, GT) as i:
                tile(2 * i, 0, False, i)
                tile(2 * i + 1, 1, False, i + 1)
            average(G - 1, 1)
            att_low(G - 1, 1)
            add_residual(G - 1, 1, GT)


FW = 4 * D
FT = FW // P


def mlp_layer(nc, tag, x_in, x_out, g2, b2n, w1, b1, w2, b2, B, N):
    HALF = 512
    CT = HALF // P
    NC = B * N // HALF

    with nc.cleanup_on_exit(), ExitStack() as ctx:
        def sb(name, shape, dt=F32):
            return ctx.enter_context(nc.sbuf_tensor(f"{tag}_{name}", shape, dt))

        def pb(name, shape):
            return ctx.enter_context(nc.psum_tensor(f"{tag}_{name}", shape, F32))

        def sem(name):
            return nc.alloc_semaphore(name=f"{tag}_{name}")

        w1_raw, w2_raw = sb("w1_raw", [P, DC, FW]), sb("w2_raw", [P, FT, D])
        w1_hi, w1_lo = sb("w1_hi", [P, DC, FW], F32R), sb("w1_lo", [P, DC, FW], F32R)
        w2_hi, w2_lo = sb("w2_hi", [P, FT, D], F32R), sb("w2_lo", [P, FT, D], F32R)
        col = sb("col", [P, 2, DC])
        b1_col, b1_all = sb("b1_col", [P, FT]), sb("b1_all", [P, FT])
        b2_row = sb("b2_row", [P, D])
        ident, small = sb("ident", [P, P]), sb("small", [P, 3])
        x_c = [sb(f"x_c{j}", [P, CT, D]) for j in range(2)]
        x_new = [sb(f"x_new{j}", [P, CT, D]) for j in range(2)]
        z = sb("z", [P, CT, D])
        zT_hi, zT_lo = sb("zT_hi", [P, DC, HALF], F32R), sb("zT_lo", [P, DC, HALF], F32R)
        h = [sb(f"h{i}", [P, HALF]) for i in range(2)]
        h_hi, h_lo = sb("h_hi", [P, FT, HALF], F32R), sb("h_lo", [P, FT, HALF], F32R)
        stats, mean_var, ln_c = sb("stats", [P, CT, 6]), sb("mean_var", [P, CT, 2]), sb("ln_c", [P, 4, CT])

        ps_z = pb("ps_z", [P, DC, HALF])
        ps_h = [pb(f"ps_h{i}", [P, HALF]) for i in range(2)]
        ps_o = [pb(f"ps_o{i}", [P, HALF]) for i in range(2)]

        names = ("w_in ready w_part b_ps w_split stored z_full zT_high zT_low h_full h_gelu h_high h_low_d h_low_p "
                 "stat_part stats_done rstd_part rstd_done z_done res_done out_full x_done passed")
        (w_in, ready, w_part, b_ps, w_split, stored, z_full, zT_high, zT_low, h_full, h_gelu, h_high, h_low_d, h_low_p,
         stat_part, stats_done, rstd_part, rstd_done, z_done, res_done, out_full, x_done, passed) = (
            sem(n) for n in names.split())
        x_in_s = [sem(f"x_in{j}") for j in range(2)]

        xi = x_in.rearrange("b (c t p) d -> (b c) p t d", p=P, t=CT)
        xo = x_out.rearrange("b (c t p) d -> (b c) p t d", p=P, t=CT)
        block = ctx.enter_context(nc.Block())
        NP2 = NC // 2

        @block.sync
        def _(sp):
            sp.dma_start(w1_raw[:], w1.rearrange("(c p) n -> p c n", p=P)).then_inc(w_in, 16)
            sp.dma_start(w2_raw[:], w2.rearrange("(c p) n -> p c n", p=P)).then_inc(w_in, 16)
            for i, c in enumerate((g2, b2n)):
                sp.dma_start(col[:, i, :].unsqueeze(2), c.rearrange("(c p o) -> p c o", p=P, o=1),
                             allow_slow_non_contiguous=True).then_inc(w_in, 16)
            sp.dma_start(b1_col[:].unsqueeze(2), b1.rearrange("(c p o) -> p c o", p=P, o=1),
                         allow_slow_non_contiguous=True).then_inc(w_in, 16)
            sp.dma_start(b2_row[:], b2.partition_broadcast(P)).then_inc(w_in, 16)
            for j in range(2):
                sp.dma_start(x_c[j][:], xi[j]).then_inc(x_in_s[j], 16)
            sp.sem_inc(stored, 16 * 2)

            def store(c, j):
                sp.wait_ge(x_done, CT * (c + 1) + 2)
                sp.dma_start(xo[c], x_new[j][:]).then_inc(stored, 16)

            with sp.Fori(0, NP2 - 1) as i:
                for j in range(2):
                    store(2 * i + j, j)
                    sp.dma_start(x_c[j][:], xi[2 * i + 2 + j]).then_inc(x_in_s[j], 16)
            for j in range(2):
                store(NC - 2 + j, j)
            sp.wait_ge(stored, 16 * (NC + 2))

        @block.gpsimd
        def _(pool):
            pool.memset(ident[:], 0.0).then_inc(ready, 1)
            pool.memset(small[:, 0:1], -0.5).then_inc(ready, 1)
            pool.memset(small[:, 1:2], -1.0).then_inc(ready, 1)
            pool.memset(small[:, 2:3], EPS).then_inc(ready, 1)
            pool.wait_ge(ready, 4)
            pool.affine_select(out=ident[:], in_=ident[:], compare_op=ALU.not_equal, fill=1.0,
                               base=0, pattern=[[-1, P]], channel_multiplier=1).then_inc(ready, 1)
            pool.wait_ge(w_in, 16 * 6)
            pool.sem_inc(h_low_p, 1)
            e = [small[:, k:k + 1].to_broadcast([P, CT]) for k in range(3)]

            def norm_consts(c):
                pool.wait_ge(stats_done, (c + 1) * CT)
                pool.tensor_tensor(ln_c[:, 0, :], mean_var[:, :, 1], e[2], ALU.add).then_inc(rstd_part, 1)
                pool.wait_ge(rstd_part, 3 * c + 1)
                pool.tensor_tensor(ln_c[:, 1, :], ln_c[:, 0, :], e[0], ALU.pow).then_inc(rstd_part, 1)
                pool.wait_ge(rstd_part, 3 * c + 2)
                pool.tensor_tensor(ln_c[:, 3, :], mean_var[:, :, 0], ln_c[:, 1, :], ALU.mult).then_inc(rstd_part, 1)
                pool.wait_ge(rstd_part, 3 * c + 3)
                pool.tensor_tensor(ln_c[:, 2, :], ln_c[:, 3, :], e[1], ALU.mult).then_inc(rstd_done, 1)

            def residual(c, j):
                pool.wait_ge(z_done, CT * (c + 1))
                pool.tensor_tensor(x_c[j][:], x_c[j][:], b2_row[:].unsqueeze(1).to_broadcast([P, CT, D]), ALU.add)\
                    .then_inc(res_done, 1)

            def chunk(c, j, last):
                if not last:
                    norm_consts(c + 1)
                for f in range(1, FT, 2):
                    pool.wait_ge(h_high, FT * c + f + 1)
                    pool.tensor_tensor(h_lo[:, f, :], h[f % 2][:], h_hi[:, f, :].bitcast(F32), ALU.subtract).then_inc(h_low_p, 1)
                    if f == 3 and not last:
                        residual(c + 1, 1 - j)

            norm_consts(0)
            residual(0, 0)
            with pool.Fori(0, NP2 - 1) as i:
                for j in range(2):
                    chunk(2 * i + j, j, False)
            chunk(NC - 2, 0, False)
            chunk(NC - 1, 1, True)

        @block.scalar
        def _(act):
            def normalise(c, j):
                act.wait_ge(rstd_done, c + 1)
                act.sem_inc(passed, 1)
                for t in range(CT):
                    act.activation(z[:, t, :], x_c[j][:, t, :], ACT.Identity, bias=ln_c[:, 2, t:t + 1],
                                   scale=ln_c[:, 1, t:t + 1]).then_inc(z_done, 1)

            def split_high(c):
                for d in range(DC):
                    act.wait_ge(z_full, DC * c + d + 1)
                    act.activation(zT_hi[:, d, :], ps_z[:, d, :], ACT.Identity).then_inc(zT_high, 1)

            def chunk(c, j, last):
                for f in range(FT):
                    act.wait_ge(h_full, FT * c + f + 1)
                    act.wait_ge(h_low_p if f % 2 else h_low_d, FT // 2 * c + f // 2 + 1)
                    act.activation(h[f % 2][:], ps_h[f % 2][:], ACT.Gelu, bias=b1_all[:, f:f + 1]).then_inc(h_gelu, 1)
                    if f == 1 and not last:
                        normalise(c + 1, 1 - j)
                if not last:
                    split_high(c + 1)

            act.wait_ge(w_split, 1)
            act.sem_inc(h_gelu, 2)
            normalise(0, 0)
            split_high(0)
            with act.Fori(0, NP2 - 1) as i:
                for j in range(2):
                    chunk(2 * i + j, j, False)
            chunk(NC - 2, 0, False)
            chunk(NC - 1, 1, True)

        @block.tensor
        def _(pe):
            def three(out, l_hi, l_lo, r_hi, r_lo, n, last):
                pe.matmul(out, l_hi, r_hi, start=(n == 0), stop=False)
                pe.matmul(out, l_hi, r_lo, start=False, stop=False)
                return pe.matmul(out, l_lo, r_hi, start=False, stop=(n == last))

            pe.wait_ge(w_in, 16 * 6)
            for f in range(FT):
                for c in range(DC):
                    mm = pe.matmul(ps_h[0][:, f:f + 1], w1_raw[:, c, f * P:(f + 1) * P], col[:, 1, c:c + 1],
                                   start=(c == 0), stop=(c == DC - 1))
            mm.then_inc(b_ps, 1)
            pe.wait_ge(ready, 5)
            pe.wait_ge(w_split, 1)

            def turn(c):
                pe.wait_ge(z_done, CT * (c + 1))
                for d in range(DC):
                    for t in range(CT):
                        mm = pe.transpose(ps_z[:, d, t * P:(t + 1) * P], z[:, t, d * P:(d + 1) * P], ident[:])
                    mm.then_inc(z_full, 1)

            def chunk(c, j, last):
                pe.wait_ge(zT_low, DC * (c + 1))
                for f in range(FT):
                    pe.wait_ge(h_gelu, FT * c + f + 1)
                    for d in range(DC):
                        s = slice(f * P, (f + 1) * P)
                        mm = three(ps_h[f % 2][:], w1_hi[:, d, s], w1_lo[:, d, s], zT_hi[:, d, :], zT_lo[:, d, :], d, DC - 1)
                    mm.then_inc(h_full, 1)
                if not last:
                    turn(c + 1)
                pe.wait_ge(h_low_d, FT // 2 * (c + 1) + 1)
                pe.wait_ge(h_low_p, FT // 2 * (c + 1) + 1)
                for t in range(CT):
                    pe.wait_ge(x_done, CT * c + t + 1)
                    s = slice(t * P, (t + 1) * P)
                    for f in range(FT):
                        mm = three(ps_o[t % 2][:, 0:D], h_hi[:, f, s], h_lo[:, f, s], w2_hi[:, f, :], w2_lo[:, f, :], f, FT - 1)
                    mm.then_inc(out_full, 1)

            turn(0)
            with pe.Fori(0, NP2 - 1) as i:
                for j in range(2):
                    chunk(2 * i + j, j, False)
            chunk(NC - 2, 0, False)
            chunk(NC - 1, 1, True)

        @block.vector
        def _(dve):
            k = 0

            def stepped(ins):
                nonlocal k
                ins.then_inc(w_part, 1)
                k += 1
                dve.wait_ge(w_part, k)

            dve.wait_ge(w_in, 16 * 6)
            dve.wait_ge(b_ps, 1)
            stepped(dve.tensor_tensor(b1_all[:], ps_h[0][:, 0:FT], b1_col[:], ALU.add))
            for c in range(DC):
                stepped(dve.tensor_scalar(w1_raw[:, c, :], w1_raw[:, c, :], col[:, 0, c:c + 1], None, ALU.mult))
            stepped(dve.tensor_copy(w1_hi[:], w1_raw[:]))
            stepped(dve.tensor_tensor(w1_lo[:], w1_raw[:], w1_hi[:].bitcast(F32), ALU.subtract))
            stepped(dve.tensor_copy(w2_hi[:], w2_raw[:]))
            stepped(dve.tensor_tensor(w2_lo[:], w2_raw[:], w2_hi[:].bitcast(F32), ALU.subtract))
            dve.sem_inc(w_split, 1)
            dve.sem_inc(x_done, 2)
            dve.sem_inc(h_low_d, 1)

            def statistics(c, j, seen):
                dve.wait_ge(x_in_s[j], 16 * seen)
                dve.sem_inc(passed, 1)
                for t in range(CT):
                    dve.bn_stats(stats[:, t, :], x_c[j][:, t, :]).then_inc(stat_part, 1)
                dve.wait_ge(stat_part, (c + 1) * CT)
                dve.sem_inc(passed, 1)
                for t in range(CT):
                    dve.bn_aggr(mean_var[:, t, :], stats[:, t, :]).then_inc(stats_done, 1)

            def split_low(c):
                for d in range(DC):
                    dve.wait_ge(zT_high, DC * c + d + 1)
                    dve.tensor_tensor(zT_lo[:, d, :], ps_z[:, d, :], zT_hi[:, d, :].bitcast(F32), ALU.subtract)\
                       .then_inc(zT_low, 1)

            def chunk(c, j, last, seen):
                if not last:
                    statistics(c + 1, 1 - j, seen)
                for f in range(FT):
                    dve.wait_ge(h_gelu, FT * c + f + 1 + 2)
                    dve.tensor_copy(h_hi[:, f, :], h[f % 2][:]).then_inc(h_high, 1)
                    if f % 2 == 0:
                        dve.wait_ge(h_high, FT * c + f + 1)
                        dve.tensor_tensor(h_lo[:, f, :], h[f % 2][:], h_hi[:, f, :].bitcast(F32), ALU.subtract)\
                           .then_inc(h_low_d, 1)
                if not last:
                    split_low(c + 1)
                dve.wait_ge(stored, 16 * (c + 1))
                dve.wait_ge(res_done, c + 1)
                dve.sem_inc(passed, 1)
                for t in range(CT):
                    dve.wait_ge(out_full, CT * c + t + 1)
                    dve.tensor_tensor(x_new[j][:, t, :], ps_o[t % 2][:, 0:D], x_c[j][:, t, :], ALU.add).then_inc(x_done, 1)

            statistics(0, 0, 1)
            split_low(0)
            with dve.Fori(0, NP2 - 1) as i:
                chunk(2 * i, 0, False, i + 1)
                chunk(2 * i + 1, 1, False, i + 2)
            chunk(NC - 2, 0, False, NP2)
            chunk(NC - 1, 1, True, NP2 + 1)


def graph_net(nc, x, adj, adj_turned, ln1_g, ln1_b, ln2_g, ln2_b, wq0, bq0, wk0, bk0, wv0, bv0, wo0, bo0, w1, b1, w2, b2,
              w_dir, b_dir, gamma1, beta1, wq2, wk2, wv2, wo2, bo2, gamma2, beta2, wq3, bq3, wk3, bk3, wc3, gamma3, beta3,
              out):
    B, N, _ = x.shape
    mid = [nc.dram_tensor(f"x_layer{i}", [B, N, D], F32).ap() for i in range(5)]
    q_parts = nc.dram_tensor("q_parts", [B * N // P, 2, D, P], F32).ap()
    k_parts = nc.dram_tensor("k_parts", [B, 2, D, N], F32).ap()
    v_heads = nc.dram_tensor("v_heads", [B, P, N // P * H * HV], F32).ap()
    heads_project(nc, "proj", x, q_parts, k_parts, v_heads, ln1_g, ln1_b, wq0, bq0, wk0, bk0, wv0, bv0, B, N)
    heads_attend(nc, "heads", x, mid[0], adj, q_parts, k_parts, v_heads, wo0, bo0, B, N)
    mlp_layer(nc, "mlp", mid[0], mid[1], ln2_g, ln2_b, w1, b1, w2, b2, B, N)
    direction_layer(nc, "dir", mid[1], mid[2], adj_turned, w_dir, b_dir, gamma1, beta1, B, N)
    attention_layer(nc, "fold", mid[2], mid[3], adj, wq2, wk2, wv2, wo2, None, None, bo2, gamma2, beta2,
                    float(D) ** -0.5, B, N)
    L, _, F = wq3.shape
    for k in range(L):
        attention_layer(nc, f"att{k}", mid[3 + k], out if k == L - 1 else mid[4 + k], adj, wq3[k], wk3[k], wc3[k], None,
                        bq3[k], bk3[k], None, gamma3[k], beta3[k], float(F) ** -0.5, B, N)


_INS = ["x", "adj", "adj_turned", "L0_gnn_ln1_g", "L0_gnn_ln1_b", "L0_gnn_ln2_g", "L0_gnn_ln2_b",
        "L0_gnn_wq", "L0_gnn_bq", "L0_gnn_wk", "L0_gnn_bk", "L0_gnn_wv", "L0_gnn_bv", "L0_gnn_wo", "L0_gnn_bo",
        "L0_gnn_w1", "L0_gnn_b1", "L0_gnn_w2", "L0_gnn_b2", "L1_gnn_W", "L1_gnn_b", "L1_gnn_gamma", "L1_gnn_beta",
        "L2_gnn_Wq", "L2_gnn_Wk", "L2_gnn_Wv", "L2_gnn_Wo", "L2_gnn_bo", "L2_gnn_gamma", "L2_gnn_beta",
        "L3_gnn_Wq", "L3_gnn_bq", "L3_gnn_Wk", "L3_gnn_bk", "L3_gnn_Wc", "L3_gnn_ln_g", "L3_gnn_ln_b"]


def kernel(**inputs):
    import numpy as _np
    import concourse.bacc as _bacc
    from concourse import mybir as _mybir
    from concourse.bass_utils import run_bass_kernel_spmd as _run

    data = dict(inputs)
    adj = _np.asarray(data["adj"])
    B, N, _ = adj.shape
    data["adj_turned"] = adj.reshape(B, N // 128, 128, N // 128, 128).transpose(0, 1, 4, 3, 2)
    for name in ("L2_gnn_Wq", "L2_gnn_Wk", "L2_gnn_Wv"):
        data[name] = _np.asarray(data[name]).T
    for name in ("L3_gnn_Wq", "L3_gnn_Wk", "L3_gnn_Wc"):
        data[name] = _np.asarray(data[name]).transpose(0, 2, 1)

    nc = _bacc.Bacc("TRN2", target_bir_lowering=False, num_devices=1)
    arrays, args = {}, []
    for name in _INS:
        a = _np.ascontiguousarray(data[name])
        arrays[f"in_{name}_dram"] = a
        args.append(nc.dram_tensor(f"in_{name}_dram", a.shape, _mybir.dt.from_np(a.dtype), kind="ExternalInput").ap())
    args.append(nc.dram_tensor("out_0_dram", data["x"].shape, _mybir.dt.float32, kind="ExternalOutput").ap())
    graph_net(nc, *args)
    r = _run(nc, [arrays], core_ids=[0])
    return r.results[0]["out_0_dram"]
```

```python
import concourse.bass as bass
from concourse import mybir
from contextlib import ExitStack

F32 = mybir.dt.float32
F32R = mybir.dt.float32r
I32 = mybir.dt.int32
ALU = mybir.AluOpType
ACT = mybir.ActivationFunctionType

P = 128
D = 256
DC = D // P
BIG = 1.0e30
EPS = 1.0e-5
DV = D + 2


def attention_layer(nc, tag, x_in, x_out, adj, wq_a, wk_a, wv_a, wo_a, bq, bk, bo, gamma, beta,
                    score_scale, B, N):
    folded = wo_a is not None
    T = N // P
    QC = DC if folded else 1
    KC = DC if folded else 1
    XB = T // 2
    KB = 0 if folded else N // 512
    VB = T // 2
    NP = XB + KB + VB
    HALF = 512

    with nc.cleanup_on_exit(), ExitStack() as ctx:
        def sb(name, shape, dt=F32):
            return ctx.enter_context(nc.sbuf_tensor(f"{tag}_{name}", shape, dt))

        def pb(name, shape):
            return ctx.enter_context(nc.psum_tensor(f"{tag}_{name}", shape, F32))

        def sem(name):
            return nc.alloc_semaphore(name=f"{tag}_{name}")

        w_raw = sb("w_raw", [P, 4 * DC * D])
        QW = D if folded else P
        wq_hi, wq_lo = sb("wq_hi", [P, DC, QW], F32R), sb("wq_lo", [P, DC, QW], F32R)
        wv_hi, wv_lo = sb("wv_hi", [P, DC, D], F32R), sb("wv_lo", [P, DC, D], F32R)
        if not folded:
            wk_hi, wk_lo = sb("wk_hi", [P, DC, P], F32R), sb("wk_lo", [P, DC, P], F32R)
            bqk = sb("bqk", [P, 2])
        else:
            bo_row = sb("bo_row", [P, D])
        w_fold = sb("w_fold", [P, 2, DC, D])
        gamma_row, beta_row = sb("gamma_row", [P, D]), sb("beta_row", [P, D])
        ident = sb("ident", [P, P])
        x_tok = sb("x_tok", [P, T, D])
        x_res = sb("x_res", [P, T, D])
        x_new = sb("x_new", [P, T, D])
        xT_hi, xT_lo = sb("xT_hi", [P, DC, N], F32R), sb("xT_lo", [P, DC, N], F32R)
        if folded:
            kT_hi, kT_lo = xT_hi, xT_lo
        else:
            kT_hi, kT_lo = sb("kT_hi", [P, 1, N], F32R), sb("kT_lo", [P, 1, N], F32R)
        v_hi, v_lo = sb("v_hi", [P, T, DV], F32R), sb("v_lo", [P, T, DV], F32R)
        qT_hi, qT_lo = sb("qT_hi", [P, QC, P], F32R), sb("qT_lo", [P, QC, P], F32R)
        adj_sb = sb("adj_sb", [P, T, N], I32)
        mask_bias = sb("mask_bias", [P, N])
        score = sb("score", [P, N])
        prob = sb("prob", [P, T, P])
        prob_hi, prob_lo = sb("prob_hi", [P, T, P], F32R), sb("prob_lo", [P, T, P], F32R)
        row_max = sb("row_max", [P, 1])
        has_key = sb("has_key", [P, 1])
        inv = sb("inv", [P, 2])
        y = sb("y", [P, D])
        stats = sb("stats", [P, 6])
        mean_var = sb("mean_var", [P, 2])
        ln_c = sb("ln_c", [P, 4])
        small = sb("small", [P, 3])

        ps_s = pb("ps_s", [P, N])
        ps_t = pb("ps_t", [P, N])
        ps_o = pb("ps_o", [P, HALF])
        ps_q = pb("ps_q", [P, HALF])
        ps_p = [pb(f"ps_p{i}", [P, HALF]) for i in range(2)]

        w_in, ready, w_ps, w_part = sem("w_in"), sem("ready"), sem("w_ps"), sem("w_part")
        x_loaded, res_in, adj_in, stored = sem("x_loaded"), sem("res_in"), sem("adj_in"), sem("stored")
        has_key_made, inv_made, stats_part, res_biased = sem("has_key_made"), sem("inv_made"), sem("stats_part"), sem("res_biased")
        proj_full, proj_hi, proj_lo = sem("proj_full"), sem("proj_hi"), sem("proj_lo")
        q_full, q_hi, q_lo = sem("q_full"), sem("q_hi"), sem("q_lo")
        score_full, shifted, turned = sem("score_full"), sem("shifted"), sem("turned")
        bias_made, bias_used = sem("bias_made"), sem("bias_used")
        exp_done, prob_high, prob_low_1, prob_low_2 = sem("exp_done"), sem("prob_high"), sem("prob_low_1"), sem("prob_low_2")
        out_full, out_read, stats_done = sem("out_full"), sem("out_read"), sem("stats_done")
        rstd_part, rstd_done, normed, new_part, new_done = (sem("rstd_part"), sem("rstd_done"),
                                                            sem("normed"), sem("new_part"), sem("new_done"))
        w_step = sem("w_step")
        ones_made = sem("ones_made")
        passed = sem("passed")

        x_in_t = x_in.rearrange("b (t p) d -> b p t d", p=P)
        x_out_t = x_out.rearrange("b (t p) d -> b p t d", p=P)
        adj_t = adj.rearrange("b (t p) m -> b t p m", p=P)
        raw = [w_raw[:, i * DC * D:(i + 1) * DC * D] for i in range(4)]

        NW = 4 + 2 + 1 if folded else 3 + 2 + 2

        def chunks(w):
            return w.rearrange("(c p) n -> p c n", p=P)

        block = ctx.enter_context(nc.Block())

        @block.sync
        def _(sp):
            weights = [wq_a, wk_a, wv_a] + ([wo_a] if folded else [])
            for i, w in enumerate(weights):
                n = w.shape[1]
                sp.dma_start(raw[i][:, 0:DC * n].rearrange("p (c n) -> p c n", c=DC), chunks(w)).then_inc(w_in, 16)
            sp.dma_start(gamma_row[:], gamma.partition_broadcast(P)).then_inc(w_in, 16)
            sp.dma_start(beta_row[:], beta.partition_broadcast(P)).then_inc(w_in, 16)
            if folded:
                sp.dma_start(bo_row[:], bo.partition_broadcast(P)).then_inc(w_in, 16)
            else:
                sp.dma_start(bqk[:, 0:1], bq.rearrange("(p o) -> p o", o=1)).then_inc(w_in, 16)
                sp.dma_start(bqk[:, 1:2], bk.rearrange("(p o) -> p o", o=1)).then_inc(w_in, 16)

            def load_tokens(b):
                sp.dma_start(x_tok[:], x_in_t[b]).then_inc(x_loaded, 16)

            def load_adj(b, t):
                sp.dma_start(adj_sb[:, t, :], adj_t[b, t]).then_inc(adj_in, 16)

            def load_residual(b):
                sp.dma_start(x_res[:], x_in_t[b]).then_inc(res_in, 16)

            def store(b, t):
                sp.wait_ge(new_done, b * T + t + 1)
                sp.dma_start(x_out_t[b][:, t, :], x_new[:, t, :]).then_inc(stored, 16)

            load_tokens(0)
            for t in range(T):
                if t > 0:
                    sp.wait_ge(adj_in, 16 * t)
                load_adj(0, t)
                if t == 0:
                    load_residual(0)
            sp.sem_inc(stored, 16 * T)
            with sp.Fori(0, B - 1) as b:
                sp.wait_ge(proj_full, b * NP + XB)
                load_tokens(b + 1)
                for t in range(T):
                    sp.wait_ge(bias_made, b * T + t + 1)
                    sp.wait_ge(adj_in, 16 * (b * T + T + t))
                    load_adj(b + 1, t)
                    if t == T - 1:
                        sp.wait_ge(out_read, (b + 1) * T + 1)
                        load_residual(b + 1)
                    store(b, t)
            for t in range(T):
                store(B - 1, t)
            sp.wait_ge(stored, 16 * T * (B + 1))

        @block.gpsimd
        def _(pool):
            pool.memset(ident[:], 0.0).then_inc(ready, 1)
            pool.memset(small[:, 0:1], -0.5).then_inc(ready, 1)
            pool.memset(small[:, 1:2], -1.0).then_inc(ready, 1)
            pool.memset(small[:, 2:3], EPS).then_inc(ready, 1)
            pool.wait_ge(ready, 4)
            pool.affine_select(out=ident[:], in_=ident[:], compare_op=ALU.not_equal, fill=1.0,
                               base=0, pattern=[[-1, P]], channel_multiplier=1).then_inc(ready, 1)
            pool.wait_ge(w_in, 16 * NW)

            def p_low(g):
                pool.wait_ge(prob_high, 2 * g + 2)
                for k in (2, 3):
                    part = slice(k * T // 4, (k + 1) * T // 4)
                    pool.tensor_tensor(prob_lo[:, part, :], prob[:, part, :], prob_hi[:, part, :].bitcast(F32),
                                       ALU.subtract).then_inc(prob_low_2, 1)

            def norm_consts(g):
                pool.wait_ge(stats_done, g + 1)
                pool.tensor_tensor(ln_c[:, 0:1], mean_var[:, 1:2], small[:, 2:3], ALU.add).then_inc(rstd_part, 1)
                pool.wait_ge(rstd_part, 3 * g + 1)
                pool.tensor_tensor(ln_c[:, 1:2], ln_c[:, 0:1], small[:, 0:1], ALU.pow).then_inc(rstd_part, 1)
                pool.wait_ge(rstd_part, 3 * g + 2)
                pool.tensor_tensor(ln_c[:, 3:4], mean_var[:, 0:1], ln_c[:, 1:2], ALU.mult).then_inc(rstd_part, 1)
                pool.wait_ge(rstd_part, 3 * g + 3)
                pool.tensor_tensor(ln_c[:, 2:3], ln_c[:, 3:4], small[:, 1:2], ALU.mult).then_inc(rstd_done, 1)

            def affine(t, g):
                pool.wait_ge(normed, g + 2)
                pool.sem_inc(passed, 1)
                pool.tensor_tensor(x_new[:, t, :], x_new[:, t, :], gamma_row[:], ALU.mult).then_inc(new_part, 1)
                pool.wait_ge(new_part, g + 1)
                pool.sem_inc(passed, 1)
                pool.tensor_tensor(x_new[:, t, :], x_new[:, t, :], beta_row[:], ALU.add).then_inc(new_done, 1)

            with pool.Fori(0, B) as b:
                p_low(b * T)
                norm_consts(b * T)
                with pool.Fori(0, T - 1) as t:
                    g = b * T + t
                    p_low(g + 1)
                    affine(t, g)
                    norm_consts(g + 1)
                affine(T - 1, b * T + T - 1)

        @block.scalar
        def _(act):
            def split_hi(dst, ps, full, at, done, bias=0.0):
                act.wait_ge(full, at)
                act.activation(dst, ps, ACT.Identity, bias=bias).then_inc(done, 1)

            def q_evac(g):
                act.wait_ge(q_full, g + 1)
                act.activation(qT_hi[:], ps_q[:, 0:QC * P].rearrange("p (c n) -> p c n", c=QC), ACT.Identity,
                               bias=bqk[:, 0:1] if not folded else 0.0).then_inc(q_hi, 1)

            def exps(g):
                for h in range(2):
                    half = slice(h * T // 2, (h + 1) * T // 2)
                    act.wait_ge(turned, 2 * g + h + 1)
                    act.activation(prob[:, half, :], ps_t[:, h * HALF:(h + 1) * HALF].rearrange("p (t n) -> p t n", n=P),
                                   ACT.Exp).then_inc(exp_done, 1)
                    act.wait_ge(exp_done, 2 * g + h + 1)
                    act.activation(prob_hi[:, half, :], prob[:, half, :], ACT.Copy).then_inc(prob_high, 1)

            def normalise(t, g):
                act.wait_ge(rstd_done, g + 1)
                act.activation(x_new[:, t, :], y[:], ACT.Identity, bias=ln_c[:, 2:3], scale=ln_c[:, 1:2]).then_inc(normed, 1)

            def high(b, n):
                ps = ps_p[n % 2][:]
                if n < XB:
                    split_hi(xT_hi[:, :, 2 * n * P:(2 * n + 2) * P], ps.rearrange("p (c n) -> p c n", c=DC),
                             proj_full, b * NP + n + 1, proj_hi)
                elif n < XB + KB:
                    i = n - XB
                    split_hi(kT_hi[:, 0, i * HALF:(i + 1) * HALF], ps, proj_full, b * NP + n + 1, proj_hi, bias=bqk[:, 1:2])
                else:
                    i = n - XB - KB
                    split_hi(v_hi[:, 2 * i:2 * i + 2, 0:D], ps.rearrange("p (t n) -> p t n", n=D),
                             proj_full, b * NP + n + 1, proj_hi)

            def highs(b, a, z):
                for n in range(a, z):
                    high(b, n)

            act.wait_ge(w_in, 16 * NW)
            act.sem_inc(normed, 1)
            highs(0, 0, XB + KB)
            q_evac(0)
            highs(0, XB + KB, XB + KB + 2)
            q_evac(1)
            highs(0, XB + KB + 2, NP)

            def middle(b):
                exps(b * T)
                act.wait_ge(stored, 16 * T * (b + 1))
                q_evac(b * T + 2)
                with act.Fori(1, T - 2) as t:
                    g = b * T + t
                    exps(g)
                    normalise(t - 1, g - 1)
                    q_evac(g + 2)

            with act.Fori(0, B - 1) as b:
                middle(b)
                g = b * T + T - 2
                exps(g)
                highs(b + 1, 0, 2)
                normalise(T - 3, g - 1)
                highs(b + 1, 2, XB)
                exps(g + 1)
                highs(b + 1, XB, XB + KB)
                q_evac(g + 2)
                normalise(T - 2, g)
                highs(b + 1, XB + KB, XB + KB + 2)
                q_evac(g + 3)
                normalise(T - 1, g + 1)
                highs(b + 1, XB + KB + 2, NP)
            middle(B - 1)
            for t in (T - 2, T - 1):
                exps((B - 1) * T + t)
                normalise(t - 1, (B - 1) * T + t - 1)
            normalise(T - 1, B * T - 1)

        @block.tensor
        def _(pe):
            pe.wait_ge(ready, 5)
            pe.wait_ge(w_in, 16 * NW)
            if folded:
                for j in range(2):
                    l = raw[2 * j].rearrange("p (c n) -> p c n", c=DC)
                    r = raw[2 * j + 1].rearrange("p (c n) -> p c n", c=DC)
                    for m in range(DC):
                        for c in range(DC):
                            mm = pe.matmul(ps_p[j][:, m * D:(m + 1) * D], l[:, c, m * P:(m + 1) * P], r[:, c, :],
                                           start=(c == 0), stop=(c == DC - 1))
                    mm.then_inc(w_ps, 1)
            pe.wait_ge(w_part, 1)

            def three(out, l_hi, l_lo, r_hi, r_lo, n, last):
                first = n == 0
                pe.matmul(out, l_hi, r_hi, start=first, stop=False)
                pe.matmul(out, l_hi, r_lo, start=False, stop=False)
                return pe.matmul(out, l_lo, r_hi, start=False, stop=(n == last))

            def q_tile(t, g):
                pe.wait_ge(q_lo, g + 1)
                for m in range(QC):
                    for c in range(DC):
                        mm = three(ps_q[:, m * P:(m + 1) * P], wq_hi[:, c, m * P:(m + 1) * P], wq_lo[:, c, m * P:(m + 1) * P],
                                   xT_hi[:, c, bass.ts(t, P)], xT_lo[:, c, bass.ts(t, P)], c, DC - 1)
                mm.then_inc(q_full, 1)

            def scores(g):
                pe.wait_ge(q_lo, g + 2)
                for h in range(2):
                    for c in range(KC):
                        mm = three(ps_s[:, h * HALF:(h + 1) * HALF], qT_hi[:, c, :], qT_lo[:, c, :],
                                   kT_hi[:, c, h * HALF:(h + 1) * HALF], kT_lo[:, c, h * HALF:(h + 1) * HALF], c, KC - 1)
                mm.then_inc(score_full, 1)

            def turn(g):
                pe.wait_ge(shifted, g + 1)
                for h in range(2):
                    for k in range(h * T // 2, (h + 1) * T // 2):
                        mm = pe.transpose(ps_t[:, k * P:(k + 1) * P], score[:, k * P:(k + 1) * P], ident[:])
                    mm.then_inc(turned, 1)

            def weigh(g, b):
                pe.wait_ge(out_read, g + 1)
                pe.wait_ge(proj_lo, b * NP + NP + 2)
                for k in range(T):
                    if k == 0:
                        pe.wait_ge(prob_low_1, g + 1)
                    elif k == T // 2 or k == 3 * T // 4:
                        pe.wait_ge(prob_low_2, 2 * g + 4 * k // T - 1)
                    mm = three(ps_o[:, 0:DV], prob_hi[:, k, :], prob_lo[:, k, :], v_hi[:, k, :], v_lo[:, k, :], k, T - 1)
                mm.then_inc(out_full, 1)

            def fill(b, n):
                ps = ps_p[n % 2]
                pe.wait_ge(proj_lo, b * NP + n + 1)
                if n < XB:
                    for c in range(DC):
                        for j in range(2):
                            mm = pe.transpose(ps[:, (2 * c + j) * P:(2 * c + j + 1) * P],
                                              x_tok[:, 2 * n + j, c * P:(c + 1) * P], ident[:])
                elif n < XB + KB:
                    for c in range(DC):
                        s = slice((n - XB) * HALF, (n - XB + 1) * HALF)
                        mm = three(ps[:], wk_hi[:, c, :], wk_lo[:, c, :], xT_hi[:, c, s], xT_lo[:, c, s], c, DC - 1)
                else:
                    for j in range(2):
                        t = 2 * (n - XB - KB) + j
                        s = slice(t * P, (t + 1) * P)
                        for c in range(DC):
                            mm = three(ps[:, j * D:(j + 1) * D], xT_hi[:, c, s], xT_lo[:, c, s],
                                       wv_hi[:, c, :], wv_lo[:, c, :], c, DC - 1)
                mm.then_inc(proj_full, 1)

            def fills(b, a, z):
                for n in range(a, z):
                    fill(b, n)

            def k_and_q(b):
                pe.wait_ge(proj_lo, b * NP + XB + 2)
                fills(b, XB, XB + KB)
                q_tile(0, b * T)

            def first_scores_and_values(b):
                pe.wait_ge(proj_lo, b * NP + XB + KB + 2)
                scores(b * T)
                fills(b, XB + KB, XB + KB + 2)
                q_tile(1, b * T + 1)
                fills(b, XB + KB + 2, NP)

            def middle(b):
                with pe.Fori(0, T - 2) as t:
                    g = b * T + t
                    turn(g)
                    scores(g + 1)
                    q_tile(t + 2, g + 2)
                    weigh(g, b)

            pe.wait_ge(x_loaded, 16)
            fills(0, 0, XB)
            k_and_q(0)
            first_scores_and_values(0)
            with pe.Fori(0, B - 1) as b:
                middle(b)
                g = b * T + T - 2
                turn(g)
                scores(g + 1)
                pe.wait_ge(x_loaded, (b + 2) * 16)
                fills(b + 1, 0, 2)
                weigh(g, b)
                fills(b + 1, 2, XB)
                turn(g + 1)
                k_and_q(b + 1)
                weigh(g + 1, b)
                first_scores_and_values(b + 1)
            middle(B - 1)
            g = B * T - 2
            turn(g)
            scores(g + 1)
            weigh(g, B - 1)
            turn(g + 1)
            weigh(g + 1, B - 1)

        @block.vector
        def _(dve):
            dve.memset(v_hi[:, :, D:D + 1].bitcast(F32), 1.0).then_inc(ones_made, 1)
            dve.memset(v_hi[:, :, D + 1:DV].bitcast(F32), 0.0).then_inc(ones_made, 1)
            dve.memset(v_lo[:, :, D:DV].bitcast(F32), 0.0).then_inc(ones_made, 1)
            dve.sem_inc(proj_lo, 2)
            dve.sem_inc(q_lo, 1)
            dve.sem_inc(out_read, 1)
            dve.sem_inc(bias_used, 1)
            dve.wait_ge(w_in, 16 * NW)
            k = 0
            if folded:
                for j in range(2):
                    dve.wait_ge(w_ps, j + 1)
                    dve.tensor_scalar(w_fold[:, j, :, :], ps_p[j][:].rearrange("p (c n) -> p c n", c=DC),
                                      score_scale if j == 0 else 1.0, None, ALU.mult).then_inc(w_step, 1)
                    k += 1
                dve.wait_ge(w_step, k)
                pairs = [(w_fold[:, 0, :, :], wq_hi, wq_lo), (w_fold[:, 1, :, :], wv_hi, wv_lo)]
            else:
                r = [raw[i][:, 0:DC * n].rearrange("p (c n) -> p c n", c=DC) for i, n in ((0, P), (1, P), (2, D))]
                dve.tensor_scalar(r[0], r[0], score_scale, None, ALU.mult).then_inc(w_step, 1)
                dve.tensor_scalar(bqk[:, 0:1], bqk[:, 0:1], score_scale, None, ALU.mult).then_inc(w_step, 1)
                k += 2
                dve.wait_ge(w_step, k)
                pairs = [(r[0], wq_hi, wq_lo), (r[1], wk_hi, wk_lo), (r[2], wv_hi, wv_lo)]
            for full, hi, lo in pairs:
                dve.tensor_copy(hi[:], full).then_inc(w_step, 1)
                k += 1
                dve.wait_ge(w_step, k)
                mm = dve.tensor_tensor(lo[:], full, hi[:].bitcast(F32), ALU.subtract)
            dve.wait_ge(ones_made, 3)
            mm.then_inc(w_part, 1)
            dve.wait_ge(w_part, 1)

            def split_lo(dst, ps, hi, at, bias=None):
                dve.wait_ge(proj_hi, at)
                if bias is None:
                    dve.tensor_tensor(dst, ps, hi.bitcast(F32), ALU.subtract).then_inc(proj_lo, 1)
                else:
                    dve.scalar_tensor_tensor(dst, ps, bias, hi.bitcast(F32), ALU.add, ALU.subtract).then_inc(proj_lo, 1)

            def q_low(g):
                dve.wait_ge(q_hi, g + 1)
                src = ps_q[:, 0:QC * P].rearrange("p (c n) -> p c n", c=QC)
                if folded:
                    dve.tensor_tensor(qT_lo[:], src, qT_hi[:].bitcast(F32), ALU.subtract).then_inc(q_lo, 1)
                else:
                    dve.scalar_tensor_tensor(qT_lo[:, 0, :], ps_q[:, 0:P], bqk[:, 0:1], qT_hi[:, 0, :].bitcast(F32),
                                             ALU.add, ALU.subtract).then_inc(q_lo, 1)

            def make_bias(t, g):
                dve.wait_ge(adj_in, 16 * (g + 1))
                dve.tensor_scalar(mask_bias[:], adj_sb[:, t, :], 0.0, -BIG, ALU.is_equal, ALU.mult).then_inc(bias_made, 1)

            def shift(g):
                dve.wait_ge(bias_made, g + 1)
                dve.wait_ge(score_full, g + 1)
                dve.sem_inc(passed, 1)
                dve.tensor_tensor_reduce(score[:], ps_s[:], mask_bias[:], 1.0, -3.0e38, ALU.add, ALU.max,
                                         row_max[:]).then_inc(bias_used, 1)
                dve.wait_ge(bias_used, g + 2)
                dve.tensor_scalar(score[:], score[:], row_max[:], None, ALU.subtract).then_inc(shifted, 1)

            def flag(g):
                dve.tensor_scalar(has_key[:], row_max[:], -0.1 * BIG, None, ALU.is_gt).then_inc(has_key_made, 1)

            def p_low(g):
                half = slice(0, T // 2)
                dve.wait_ge(prob_high, 2 * g + 1)
                dve.tensor_tensor(prob_lo[:, half, :], prob[:, half, :], prob_hi[:, half, :].bitcast(F32),
                                  ALU.subtract).then_inc(prob_low_1, 1)

            def finish(t, g):
                dve.wait_ge(out_full, g + 1)
                dve.reciprocal(inv[:, 0:1], ps_o[:, D:D + 1]).then_inc(inv_made, 1)
                if folded:
                    dve.wait_ge(inv_made, g + 1)
                    iv = inv[:, 0:1]
                else:
                    dve.wait_ge(inv_made, 2 * g + 1)
                    dve.wait_ge(has_key_made, g + 1)
                    dve.tensor_tensor(inv[:, 1:2], inv[:, 0:1], has_key[:], ALU.mult).then_inc(inv_made, 1)
                    dve.wait_ge(inv_made, 2 * g + 2)
                    iv = inv[:, 1:2]
                dve.wait_ge(normed, g + 1)
                dve.scalar_tensor_tensor(y[:], ps_o[:, 0:D], iv, x_res[:, t, :], ALU.mult, ALU.add).then_inc(out_read, 1)
                dve.wait_ge(out_read, g + 2)
                dve.bn_stats(stats[:], y[:]).then_inc(stats_part, 1)
                dve.wait_ge(stats_part, g + 1)
                dve.sem_inc(passed, 1)
                dve.bn_aggr(mean_var[:], stats[:]).then_inc(stats_done, 1)

            def low(b, n):
                ps = ps_p[n % 2][:]
                if n < XB:
                    s = slice(2 * n * P, (2 * n + 2) * P)
                    split_lo(xT_lo[:, :, s], ps.rearrange("p (c n) -> p c n", c=DC), xT_hi[:, :, s], b * NP + n + 1)
                elif n < XB + KB:
                    s = slice((n - XB) * HALF, (n - XB + 1) * HALF)
                    split_lo(kT_lo[:, 0, s], ps, kT_hi[:, 0, s], b * NP + n + 1, bias=bqk[:, 1:2])
                else:
                    i = n - XB - KB
                    s = slice(2 * i, 2 * i + 2)
                    split_lo(v_lo[:, s, 0:D], ps.rearrange("p (t n) -> p t n", n=D), v_hi[:, s, 0:D], b * NP + n + 1)

            def lows(b, a, z):
                for n in range(a, z):
                    low(b, n)

            def first_shift_and_values(b):
                make_bias(0, b * T)
                shift(b * T)
                lows(b, XB + KB, XB + KB + 2)
                q_low(b * T + 1)
                lows(b, XB + KB + 2, NP)

            def tile(t, g, with_q):
                p_low(g)
                if not folded:
                    flag(g)
                make_bias(t + 1, g + 1)
                shift(g + 1)
                if with_q:
                    q_low(g + 2)

            def middle(b):
                dve.wait_ge(res_in, (b + 1) * 16)
                if folded:
                    dve.tensor_tensor(x_res[:], x_res[:], bo_row[:].unsqueeze(1).to_broadcast([P, T, D]), ALU.add)\
                       .then_inc(res_biased, 1)
                    dve.wait_ge(res_biased, b + 1)
                dve.sem_inc(passed, 1)
                tile(0, b * T, True)
                with dve.Fori(1, T - 2) as t:
                    finish(t - 1, b * T + t - 1)
                    tile(t, b * T + t, True)
                finish(T - 3, b * T + T - 3)
                tile(T - 2, b * T + T - 2, False)

            def last_tile(g):
                p_low(g)
                if not folded:
                    flag(g)

            lows(0, 0, XB + KB)
            q_low(0)
            first_shift_and_values(0)
            with dve.Fori(0, B - 1) as b:
                middle(b)
                g = b * T + T - 2
                lows(b + 1, 0, XB)
                finish(T - 2, g)
                last_tile(g + 1)
                lows(b + 1, XB, XB + KB)
                q_low(g + 2)
                finish(T - 1, g + 1)
                first_shift_and_values(b + 1)
            middle(B - 1)
            finish(T - 2, B * T - 2)
            last_tile(B * T - 1)
            finish(T - 1, B * T - 1)


TINY = 1.0e-13


def direction_layer(nc, tag, x_in, x_out, adjT, w, bias, gamma, beta, B, N):
    T = N // P
    XB, YB = T // 2, T
    NP = XB + YB
    RING = 4
    HALF = 512
    W2 = 2 * D

    with nc.cleanup_on_exit(), ExitStack() as ctx:
        def sb(name, shape, dt=F32):
            return ctx.enter_context(nc.sbuf_tensor(f"{tag}_{name}", shape, dt))

        def pb(name, shape):
            return ctx.enter_context(nc.psum_tensor(f"{tag}_{name}", shape, F32))

        def sem(name):
            return nc.alloc_semaphore(name=f"{tag}_{name}")

        w_raw = sb("w_raw", [P, DC, W2])
        w_hi, w_lo = sb("w_hi", [P, DC, W2], F32R), sb("w_lo", [P, DC, W2], F32R)
        bias_row, gamma_row, beta_row = sb("bias_row", [P, D]), sb("gamma_row", [P, D]), sb("beta_row", [P, D])
        ident, small = sb("ident", [P, P]), sb("small", [P, 3])
        small2 = sb("small2", [P, 2])
        x_tok, x_res, x_new = sb("x_tok", [P, T, D]), sb("x_res", [P, T, D]), sb("x_new", [P, T, D])
        xT_hi, xT_lo = sb("xT_hi", [P, DC, N], F32R), sb("xT_lo", [P, DC, N], F32R)
        y_hi, y_lo = sb("y_hi", [P, T, 2, DV], F32R), sb("y_lo", [P, T, 2, DV], F32R)
        adj_sb = [sb(f"adj_sb{j}", [P, T, P], I32) for j in range(2)]
        off = [sb(f"off{j}", [P, T, P]) for j in range(2)]
        kind1 = [sb(f"kind1_{j}", [P, T, P], F32R) for j in range(2)]
        kind2 = [sb(f"kind2_{j}", [P, T, P], F32R) for j in range(2)]
        cnt, inv = sb("cnt", [P, 2, 1]), sb("inv", [P, 2, 1])
        mean1, mean12, y = sb("mean1", [P, D]), sb("mean12", [P, D]), sb("y", [P, D])
        stats, mean_var, ln_c = sb("stats", [P, 6]), sb("mean_var", [P, 2]), sb("ln_c", [P, 4])

        ps_p = [pb(f"ps_p{i}", [P, HALF]) for i in range(RING)]
        ps_o = [pb(f"ps_o{i}", [P, 2, HALF]) for i in range(2)]

        w_in, w_part, w_split, ready, ones_in = sem("w_in"), sem("w_part"), sem("w_split"), sem("ready"), sem("ones_in")
        x_loaded, res_in, stored = sem("x_loaded"), sem("res_in"), sem("stored")
        adj_in = [sem(f"adj_in{j}") for j in range(2)]
        proj_full, proj_hi, proj_lo = sem("proj_full"), sem("proj_hi"), sem("proj_lo")
        kind1_made, kind2_part, kind2_made = sem("kind1_made"), sem("kind2_part"), sem("kind2_made")
        out_full, out_read = sem("out_full"), sem("out_read")
        fin_part, stats_done = sem("fin_part"), sem("stats_done")
        rstd_part, rstd_done, normed, new_part, new_done = (sem("rstd_part"), sem("rstd_done"), sem("normed"),
                                                            sem("new_part"), sem("new_done"))
        passed, small2_in = sem("passed"), sem("small2_in")

        x_in_t = x_in.rearrange("b (t p) d -> b p t d", p=P)
        x_out_t = x_out.rearrange("b (t p) d -> b p t d", p=P)
        block = ctx.enter_context(nc.Block())
        H = T // 2

        @block.sync
        def _(sp):
            sp.dma_start(w_raw[:, :, 0:D], w[0:D, :].rearrange("(c p) n -> p c n", p=P)).then_inc(w_in, 16)
            sp.dma_start(w_raw[:, :, D:W2], w[D:W2, :].rearrange("(c p) n -> p c n", p=P)).then_inc(w_in, 16)
            for dst, src in ((bias_row, bias), (gamma_row, gamma), (beta_row, beta)):
                sp.dma_start(dst[:], src.partition_broadcast(P)).then_inc(w_in, 16)

            def load_tokens(b):
                sp.dma_start(x_tok[:], x_in_t[b]).then_inc(x_loaded, 16)

            def load_residual(b):
                sp.dma_start(x_res[:], x_in_t[b]).then_inc(res_in, 16)

            def load_adj(b, t, j):
                sp.dma_start(adj_sb[j][:], adjT[b, t]).then_inc(adj_in[j], 16)

            def store_last(b):
                t = T - 1
                sp.wait_ge(new_done, b * T + t + 1)
                sp.dma_start(x_out_t[b][:, t, :], x_new[:, t, :]).then_inc(stored, 16)

            load_tokens(0)
            load_adj(0, 0, 0)
            load_adj(0, 1, 1)
            load_residual(0)
            sp.sem_inc(stored, 16 * T)

            with sp.Fori(0, B - 1) as b:
                sp.wait_ge(proj_full, b * NP + XB)
                load_tokens(b + 1)
                with sp.Fori(0, H - 1) as i:
                    for j in range(2):
                        sp.wait_ge(kind1_made, b * T + 2 * i + j + 1)
                        sp.wait_ge(kind2_made, b * T + 2 * i + j + 1)
                        load_adj(b, 2 * i + 2 + j, j)
                for j in range(2):
                    sp.wait_ge(kind1_made, b * T + T - 1 + j)
                    sp.wait_ge(kind2_made, b * T + T - 1 + j)
                    load_adj(b + 1, j, j)
                sp.wait_ge(out_read, (b + 1) * T + 2)
                load_residual(b + 1)
                store_last(b)
            b = B - 1
            with sp.Fori(0, H - 1) as i:
                for j in range(2):
                    sp.wait_ge(kind1_made, b * T + 2 * i + j + 1)
                    sp.wait_ge(kind2_made, b * T + 2 * i + j + 1)
                    load_adj(b, 2 * i + 2 + j, j)
            store_last(b)
            sp.wait_ge(stored, 16 * T * (B + 1))

        @block.gpsimd
        def _(pool):
            pool.memset(ident[:], 0.0).then_inc(ready, 1)
            pool.memset(small[:, 0:1], -0.5).then_inc(ready, 1)
            pool.memset(small[:, 1:2], -1.0).then_inc(ready, 1)
            pool.memset(small[:, 2:3], EPS).then_inc(ready, 1)
            pool.wait_ge(ready, 4)
            pool.affine_select(out=ident[:], in_=ident[:], compare_op=ALU.not_equal, fill=1.0,
                               base=0, pattern=[[-1, P]], channel_multiplier=1).then_inc(ready, 1)
            pool.wait_ge(w_in, 16 * 5)

            def norm_consts(g):
                pool.wait_ge(stats_done, g + 1)
                pool.tensor_tensor(ln_c[:, 0:1], mean_var[:, 1:2], small[:, 2:3], ALU.add).then_inc(rstd_part, 1)
                pool.wait_ge(rstd_part, 3 * g + 1)
                pool.tensor_tensor(ln_c[:, 1:2], ln_c[:, 0:1], small[:, 0:1], ALU.pow).then_inc(rstd_part, 1)
                pool.wait_ge(rstd_part, 3 * g + 2)
                pool.tensor_tensor(ln_c[:, 3:4], mean_var[:, 0:1], ln_c[:, 1:2], ALU.mult).then_inc(rstd_part, 1)
                pool.wait_ge(rstd_part, 3 * g + 3)
                pool.tensor_tensor(ln_c[:, 2:3], ln_c[:, 3:4], small[:, 1:2], ALU.mult).then_inc(rstd_done, 1)

            def affine(t, g):
                pool.wait_ge(normed, g + 2)
                pool.sem_inc(passed, 1)
                pool.tensor_tensor(x_new[:, t, :], x_new[:, t, :], gamma_row[:], ALU.mult).then_inc(new_part, 1)
                pool.wait_ge(new_part, g + 1)
                pool.sem_inc(passed, 1)
                pool.tensor_tensor(x_new[:, t, :], x_new[:, t, :], beta_row[:], ALU.add).then_inc(new_done, 1)

            with pool.Fori(0, B) as b:
                with pool.Fori(0, T) as t:
                    g = b * T + t
                    norm_consts(g)
                    affine(t, g)

        @block.scalar
        def _(act):
            def split_hi(dst, ps, at):
                act.wait_ge(proj_full, at)
                act.activation(dst, ps, ACT.Identity).then_inc(proj_hi, 1)

            def make_kind2(g, j, seen):
                act.wait_ge(adj_in[j], 16 * seen)
                act.activation(off[j][:], adj_sb[j][:], ACT.Abs, bias=small2[:, 0:1]).then_inc(kind2_part, 1)
                act.wait_ge(kind2_part, g + 1)
                act.wait_ge(out_full, g + 1)
                act.activation(kind2[j][:], off[j][:], ACT.Relu, bias=small2[:, 1:2], scale=-1.0).then_inc(kind2_made, 1)

            def normalise(t, g):
                act.wait_ge(rstd_done, g + 1)
                act.activation(x_new[:, t, :], y[:], ACT.Identity, bias=ln_c[:, 2:3], scale=ln_c[:, 1:2]).then_inc(normed, 1)

            def store(b, t, g):
                act.wait_ge(new_done, g + 1)
                act.dma_start(x_out_t[b][:, t, :], x_new[:, t, :]).then_inc(stored, 16)

            def highs(b, a, z):
                for n in range(a, z):
                    ps = ps_p[n % RING][:]
                    if n < XB:
                        split_hi(xT_hi[:, :, 2 * n * P:(2 * n + 2) * P], ps.rearrange("p (c n) -> p c n", c=DC),
                                 b * NP + n + 1)
                    else:
                        split_hi(y_hi[:, n - XB, :, 0:D], ps.rearrange("p (j n) -> p j n", j=2), b * NP + n + 1)

            def middle(b):
                act.wait_ge(stored, 16 * T * (b + 1))
                act.sem_inc(passed, 1)
                g = b * T
                make_kind2(g + 2, 0, b * H + 2)
                normalise(0, g)
                make_kind2(g + 3, 1, b * H + 2)
                normalise(1, g + 1)
                store(b, 0, g)
                with act.Fori(1, H - 1) as i:
                    for j in range(2):
                        g = b * T + 2 * i + j
                        make_kind2(g + 2, j, b * H + i + 2)
                        normalise(2 * i + j, g)
                        store(b, 2 * i + j - 1, g - 1)

            act.sem_inc(normed, 1)
            act.wait_ge(small2_in, 2)
            highs(0, 0, NP)
            make_kind2(0, 0, 1)
            make_kind2(1, 1, 1)
            with act.Fori(0, B - 1) as b:
                middle(b)
                g = b * T + T - 2
                highs(b + 1, 0, XB)
                normalise(T - 2, g)
                make_kind2(g + 2, 0, (b + 1) * H + 1)
                store(b, T - 3, g - 1)
                highs(b + 1, XB, XB + 5)
                normalise(T - 1, g + 1)
                store(b, T - 2, g)
                highs(b + 1, XB + 5, NP)
                make_kind2(g + 3, 1, (b + 1) * H + 1)
            middle(B - 1)
            for t in (T - 2, T - 1):
                normalise(t, (B - 1) * T + t)
                store(B - 1, t - 1, (B - 1) * T + t - 1)

        @block.tensor
        def _(pe):
            pe.wait_ge(ready, 5)
            pe.wait_ge(w_split, 1)
            pe.wait_ge(ones_in, 3)
            pe.sem_inc(out_full, 2)

            def three(out, l_hi, l_lo, r_hi, r_lo, n, last):
                pe.matmul(out, l_hi, r_hi, start=(n == 0), stop=False)
                pe.matmul(out, l_hi, r_lo, start=False, stop=False)
                return pe.matmul(out, l_lo, r_hi, start=False, stop=(n == last))

            def aggregate(g, j):
                pe.wait_ge(kind1_made, g + 1)
                pe.wait_ge(out_read, g + 1)
                for d, kind in ((0, kind1), (1, kind2)):
                    if d == 1:
                        pe.wait_ge(kind2_made, g + 1)
                    for k in range(T):
                        pe.matmul(ps_o[j][:, d, 0:DV], kind[j][:, k, :], y_hi[:, k, d, :], start=(k == 0), stop=False)
                        mm = pe.matmul(ps_o[j][:, d, 0:DV], kind[j][:, k, :], y_lo[:, k, d, :], start=False,
                                       stop=(k == T - 1))
                mm.then_inc(out_full, 1)

            def fills(b, a, z):
                for n in range(a, z):
                    ps = ps_p[n % RING]
                    pe.wait_ge(proj_lo, b * NP + n + 1)
                    if n < XB:
                        for c in range(DC):
                            for j in range(2):
                                mm = pe.transpose(ps[:, (2 * c + j) * P:(2 * c + j + 1) * P],
                                                  x_tok[:, 2 * n + j, c * P:(c + 1) * P], ident[:])
                    else:
                        pe.wait_ge(proj_lo, b * NP + (n - XB) // 2 + 1 + RING)
                        for c in range(DC):
                            s = slice((n - XB) * P, (n - XB + 1) * P)
                            mm = three(ps[:], xT_hi[:, c, s], xT_lo[:, c, s], w_hi[:, c, :], w_lo[:, c, :], c, DC - 1)
                    mm.then_inc(proj_full, 1)

            def middle(b, n):
                pe.wait_ge(proj_lo, (b + 1) * NP + RING)
                pe.sem_inc(passed, 1)
                with pe.Fori(0, n) as i:
                    for j in range(2):
                        aggregate(b * T + 2 * i + j, j)

            pe.wait_ge(x_loaded, 16)
            fills(0, 0, NP)
            with pe.Fori(0, B - 1) as b:
                middle(b, H - 1)
                aggregate(b * T + T - 2, 0)
                pe.wait_ge(x_loaded, (b + 2) * 16)
                fills(b + 1, 0, XB)
                aggregate(b * T + T - 1, 1)
                fills(b + 1, XB, NP)
            middle(B - 1, H)

        @block.vector
        def _(dve):
            dve.memset(small2[:, 0:1], -2.0).then_inc(small2_in, 1)
            dve.memset(small2[:, 1:2], 1.0).then_inc(small2_in, 1)
            dve.memset(y_hi[:, :, :, D:D + 1].bitcast(F32), 1.0).then_inc(ones_in, 1)
            dve.memset(y_hi[:, :, :, D + 1:DV].bitcast(F32), 0.0).then_inc(ones_in, 1)
            dve.memset(y_lo[:, :, :, D:DV].bitcast(F32), 0.0).then_inc(ones_in, 1)
            dve.sem_inc(proj_lo, RING)
            dve.sem_inc(out_read, 2)
            dve.wait_ge(w_in, 16 * 5)
            dve.tensor_copy(w_hi[:], w_raw[:]).then_inc(w_part, 1)
            dve.wait_ge(w_part, 1)
            dve.tensor_tensor(w_lo[:], w_raw[:], w_hi[:].bitcast(F32), ALU.subtract).then_inc(w_split, 1)

            def split_lo(dst, ps, hi, at):
                dve.wait_ge(proj_hi, at)
                dve.tensor_tensor(dst, ps, hi.bitcast(F32), ALU.subtract).then_inc(proj_lo, 1)

            def make_kind1(g, j, seen):
                dve.wait_ge(adj_in[j], 16 * seen)
                dve.wait_ge(out_full, g + 1)
                dve.tensor_scalar(kind1[j][:], adj_sb[j][:], 1.0, None, ALU.is_equal).then_inc(kind1_made, 1)

            def finish(t, g, j):
                dve.wait_ge(out_full, g + 3)
                dve.tensor_scalar(cnt[:], ps_o[j][:, :, D:D + 1], TINY, None, ALU.add).then_inc(fin_part, 1)
                dve.wait_ge(fin_part, 5 * g + 1)
                dve.reciprocal(inv[:], cnt[:]).then_inc(fin_part, 1)
                dve.wait_ge(fin_part, 5 * g + 2)
                dve.scalar_tensor_tensor(mean1[:], ps_o[j][:, 0, 0:D], inv[:, 0, :], bias_row[:], ALU.mult, ALU.add)\
                   .then_inc(fin_part, 1)
                dve.wait_ge(fin_part, 5 * g + 3)
                dve.scalar_tensor_tensor(mean12[:], ps_o[j][:, 1, 0:D], inv[:, 1, :], mean1[:], ALU.mult, ALU.add)\
                   .then_inc(fin_part, 1)
                dve.wait_ge(fin_part, 5 * g + 4)
                dve.wait_ge(normed, g + 1)
                dve.scalar_tensor_tensor(y[:], mean12[:], 0.0, x_res[:, t, :], ALU.max, ALU.add).then_inc(out_read, 1)
                dve.wait_ge(out_read, g + 3)
                dve.bn_stats(stats[:], y[:]).then_inc(fin_part, 1)
                dve.wait_ge(fin_part, 5 * g + 5)
                dve.sem_inc(passed, 1)
                dve.bn_aggr(mean_var[:], stats[:]).then_inc(stats_done, 1)

            def lows(b, a, z):
                for n in range(a, z):
                    ps = ps_p[n % RING][:]
                    if n < XB:
                        s = slice(2 * n * P, (2 * n + 2) * P)
                        split_lo(xT_lo[:, :, s], ps.rearrange("p (c n) -> p c n", c=DC), xT_hi[:, :, s], b * NP + n + 1)
                    else:
                        t = n - XB
                        split_lo(y_lo[:, t, :, 0:D], ps.rearrange("p (j n) -> p j n", j=2), y_hi[:, t, :, 0:D],
                                 b * NP + n + 1)

            def middle(b):
                dve.wait_ge(res_in, (b + 1) * 16)
                dve.sem_inc(passed, 1)
                with dve.Fori(0, H - 1) as i:
                    for j in range(2):
                        g = b * T + 2 * i + j
                        make_kind1(g + 2, j, b * H + i + 2)
                        finish(2 * i + j, g, j)

            lows(0, 0, NP)
            make_kind1(0, 0, 1)
            make_kind1(1, 1, 1)
            with dve.Fori(0, B - 1) as b:
                middle(b)
                g = b * T + T - 2
                finish(T - 2, g, 0)
                lows(b + 1, 0, XB)
                make_kind1(g + 2, 0, (b + 1) * H + 1)
                lows(b + 1, XB, XB + 2)
                finish(T - 1, g + 1, 1)
                lows(b + 1, XB + 2, NP)
                make_kind1(g + 3, 1, (b + 1) * H + 1)
            middle(B - 1)
            for t in (T - 2, T - 1):
                finish(t, (B - 1) * T + t, t % 2)


H = 8
HD = D // H
HV = HD + 1


def heads_project(nc, tag, x_in, q_parts, k_parts, v_out, g1, b1, wq, bq, wk, bk, wv, bv, B, N):
    T = N // P
    HALF = 512
    RING = 8
    X, KQ, V = T // 2, DC * N // HALF, T // 2
    NF = X + 2 * KQ + V
    NH = X + 2 * KQ
    SCALE = float(HD) ** -0.5

    with nc.cleanup_on_exit(), ExitStack() as ctx:
        def sb(name, shape, dt=F32):
            return ctx.enter_context(nc.sbuf_tensor(f"{tag}_{name}", shape, dt))

        def sem(name):
            return nc.alloc_semaphore(name=f"{tag}_{name}")

        w_raw = [sb(f"w_raw{i}", [P, DC, D]) for i in range(3)]
        w_hi = [sb(f"w_hi{i}", [P, DC, D], F32R) for i in range(3)]
        w_lo = [sb(f"w_lo{i}", [P, DC, D], F32R) for i in range(3)]
        col = sb("col", [P, 4, DC])
        bcol = sb("bcol", [P, 2, DC])
        b1_wide = sb("b1_wide", [P, DC, P])
        bv_row = sb("bv_row", [P, D])
        ident, small = sb("ident", [P, P]), sb("small", [P, 3])
        x_tok = [sb(f"x_tok{j}", [P, T, D]) for j in range(2)]
        zT_hi = [sb(f"zT_hi{j}", [P, DC, N], F32R) for j in range(2)]
        zT_lo = [sb(f"zT_lo{j}", [P, DC, N], F32R) for j in range(2)]
        kT = [[sb(f"kT_{part}{j}", [P, DC, N], F32R) for part in ("hi", "lo")] for j in range(2)]
        qT = [[sb(f"qT_{part}{j}", [P, DC, N], F32R) for part in ("hi", "lo")] for j in range(2)]
        v = [sb(f"v{j}", [P, T, H, HV]) for j in range(2)]
        stats, mean_var, ln_c = sb("stats", [P, T, 6]), sb("mean_var", [P, T, 2]), sb("ln_c", [P, 4, T])
        ring = [ctx.enter_context(nc.psum_tensor(f"{tag}_ring{i}", [P, HALF], F32)) for i in range(RING)]

        names = ("w_in ready w_part b_ps w_scaled w_high w_split full high low stat_part stats_done rstd_part rstd_done z_done passed")
        (w_in, ready, w_part, b_ps, w_scaled, w_high, w_split, full, high, low, stat_part, stats_done, rstd_part, rstd_done, z_done,
         passed) = (sem(n) for n in names.split())
        x_loaded = [sem(f"x_loaded{j}") for j in range(2)]
        stored = [sem(f"stored{j}") for j in range(2)]

        x_in_t = x_in.rearrange("b (t p) d -> b p t d", p=P)
        q_t = q_parts.rearrange("(b t) s (c p) n -> b s c p t n", t=T, p=P)
        k_t = k_parts.rearrange("b s (c p) n -> b s p c n", p=P)
        NW = 3 + 4 + 1
        NS = 2 * DC + 2 + 1
        block = ctx.enter_context(nc.Block())

        def fill(b, n, has_x):
            return X + NF * b + n - (0 if has_x else X)

        def bank(n, has_x):
            return ring[(X + n - (0 if has_x else X)) % RING]

        def split(b, n, has_x):
            return X + NH * b + n - (0 if has_x else X)

        @block.sync
        def _(sp):
            for i, c in enumerate((g1, b1, bq, bk)):
                sp.dma_start(col[:, i, :].unsqueeze(2), c.rearrange("(c p o) -> p c o", p=P, o=1),
                             allow_slow_non_contiguous=True).then_inc(w_in, 16)
            sp.dma_start(x_tok[0][:], x_in_t[0]).then_inc(x_loaded[0], 16)
            for i, w in enumerate((wq, wk, wv)):
                sp.dma_start(w_raw[i][:], w.rearrange("(c p) n -> p c n", p=P)).then_inc(w_in, 16)
            sp.dma_start(bv_row[:], bv.partition_broadcast(P)).then_inc(w_in, 16)
            sp.dma_start(x_tok[1][:], x_in_t[1]).then_inc(x_loaded[1], 16)
            for j in range(2):
                sp.sem_inc(stored[j], 16 * NS)

            def batch(b, j, has_x, has_load):
                if has_load:
                    sp.wait_ge(full, fill(b, X - 1, True) + 1)
                    sp.dma_start(x_tok[1 - j][:], x_in_t[b + 3]).then_inc(x_loaded[1 - j], 16)
                sp.wait_ge(low, fill(b, X + KQ - 1, has_x) + 1 + RING)
                for s in range(2):
                    sp.dma_start(k_t[b, s], kT[j][s][:].bitcast(F32)).then_inc(stored[j], 16)
                sp.wait_ge(low, fill(b, X + 2 * KQ - 1, has_x) + 1 + RING)
                for s in range(2):
                    for c in range(DC):
                        sp.dma_start(q_t[b, s, c], qT[j][s][:, c, :].rearrange("p (t n) -> p t n", n=P).bitcast(F32))\
                          .then_inc(stored[j], 16)
                sp.wait_ge(low, fill(b, NF - 1, has_x) + 1 + RING)
                sp.dma_start(v_out[b], v[j][:].rearrange("p t h d -> p (t h d)")).then_inc(stored[j], 16)

            sp.wait_ge(full, X)
            sp.dma_start(x_tok[0][:], x_in_t[2]).then_inc(x_loaded[0], 16)
            batch(0, 0, True, True)
            with sp.Fori(0, (B - 4) // 2) as i:
                for j in range(2):
                    batch(2 * i + 1 + j, 1 - j, True, True)
            for b in range(B - 3, B):
                batch(b, b % 2, b < B - 1, False)
            for j in range(2):
                sp.wait_ge(stored[j], 16 * NS * (B // 2 + 1))

        @block.gpsimd
        def _(pool):
            pool.memset(ident[:], 0.0).then_inc(ready, 1)
            pool.memset(small[:, 0:1], -0.5).then_inc(ready, 1)
            pool.memset(small[:, 1:2], -1.0).then_inc(ready, 1)
            pool.memset(small[:, 2:3], EPS).then_inc(ready, 1)
            pool.wait_ge(ready, 4)
            pool.affine_select(out=ident[:], in_=ident[:], compare_op=ALU.not_equal, fill=1.0,
                               base=0, pattern=[[-1, P]], channel_multiplier=1).then_inc(ready, 1)
            half, minus, eps = (small[:, k:k + 1].to_broadcast([P, T]) for k in range(3))

            def norm_consts(b):
                pool.wait_ge(stats_done, (b + 1) * T)
                pool.tensor_tensor(ln_c[:, 0, :], mean_var[:, :, 1], eps, ALU.add).then_inc(rstd_part, 1)
                pool.wait_ge(rstd_part, 3 * b + 1)
                pool.tensor_tensor(ln_c[:, 1, :], ln_c[:, 0, :], half, ALU.pow).then_inc(rstd_part, 1)
                pool.wait_ge(rstd_part, 3 * b + 2)
                pool.tensor_tensor(ln_c[:, 3, :], mean_var[:, :, 0], ln_c[:, 1, :], ALU.mult).then_inc(rstd_part, 1)
                pool.wait_ge(rstd_part, 3 * b + 3)
                pool.tensor_tensor(ln_c[:, 2, :], ln_c[:, 3, :], minus, ALU.mult).then_inc(rstd_done, 1)

            norm_consts(0)
            with pool.Fori(1, B) as b:
                pool.wait_ge(z_done, b * T)
                norm_consts(b)

        @block.scalar
        def _(act):
            def normalise(b, j):
                act.wait_ge(rstd_done, b + 1)
                act.sem_inc(passed, 1)
                for t in range(T):
                    act.activation(x_tok[j][:, t, :], x_tok[j][:, t, :], ACT.Identity, bias=ln_c[:, 2, t:t + 1],
                                   scale=ln_c[:, 1, t:t + 1]).then_inc(z_done, 1)

            def high_x(dst, ps, i, at):
                act.wait_ge(full, at + 1)
                act.activation(dst[:, :, 2 * i * P:(2 * i + 2) * P], ps[:].rearrange("p (c n) -> p c n", c=DC),
                               ACT.Identity).then_inc(high, 1)

            def batch(b, j, has_x, has_load, seen):
                if has_x:
                    for n in range(X):
                        high_x(zT_hi[1 - j], bank(n, True), n, fill(b, n, True))
                act.wait_ge(stored[j], 16 * NS * seen)
                for which, dst in ((1, kT[j][0]), (0, qT[j][0])):
                    for k in range(KQ):
                        n = X + (1 - which) * KQ + k
                        m, s = k // 2, slice(k % 2 * HALF, (k % 2 + 1) * HALF)
                        act.wait_ge(full, fill(b, n, has_x) + 1)
                        act.activation(dst[:, m, s], bank(n, has_x)[:], ACT.Identity, bias=bcol[:, which, m:m + 1])\
                           .then_inc(high, 1)
                    if which == 1 and has_load:
                        normalise(b + 2, j)

            normalise(0, 0)
            for n in range(X):
                high_x(zT_hi[0], ring[n], n, n)
            normalise(1, 1)
            act.wait_ge(w_scaled, 1)
            for i in range(3):
                act.activation(w_hi[i][:], w_raw[i][:], ACT.Identity).then_inc(w_high, 1)
            with act.Fori(0, (B - 2) // 2) as i:
                for j in range(2):
                    batch(2 * i + j, j, True, True, i + 1)
            batch(B - 2, 0, True, False, B // 2)
            batch(B - 1, 1, False, False, B // 2)

        @block.tensor
        def _(pe):
            def three(out, l_hi, l_lo, r_hi, r_lo, n, last):
                pe.matmul(out, l_hi, r_hi, start=(n == 0), stop=False)
                pe.matmul(out, l_hi, r_lo, start=False, stop=False)
                return pe.matmul(out, l_lo, r_hi, start=False, stop=(n == last))

            def turn(b, j, at):
                for n in range(X):
                    k, ps = at(n)
                    pe.wait_ge(low, k + 1)
                    pe.wait_ge(z_done, b * T + 2 * n + 2)
                    for c in range(DC):
                        for r in range(2):
                            mm = pe.transpose(ps[:, (2 * c + r) * P:(2 * c + r + 1) * P],
                                              x_tok[j][:, 2 * n + r, c * P:(c + 1) * P], ident[:])
                    mm.then_inc(full, 1)

            def batch(b, j, has_x):
                if has_x:
                    turn(b + 1, 1 - j, lambda n: (fill(b, n, True), bank(n, True)))
                pe.wait_ge(low, NF * b + X + RING)
                for which in (1, 0):
                    for k in range(KQ):
                        n = X + (1 - which) * KQ + k
                        ws, ts = slice(k // 2 * P, (k // 2 + 1) * P), slice(k % 2 * HALF, (k % 2 + 1) * HALF)
                        pe.wait_ge(low, fill(b, n, has_x) + 1)
                        for c in range(DC):
                            mm = three(bank(n, has_x)[:], w_hi[which][:, c, ws], w_lo[which][:, c, ws],
                                       zT_hi[j][:, c, ts], zT_lo[j][:, c, ts], c, DC - 1)
                        mm.then_inc(full, 1)
                for k in range(V):
                    n = X + 2 * KQ + k
                    pe.wait_ge(low, fill(b, n, has_x) + 1)
                    for r in range(2):
                        ts = slice((2 * k + r) * P, (2 * k + r + 1) * P)
                        for c in range(DC):
                            mm = three(bank(n, has_x)[:, r * D:(r + 1) * D], zT_hi[j][:, c, ts], zT_lo[j][:, c, ts],
                                       w_hi[2][:, c, :], w_lo[2][:, c, :], c, DC - 1)
                    mm.then_inc(full, 1)

            pe.wait_ge(ready, 5)
            turn(0, 0, lambda n: (n, ring[n]))
            pe.wait_ge(w_in, 16 * NW)
            for i in range(2):
                for m in range(DC):
                    for c in range(DC):
                        mm = pe.matmul(ring[RING - 2][:, i * DC + m:i * DC + m + 1], w_raw[i][:, c, m * P:(m + 1) * P],
                                       col[:, 1, c:c + 1], start=(c == 0), stop=(c == DC - 1))
            mm.then_inc(b_ps, 1)
            pe.wait_ge(w_part, 1)
            for c in range(DC):
                mm = pe.matmul(ring[RING - 1][:, 0:D], b1_wide[:, c, :], w_raw[2][:, c, :], start=(c == 0), stop=(c == DC - 1))
            mm.then_inc(b_ps, 1)
            pe.wait_ge(w_split, 1)
            with pe.Fori(0, (B - 2) // 2) as i:
                for j in range(2):
                    batch(2 * i + j, j, True)
            batch(B - 2, 0, True)
            batch(B - 1, 1, False)

        @block.vector
        def _(dve):
            done = 0

            def stepped(ins):
                nonlocal done
                ins.then_inc(w_part, 1)
                done += 1
                dve.wait_ge(w_part, done)

            def statistics(b, j, seen):
                dve.wait_ge(x_loaded[j], 16 * seen)
                dve.sem_inc(passed, 1)
                for t in range(T):
                    dve.bn_stats(stats[:, t, :], x_tok[j][:, t, :]).then_inc(stat_part, 1)
                dve.wait_ge(stat_part, (b + 1) * T)
                dve.sem_inc(passed, 1)
                for t in range(T):
                    dve.bn_aggr(mean_var[:, t, :], stats[:, t, :]).then_inc(stats_done, 1)

            def low_x(j, ps, i, at):
                ts = slice(2 * i * P, (2 * i + 2) * P)
                dve.wait_ge(high, at + 1)
                dve.tensor_tensor(zT_lo[j][:, :, ts], ps[:].rearrange("p (c n) -> p c n", c=DC),
                                  zT_hi[j][:, :, ts].bitcast(F32), ALU.subtract).then_inc(low, 1)

            def batch(b, j, has_x, has_load, seen):
                if has_x:
                    for n in range(X):
                        low_x(1 - j, bank(n, True), n, split(b, n, True))
                if has_load:
                    statistics(b + 2, j, seen + 1)
                dve.wait_ge(stored[j], 16 * NS * seen)
                for which, (hi, lo) in ((1, kT[j]), (0, qT[j])):
                    for k in range(KQ):
                        n = X + (1 - which) * KQ + k
                        m, s = k // 2, slice(k % 2 * HALF, (k % 2 + 1) * HALF)
                        dve.wait_ge(high, split(b, n, has_x) + 1)
                        dve.scalar_tensor_tensor(lo[:, m, s], bank(n, has_x)[:], bcol[:, which, m:m + 1],
                                                 hi[:, m, s].bitcast(F32), ALU.add, ALU.subtract).then_inc(low, 1)
                for k in range(V):
                    n = X + 2 * KQ + k
                    dve.wait_ge(full, fill(b, n, has_x) + 1)
                    dve.tensor_tensor(v[j][:, 2 * k:2 * k + 2, :, 0:HD],
                                      bank(n, has_x)[:].rearrange("p (t h d) -> p t h d", t=2, h=H),
                                      bv_row[:].rearrange("p (h d) -> p h d", h=H).unsqueeze(1).to_broadcast([P, 2, H, HD]),
                                      ALU.add).then_inc(low, 1)

            dve.sem_inc(low, RING)
            statistics(0, 0, 1)
            dve.wait_ge(rstd_done, 1)
            statistics(1, 1, 1)
            dve.wait_ge(w_in, 16 * NW)
            stepped(dve.tensor_copy(b1_wide[:], col[:, 1, :].unsqueeze(2).to_broadcast([P, DC, P])))
            for j in range(2):
                stepped(dve.memset(v[j][:, :, :, HD:HV], 1.0))
            dve.wait_ge(b_ps, 2)
            stepped(dve.tensor_tensor(bcol[:], ring[RING - 2][:, 0:2 * DC].rearrange("p (i c) -> p i c", i=2),
                                      col[:, 2:4, :], ALU.add))
            stepped(dve.tensor_scalar(bcol[:, 0, :], bcol[:, 0, :], SCALE, None, ALU.mult))
            stepped(dve.tensor_tensor(bv_row[:], ring[RING - 1][:, 0:D], bv_row[:], ALU.add))
            for i in range(3):
                for c in range(DC):
                    dve.tensor_scalar(w_raw[i][:, c, :], w_raw[i][:, c, :], col[:, 0, c:c + 1],
                                      SCALE if i == 0 else 1.0, ALU.mult, ALU.mult).then_inc(w_part, 1)
            dve.wait_ge(w_part, done + 3 * DC)
            dve.sem_inc(w_scaled, 1)
            dve.wait_ge(w_high, 3)
            for i in range(3):
                dve.tensor_tensor(w_lo[i][:], w_raw[i][:], w_hi[i][:].bitcast(F32), ALU.subtract).then_inc(w_part, 1)
            dve.wait_ge(w_part, done + 3 * DC + 3)
            dve.sem_inc(w_split, 1)
            for n in range(X):
                low_x(0, ring[n], n, n)
            with dve.Fori(0, (B - 2) // 2) as i:
                for j in range(2):
                    batch(2 * i + j, j, True, True, i + 1)
            batch(B - 2, 0, True, False, B // 2)
            batch(B - 1, 1, False, False, B // 2)


SHIFT_ON_ACT = (2, 4, 7)
SHIFT_ON_DVE = tuple(h for h in range(H) if h not in SHIFT_ON_ACT)


def heads_attend(nc, tag, x_in, x_out, adj, q_parts, k_parts, v_in, wo, bo, B, N):
    T = N // P
    G = B * T
    HALF = 512
    HT = T // 2
    nA, nD = len(SHIFT_ON_ACT), len(SHIFT_ON_DVE)

    with nc.cleanup_on_exit(), ExitStack() as ctx:
        def sb(name, shape, dt=F32):
            return ctx.enter_context(nc.sbuf_tensor(f"{tag}_{name}", shape, dt))

        def pb(name, shape):
            return ctx.enter_context(nc.psum_tensor(f"{tag}_{name}", shape, F32))

        def sem(name):
            return nc.alloc_semaphore(name=f"{tag}_{name}")

        q_tile = [sb(f"q_tile{j}", [P, H, P], F32R) for j in range(2)]
        k_stack = sb("k_stack", [P, 2, H, N], F32R)
        v = sb("v", [P, 2, T, H, HV])
        wo_raw, wo_hi, wo_lo = sb("wo_raw", [P, DC, D]), sb("wo_hi", [P, DC, D], F32R), sb("wo_lo", [P, DC, D], F32R)
        bo_row = sb("bo_row", [P, D])
        ident, tenth = sb("ident", [P, P]), sb("tenth", [P, 1])
        x_res = [sb(f"x_res{j}", [P, D]) for j in range(2)]
        x_new = [sb(f"x_new{j}", [P, D]) for j in range(2)]
        adj_sb = [sb(f"adj_sb{j}", [P, N], I32) for j in range(2)]
        bias = [sb(f"bias{j}", [P, N]) for j in range(2)]
        adj_f, edge, masked = sb("adj_f", [P, N]), sb("edge", [P, N]), sb("masked", [P, N])
        score = [sb(f"score{j}", [P, N]) for j in range(2)]
        prob = [sb(f"prob{j}", [P, T, P]) for j in range(2)]
        row_max = [sb(f"row_max{j}", [P, 1]) for j in range(2)]
        inv, att = sb("inv", [P, H, 1]), sb("att", [P, H, HD])
        attT_hi, attT_lo = sb("attT_hi", [P, DC, P], F32R), sb("attT_lo", [P, DC, P], F32R)

        ps_s = [pb(f"ps_s{j}", [P, N]) for j in range(2)]
        ps_t = pb("ps_t", [P, N])
        ps_o = [pb(f"ps_o{j}", [P, HALF]) for j in range(2)]

        names = ("w_in ready w_part w_split bias_part bias_made score_full taken shifted_d shifted_a turned exp_done "
                 "out_full inv_done att_done attT_full attT_high attT_low wo_full x_done res_ready kv_in passed")
        (w_in, ready, w_part, w_split, bias_part, bias_made, score_full, taken, shifted_d, shifted_a, turned, exp_done,
         out_full, inv_done, att_done, attT_full, attT_high, attT_low, wo_full, x_done, res_ready, kv_in, passed) = (
            sem(n) for n in names.split())
        first_k = [sem(f"first_k{c}") for c in range(HT)]
        adj_in, q_in, res_in, stored = ([sem(f"{n}{j}") for j in range(2)] for n in ("adj_in", "q_in", "res_in", "stored"))

        x_in_g = x_in.rearrange("b (t p) d -> (b t) p d", p=P)
        x_out_g = x_out.rearrange("b (t p) d -> (b t) p d", p=P)
        adj_g = adj.rearrange("b (t p) m -> (b t) p m", p=P)
        q_g = q_parts.rearrange("g s (h p) n -> g s p h n", h=H)
        k_b = k_parts.rearrange("b s (h p) n -> b s p h n", h=H)
        GT = G // 2
        KV = 16 * 5 * HT
        block = ctx.enter_context(nc.Block())

        @block.sync
        def _(sp):
            def load_q(g, j):
                for r, part in enumerate((0, 0, 1, 1)):
                    sp.dma_start(q_tile[j][32 * r:32 * r + 32, :, :].bitcast(F32), q_g[g, part]).then_inc(q_in[j], 16)

            def load_kv(b, slot, c):
                for r, part in enumerate((0, 1, 0, 1)):
                    sp.dma_start(k_stack[32 * r:32 * r + 32, slot, bass.ts(c, 2), :].bitcast(F32),
                                 k_b[b, part][:, bass.ts(c, 2), :]).then_inc(kv_in, 16)
                sp.dma_start(v[:, slot, bass.ts(c, 2)].rearrange("p t h d -> p (t h d)"),
                             v_in[b][:, bass.ts(c, 2 * H * HV)]).then_inc(kv_in, 16)

            def load_adj(g, j):
                sp.dma_start(adj_sb[j][:], adj_g[g]).then_inc(adj_in[j], 16)

            def load_residual(g, j):
                sp.dma_start(x_res[j][:], x_in_g[g]).then_inc(res_in[j], 16)

            def pair(i, last, kv=None):
                if kv is not None:
                    b, slot, c = kv
                    sp.wait_ge(out_full, b * T)
                    sp.wait_ge(kv_in, KV * (b + 1))
                    sp.sem_inc(passed, 1)
                    load_kv(b + 1, slot, c)
                if not last:
                    for j in range(2):
                        sp.wait_ge(bias_part, 4 * (2 * i + j) + 1)
                        load_adj(2 * i + j + 2, j)
                        sp.wait_ge(score_full, (2 * i + j + 1) * H)
                        load_q(2 * i + j + 2, j)
                for j in range(2):
                    sp.wait_ge(x_done, 2 * i + j + 1 + 2)
                    sp.dma_start(x_out_g[2 * i + j], x_new[j][:]).then_inc(stored[j], 16)
                    if not last:
                        load_residual(2 * i + j + 2, j)

            load_adj(0, 0)
            load_q(0, 0)
            sp.dma_start(wo_raw[:], wo.rearrange("(c p) n -> p c n", p=P)).then_inc(w_in, 16)
            sp.dma_start(bo_row[:], bo.partition_broadcast(P)).then_inc(w_in, 16)
            sp.dma_start(v[:, 0].rearrange("p t h d -> p (t h d)"), v_in[0]).then_inc(kv_in, 16)
            for c in range(HT):
                for r, part in enumerate((0, 1, 0, 1)):
                    sp.dma_start(k_stack[32 * r:32 * r + 32, 0, 2 * c:2 * c + 2, :].bitcast(F32),
                                 k_b[0, part][:, 2 * c:2 * c + 2, :]).then_inc(first_k[c], 16)
            load_adj(1, 1)
            load_q(1, 1)
            for j in range(2):
                load_residual(j, j)
                sp.sem_inc(stored[j], 16)
            sp.sem_inc(kv_in, KV - 16)
            sp.wait_ge(kv_in, KV)
            sp.sem_inc(passed, 1)
            for c in range(HT):
                load_kv(1, 1, c)
            with sp.Fori(0, HT) as i:
                pair(i, False)
            with sp.Fori(0, (B - 2) // 2) as bb:
                for k in range(2):
                    b = 2 * bb + 1 + k
                    with sp.Fori(0, HT) as i:
                        pair(b * HT + i, False, (b, k, i))
            with sp.Fori(0, HT - 1) as i:
                pair((B - 1) * HT + i, False)
            pair(GT - 1, True)
            for j in range(2):
                sp.wait_ge(stored[j], 16 * (GT + 1))

        @block.gpsimd
        def _(pool):
            pool.memset(ident[:], 0.0).then_inc(ready, 1)
            pool.memset(tenth[:], 0.1).then_inc(ready, 1)
            pool.wait_ge(ready, 2)
            pool.affine_select(out=ident[:], in_=ident[:], compare_op=ALU.not_equal, fill=1.0,
                               base=0, pattern=[[-1, P]], channel_multiplier=1).then_inc(ready, 1)

            def make_bias(g, j, seen):
                pool.wait_ge(adj_in[j], 16 * seen)
                pool.sem_inc(passed, 1)
                pool.tensor_copy(adj_f[:], adj_sb[j][:]).then_inc(bias_part, 1)
                pool.wait_ge(bias_part, 4 * g + 1)
                pool.tensor_tensor(edge[:], adj_f[:], tenth[:].to_broadcast([P, N]), ALU.mult).then_inc(bias_part, 1)
                pool.tensor_scalar(masked[:], adj_f[:], 0.0, -BIG, ALU.is_le, ALU.mult).then_inc(bias_part, 1)
                pool.wait_ge(bias_part, 4 * g + 3)
                pool.tensor_tensor(edge[:], edge[:], adj_f[:], ALU.mult).then_inc(bias_part, 1)
                pool.wait_ge(bias_part, 4 * g + 4)
                pool.wait_ge(taken, (g + 1) * H)
                pool.tensor_tensor(bias[j][:], edge[:], masked[:], ALU.add).then_inc(bias_made, 1)

            def residual(j, seen):
                pool.wait_ge(w_in, 16 * 2)
                pool.wait_ge(res_in[j], 16 * seen)
                pool.tensor_tensor(x_res[j][:], x_res[j][:], bo_row[:], ALU.add).then_inc(res_ready, 1)

            with pool.Fori(0, GT) as i:
                for j in range(2):
                    make_bias(2 * i + j, j, i + 1)
                    residual(j, i + 1)

        @block.scalar
        def _(act):
            def shift(g, h):
                act.wait_ge(taken, g * H + h + 1 + 2 * H)
                act.activation(score[h % 2][:], score[h % 2][:], ACT.Identity, bias=row_max[h % 2][:], scale=-1.0)\
                   .then_inc(shifted_a, 1)

            def exps(g, h):
                sign = -1.0 if h in SHIFT_ON_ACT else 1.0
                for k in range(2):
                    half = slice(k * T // 2, (k + 1) * T // 2)
                    act.wait_ge(turned, 2 * (g * H + h) + k + 1)
                    act.activation(prob[h % 2][:, half, :], ps_t[:, k * HALF:(k + 1) * HALF].rearrange("p (t n) -> p t n", n=P),
                                   ACT.Exp, scale=sign).then_inc(exp_done, 1)

            def att_split(g, j):
                act.wait_ge(attT_full, g + 1)
                act.activation(attT_hi[:], ps_o[j][:, 0:D].rearrange("p (c n) -> p c n", c=DC), ACT.Identity)\
                   .then_inc(attT_high, 1)

            def tile(g, j, first):
                for h in range(H):
                    exps(g, h)
                    if h + 1 in SHIFT_ON_ACT:
                        shift(g, h + 1)
                    if h == 3 and not first:
                        att_split(g - 1, 1 - j)

            act.sem_inc(exp_done, 2)
            tile(0, 0, True)
            tile(1, 1, False)
            with act.Fori(1, GT) as i:
                for j in range(2):
                    tile(2 * i + j, j, False)
            att_split(G - 1, 1)

        @block.tensor
        def _(pe):
            def three(out, l_hi, l_lo, r_hi, r_lo, n, last):
                pe.matmul(out, l_hi, r_hi, start=(n == 0), stop=False)
                pe.matmul(out, l_hi, r_lo, start=False, stop=False)
                return pe.matmul(out, l_lo, r_hi, start=False, stop=(n == last))

            def scores(h, j, slot):
                for k in range(2):
                    mm = pe.matmul(ps_s[h % 2][:, k * HALF:(k + 1) * HALF], q_tile[j][:, h, :],
                                   k_stack[:, slot, h, k * HALF:(k + 1) * HALF], start=True, stop=True)
                mm.then_inc(score_full, 1)

            def turn(g, h):
                if h in SHIFT_ON_ACT:
                    pe.wait_ge(shifted_a, g * nA + SHIFT_ON_ACT.index(h) + 1)
                else:
                    pe.wait_ge(shifted_d, g * nD + SHIFT_ON_DVE.index(h) + 1)
                for k in range(2):
                    pe.wait_ge(exp_done, 2 * (g * H + h) + k + 1)
                    for c in range(k * T // 2, (k + 1) * T // 2):
                        mm = pe.transpose(ps_t[:, c * P:(c + 1) * P], score[h % 2][:, c * P:(c + 1) * P], ident[:])
                    mm.then_inc(turned, 1)

            def weigh(g, h, j, slot):
                if h == 0:
                    pe.wait_ge(x_done, g + 1)
                for c in range(T):
                    if c % (T // 2) == 0:
                        pe.wait_ge(exp_done, 2 * (g * H + h) + 2 * c // T + 1 + 2)
                    mm = pe.matmul(ps_o[j][:, h * HV:(h + 1) * HV], prob[h % 2][:, c, :], v[:, slot, c, h, :],
                                   start=(c == 0), stop=(c == T - 1))
                if h == H - 1:
                    mm.then_inc(out_full, 1)

            def turn_att(g, j):
                pe.wait_ge(att_done, g + 1)
                for c in range(DC):
                    mm = pe.transpose(ps_o[j][:, c * P:(c + 1) * P], att[:].rearrange("p h d -> p (h d)")[:, c * P:(c + 1) * P],
                                      ident[:])
                mm.then_inc(attT_full, 1)

            def project_att(g, j):
                pe.wait_ge(attT_low, g + 1)
                for c in range(DC):
                    mm = three(ps_o[j][:, D:2 * D], attT_hi[:, c, :], attT_lo[:, c, :], wo_hi[:, c, :], wo_lo[:, c, :],
                               c, DC - 1)
                mm.then_inc(wo_full, 1)

            def tile(b, i, j, slot, prev, then):
                g = b * T + 2 * i + j
                for h in range(H):
                    turn(g, h)
                    if h + 2 < H:
                        if prev is None and h % 2 == 0:
                            pe.wait_ge(first_k[h // 2 + 1], 16 * 4)
                        scores(h + 2, j, slot)
                    elif then is not None:
                        if h + 2 == H:
                            pe.wait_ge(q_in[1 - j], 16 * 4 * (b * HT + i + j + 1))
                        scores(h + 2 - H, 1 - j, then)
                    if h > 0:
                        if prev is None and h == 1:
                            pe.wait_ge(kv_in, KV)
                        weigh(g, h - 1, j, slot)
                    elif prev is not None:
                        weigh(g - 1, H - 1, 1 - j, prev)
                    if prev is not None:
                        if h == 2:
                            turn_att(g - 1, 1 - j)
                        if h == 5:
                            project_att(g - 1, 1 - j)

            def batch(b, slot, first, last):
                tile(b, 0, 0, slot, None if first else 1 - slot, slot)
                with pe.Fori(0, HT - 1) as i:
                    tile(b, i, 1, slot, slot, slot)
                    tile(b, i + 1, 0, slot, slot, slot)
                if not last:
                    pe.wait_ge(kv_in, KV * (b + 2))
                tile(b, HT - 1, 1, slot, slot, None if last else 1 - slot)

            pe.wait_ge(ready, 3)
            pe.wait_ge(w_split, 1)
            pe.wait_ge(q_in[0], 16 * 4)
            pe.wait_ge(first_k[0], 16 * 4)
            scores(0, 0, 0)
            scores(1, 0, 0)
            batch(0, 0, True, False)
            if B > 2:
                with pe.Fori(0, (B - 2) // 2) as i:
                    batch(2 * i + 1, 1, False, False)
                    batch(2 * i + 2, 0, False, False)
            batch(B - 1, 1, False, True)
            weigh(G - 1, H - 1, 1, 1)
            turn_att(G - 1, 1)
            project_att(G - 1, 1)

        @block.vector
        def _(dve):
            dve.wait_ge(w_in, 16 * 2)
            dve.tensor_copy(wo_hi[:], wo_raw[:]).then_inc(w_part, 1)
            dve.wait_ge(w_part, 1)
            dve.tensor_tensor(wo_lo[:], wo_raw[:], wo_hi[:].bitcast(F32), ALU.subtract).then_inc(w_split, 1)
            dve.sem_inc(taken, 2 * H)
            dve.sem_inc(x_done, 2)

            def take(g, h, j):
                dve.wait_ge(score_full, g * H + h + 1)
                if h == 0:
                    dve.wait_ge(bias_made, g + 1)
                dve.sem_inc(passed, 1)
                dve.tensor_tensor_reduce(score[h % 2][:], ps_s[h % 2][:], bias[j][:], 1.0, -3.0e38, ALU.add, ALU.max,
                                         row_max[h % 2][:]).then_inc(taken, 1)
                if h not in SHIFT_ON_ACT:
                    dve.wait_ge(taken, g * H + h + 1 + 2 * H)
                    dve.tensor_scalar(score[h % 2][:], score[h % 2][:], row_max[h % 2][:], None, ALU.subtract)\
                       .then_inc(shifted_d, 1)

            def average(g, j):
                dve.wait_ge(out_full, g + 1)
                o = ps_o[j][:, 0:H * HV].rearrange("p (h d) -> p h d", h=H)
                dve.reciprocal(inv[:], o[:, :, HD:HV]).then_inc(inv_done, 1)
                dve.wait_ge(inv_done, g + 1)
                dve.tensor_tensor(att[:], o[:, :, 0:HD], inv[:].to_broadcast([P, H, HD]), ALU.mult).then_inc(att_done, 1)

            def att_low(g, j):
                dve.wait_ge(attT_high, g + 1)
                dve.tensor_tensor(attT_lo[:], ps_o[j][:, 0:D].rearrange("p (c n) -> p c n", c=DC),
                                  attT_hi[:].bitcast(F32), ALU.subtract).then_inc(attT_low, 1)

            def add_residual(g, j, seen):
                dve.wait_ge(stored[j], 16 * seen)
                dve.wait_ge(res_ready, g + 1)
                dve.wait_ge(wo_full, g + 1)
                dve.tensor_tensor(x_new[j][:], ps_o[j][:, D:2 * D], x_res[j][:], ALU.add).then_inc(x_done, 1)

            def tile(g, j, first, seen):
                for h in range(H):
                    take(g, h, j)
                    if not first:
                        if h == 2:
                            average(g - 1, 1 - j)
                        if h == 4:
                            att_low(g - 1, 1 - j)
                        if h == 7:
                            add_residual(g - 1, 1 - j, seen)

            tile(0, 0, True, 0)
            tile(1, 1, False, 1)
            with dve.Fori(1, GT) as i:
                tile(2 * i, 0, False, i)
                tile(2 * i + 1, 1, False, i + 1)
            average(G - 1, 1)
            att_low(G - 1, 1)
            add_residual(G - 1, 1, GT)


FW = 4 * D
FT = FW // P


def mlp_layer(nc, tag, x_in, x_out, g2, b2n, w1, b1, w2, b2, B, N):
    HALF = 512
    CT = HALF // P
    NC = B * N // HALF

    with nc.cleanup_on_exit(), ExitStack() as ctx:
        def sb(name, shape, dt=F32):
            return ctx.enter_context(nc.sbuf_tensor(f"{tag}_{name}", shape, dt))

        def pb(name, shape):
            return ctx.enter_context(nc.psum_tensor(f"{tag}_{name}", shape, F32))

        def sem(name):
            return nc.alloc_semaphore(name=f"{tag}_{name}")

        w1_raw, w2_raw = sb("w1_raw", [P, DC, FW]), sb("w2_raw", [P, FT, D])
        w1_hi, w1_lo = sb("w1_hi", [P, DC, FW], F32R), sb("w1_lo", [P, DC, FW], F32R)
        w2_hi, w2_lo = sb("w2_hi", [P, FT, D], F32R), sb("w2_lo", [P, FT, D], F32R)
        col = sb("col", [P, 2, DC])
        b1_col, b1_all = sb("b1_col", [P, FT]), sb("b1_all", [P, FT])
        b2_row = sb("b2_row", [P, D])
        ident, small = sb("ident", [P, P]), sb("small", [P, 3])
        x_c = [sb(f"x_c{j}", [P, CT, D]) for j in range(2)]
        x_new = [sb(f"x_new{j}", [P, CT, D]) for j in range(2)]
        z = sb("z", [P, CT, D])
        zT_hi, zT_lo = sb("zT_hi", [P, DC, HALF], F32R), sb("zT_lo", [P, DC, HALF], F32R)
        h = [sb(f"h{i}", [P, HALF]) for i in range(2)]
        h_hi, h_lo = sb("h_hi", [P, FT, HALF], F32R), sb("h_lo", [P, FT, HALF], F32R)
        stats, mean_var, ln_c = sb("stats", [P, CT, 6]), sb("mean_var", [P, CT, 2]), sb("ln_c", [P, 4, CT])

        ps_z = pb("ps_z", [P, DC, HALF])
        ps_h = [pb(f"ps_h{i}", [P, HALF]) for i in range(2)]
        ps_o = [pb(f"ps_o{i}", [P, HALF]) for i in range(2)]

        names = ("w_in ready w_part b_ps w_split w2_high w2_split stored z_full zT_high zT_low h_full h_gelu h_high h_low_d h_low_p "
                 "stat_part stats_done rstd_part rstd_done z_done res_done out_full x_done passed")
        (w_in, ready, w_part, b_ps, w_split, w2_high, w2_split, stored, z_full, zT_high, zT_low, h_full, h_gelu, h_high, h_low_d, h_low_p,
         stat_part, stats_done, rstd_part, rstd_done, z_done, res_done, out_full, x_done, passed) = (
            sem(n) for n in names.split())
        x_in_s = [sem(f"x_in{j}") for j in range(2)]

        xi = x_in.rearrange("b (c t p) d -> (b c) p t d", p=P, t=CT)
        xo = x_out.rearrange("b (c t p) d -> (b c) p t d", p=P, t=CT)
        block = ctx.enter_context(nc.Block())
        NP2 = NC // 2

        @block.sync
        def _(sp):
            sp.dma_start(w1_raw[:], w1.rearrange("(c p) n -> p c n", p=P)).then_inc(w_in, 16)
            sp.dma_start(w2_raw[:], w2.rearrange("(c p) n -> p c n", p=P)).then_inc(w_in, 16)
            for i, c in enumerate((g2, b2n)):
                sp.dma_start(col[:, i, :].unsqueeze(2), c.rearrange("(c p o) -> p c o", p=P, o=1),
                             allow_slow_non_contiguous=True).then_inc(w_in, 16)
            sp.dma_start(b1_col[:].unsqueeze(2), b1.rearrange("(c p o) -> p c o", p=P, o=1),
                         allow_slow_non_contiguous=True).then_inc(w_in, 16)
            sp.dma_start(b2_row[:], b2.partition_broadcast(P)).then_inc(w_in, 16)
            for j in range(2):
                sp.dma_start(x_c[j][:], xi[j]).then_inc(x_in_s[j], 16)
            sp.sem_inc(stored, 16 * 2)

            def store(c, j):
                sp.wait_ge(x_done, CT * (c + 1) + 2)
                sp.dma_start(xo[c], x_new[j][:]).then_inc(stored, 16)

            with sp.Fori(0, NP2 - 1) as i:
                for j in range(2):
                    store(2 * i + j, j)
                    sp.dma_start(x_c[j][:], xi[2 * i + 2 + j]).then_inc(x_in_s[j], 16)
            for j in range(2):
                store(NC - 2 + j, j)
            sp.wait_ge(stored, 16 * (NC + 2))

        @block.gpsimd
        def _(pool):
            pool.memset(ident[:], 0.0).then_inc(ready, 1)
            pool.memset(small[:, 0:1], -0.5).then_inc(ready, 1)
            pool.memset(small[:, 1:2], -1.0).then_inc(ready, 1)
            pool.memset(small[:, 2:3], EPS).then_inc(ready, 1)
            pool.wait_ge(ready, 4)
            pool.affine_select(out=ident[:], in_=ident[:], compare_op=ALU.not_equal, fill=1.0,
                               base=0, pattern=[[-1, P]], channel_multiplier=1).then_inc(ready, 1)
            pool.wait_ge(w_in, 16 * 6)
            pool.wait_ge(w2_high, 1)
            pool.tensor_tensor(w2_lo[:], w2_raw[:], w2_hi[:].bitcast(F32), ALU.subtract).then_inc(w2_split, 1)
            pool.sem_inc(h_low_p, 1)
            e = [small[:, k:k + 1].to_broadcast([P, CT]) for k in range(3)]

            def norm_consts(c):
                pool.wait_ge(stats_done, (c + 1) * CT)
                pool.tensor_tensor(ln_c[:, 0, :], mean_var[:, :, 1], e[2], ALU.add).then_inc(rstd_part, 1)
                pool.wait_ge(rstd_part, 3 * c + 1)
                pool.tensor_tensor(ln_c[:, 1, :], ln_c[:, 0, :], e[0], ALU.pow).then_inc(rstd_part, 1)
                pool.wait_ge(rstd_part, 3 * c + 2)
                pool.tensor_tensor(ln_c[:, 3, :], mean_var[:, :, 0], ln_c[:, 1, :], ALU.mult).then_inc(rstd_part, 1)
                pool.wait_ge(rstd_part, 3 * c + 3)
                pool.tensor_tensor(ln_c[:, 2, :], ln_c[:, 3, :], e[1], ALU.mult).then_inc(rstd_done, 1)

            def residual(c, j):
                pool.wait_ge(z_done, CT * (c + 1))
                pool.tensor_tensor(x_c[j][:], x_c[j][:], b2_row[:].unsqueeze(1).to_broadcast([P, CT, D]), ALU.add)\
                    .then_inc(res_done, 1)

            def chunk(c, j, last):
                for f in range(1, FT, 2):
                    pool.wait_ge(h_high, FT * c + f + 1)
                    pool.tensor_tensor(h_lo[:, f, :], h[f % 2][:], h_hi[:, f, :].bitcast(F32), ALU.subtract).then_inc(h_low_p, 1)
                    if f == 3 and not last:
                        norm_consts(c + 1)
                if not last:
                    residual(c + 1, 1 - j)

            norm_consts(0)
            residual(0, 0)
            with pool.Fori(0, NP2 - 1) as i:
                for j in range(2):
                    chunk(2 * i + j, j, False)
            chunk(NC - 2, 0, False)
            chunk(NC - 1, 1, True)

        @block.scalar
        def _(act):
            def normalise(c, j, tiles):
                for t in tiles:
                    act.wait_ge(rstd_done, c + 1)
                    act.sem_inc(passed, 1)
                    act.activation(z[:, t, :], x_c[j][:, t, :], ACT.Identity, bias=ln_c[:, 2, t:t + 1],
                                   scale=ln_c[:, 1, t:t + 1]).then_inc(z_done, 1)

            def split_high(c):
                for d in range(DC):
                    act.wait_ge(z_full, DC * c + d + 1)
                    act.activation(zT_hi[:, d, :], ps_z[:, d, :], ACT.Identity).then_inc(zT_high, 1)

            def chunk(c, j, last):
                for f in range(FT):
                    act.wait_ge(h_full, FT * c + f + 1)
                    act.wait_ge(h_low_p if f % 2 else h_low_d, FT // 2 * c + f // 2 + 1)
                    act.activation(h[f % 2][:], ps_h[f % 2][:], ACT.Gelu, bias=b1_all[:, f:f + 1]).then_inc(h_gelu, 1)
                if not last:
                    normalise(c + 1, 1 - j, range(CT))
                if not last:
                    split_high(c + 1)

            act.wait_ge(w_in, 16 * 6)
            act.activation(w2_hi[:], w2_raw[:], ACT.Identity).then_inc(w2_high, 1)
            act.wait_ge(w_split, 1)
            act.sem_inc(h_gelu, 2)
            normalise(0, 0, range(CT))
            split_high(0)
            with act.Fori(0, NP2 - 1) as i:
                for j in range(2):
                    chunk(2 * i + j, j, False)
            chunk(NC - 2, 0, False)
            chunk(NC - 1, 1, True)

        @block.tensor
        def _(pe):
            def three(out, l_hi, l_lo, r_hi, r_lo, n, last):
                pe.matmul(out, l_hi, r_hi, start=(n == 0), stop=False)
                pe.matmul(out, l_hi, r_lo, start=False, stop=False)
                return pe.matmul(out, l_lo, r_hi, start=False, stop=(n == last))

            pe.wait_ge(w_in, 16 * 6)
            for f in range(FT):
                for c in range(DC):
                    mm = pe.matmul(ps_h[0][:, f:f + 1], w1_raw[:, c, f * P:(f + 1) * P], col[:, 1, c:c + 1],
                                   start=(c == 0), stop=(c == DC - 1))
            mm.then_inc(b_ps, 1)
            pe.wait_ge(ready, 5)
            pe.wait_ge(w_split, 1)

            def turn(c):
                pe.wait_ge(z_done, CT * (c + 1))
                for d in range(DC):
                    for t in range(CT):
                        mm = pe.transpose(ps_z[:, d, t * P:(t + 1) * P], z[:, t, d * P:(d + 1) * P], ident[:])
                    mm.then_inc(z_full, 1)

            def chunk(c, j, last):
                pe.wait_ge(zT_low, DC * (c + 1))
                for f in range(FT):
                    pe.wait_ge(h_gelu, FT * c + f + 1)
                    for d in range(DC):
                        s = slice(f * P, (f + 1) * P)
                        mm = three(ps_h[f % 2][:], w1_hi[:, d, s], w1_lo[:, d, s], zT_hi[:, d, :], zT_lo[:, d, :], d, DC - 1)
                    mm.then_inc(h_full, 1)
                for t in range(CT):
                    if t == 1 and not last:
                        turn(c + 1)
                    pe.wait_ge(x_done, CT * c + t + 1)
                    s = slice(t * P, (t + 1) * P)
                    for f in range(FT):
                        if t == 0:
                            pe.wait_ge(h_low_p if f % 2 else h_low_d, FT // 2 * c + f // 2 + 1 + 1)
                        mm = three(ps_o[t % 2][:, 0:D], h_hi[:, f, s], h_lo[:, f, s], w2_hi[:, f, :], w2_lo[:, f, :], f, FT - 1)
                    mm.then_inc(out_full, 1)

            turn(0)
            pe.wait_ge(w2_split, 1)
            pe.sem_inc(passed, 1)
            with pe.Fori(0, NP2 - 1) as i:
                for j in range(2):
                    chunk(2 * i + j, j, False)
            chunk(NC - 2, 0, False)
            chunk(NC - 1, 1, True)

        @block.vector
        def _(dve):
            k = 0

            def stepped(ins):
                nonlocal k
                ins.then_inc(w_part, 1)
                k += 1
                dve.wait_ge(w_part, k)

            dve.wait_ge(w_in, 16 * 6)
            dve.wait_ge(b_ps, 1)
            stepped(dve.tensor_tensor(b1_all[:], ps_h[0][:, 0:FT], b1_col[:], ALU.add))
            for c in range(DC):
                stepped(dve.tensor_scalar(w1_raw[:, c, :], w1_raw[:, c, :], col[:, 0, c:c + 1], None, ALU.mult))
            stepped(dve.tensor_copy(w1_hi[:], w1_raw[:]))
            stepped(dve.tensor_tensor(w1_lo[:], w1_raw[:], w1_hi[:].bitcast(F32), ALU.subtract))
            dve.sem_inc(w_split, 1)
            dve.sem_inc(x_done, 2)
            dve.sem_inc(h_low_d, 1)

            def statistics(c, j, seen, tiles):
                dve.wait_ge(x_in_s[j], 16 * seen)
                dve.sem_inc(passed, 1)
                for t in tiles:
                    dve.bn_stats(stats[:, t, :], x_c[j][:, t, :]).then_inc(stat_part, 1)

            def aggregate(c):
                dve.wait_ge(stat_part, (c + 1) * CT)
                dve.sem_inc(passed, 1)
                for t in range(CT):
                    dve.bn_aggr(mean_var[:, t, :], stats[:, t, :]).then_inc(stats_done, 1)

            def split_low(c):
                for d in range(DC):
                    dve.wait_ge(zT_high, DC * c + d + 1)
                    dve.tensor_tensor(zT_lo[:, d, :], ps_z[:, d, :], zT_hi[:, d, :].bitcast(F32), ALU.subtract)\
                       .then_inc(zT_low, 1)

            def chunk(c, j, last, seen):
                for f in range(FT):
                    if not last and f in (2, 3):
                        statistics(c + 1, 1 - j, seen, range((f - 2) * CT // 2, (f - 1) * CT // 2))
                    if not last and f == 4:
                        aggregate(c + 1)
                    dve.wait_ge(h_gelu, FT * c + f + 1 + 2)
                    dve.tensor_copy(h_hi[:, f, :], h[f % 2][:]).then_inc(h_high, 1)
                    if f % 2 == 0:
                        dve.wait_ge(h_high, FT * c + f + 1)
                        dve.tensor_tensor(h_lo[:, f, :], h[f % 2][:], h_hi[:, f, :].bitcast(F32), ALU.subtract)\
                           .then_inc(h_low_d, 1)
                dve.wait_ge(stored, 16 * (c + 1))
                dve.wait_ge(res_done, c + 1)
                dve.sem_inc(passed, 1)
                for t in range(CT):
                    if t == 1 and not last:
                        split_low(c + 1)
                    dve.wait_ge(out_full, CT * c + t + 1)
                    dve.tensor_tensor(x_new[j][:, t, :], ps_o[t % 2][:, 0:D], x_c[j][:, t, :], ALU.add).then_inc(x_done, 1)

            statistics(0, 0, 1, range(CT))
            aggregate(0)
            split_low(0)
            with dve.Fori(0, NP2 - 1) as i:
                chunk(2 * i, 0, False, i + 1)
                chunk(2 * i + 1, 1, False, i + 2)
            chunk(NC - 2, 0, False, NP2)
            chunk(NC - 1, 1, True, NP2 + 1)


def graph_net(nc, x, adj, adj_turned, ln1_g, ln1_b, ln2_g, ln2_b, wq0, bq0, wk0, bk0, wv0, bv0, wo0, bo0, w1, b1, w2, b2,
              w_dir, b_dir, gamma1, beta1, wq2, wk2, wv2, wo2, bo2, gamma2, beta2, wq3, bq3, wk3, bk3, wc3, gamma3, beta3,
              out):
    B, N, _ = x.shape
    mid = [nc.dram_tensor(f"x_layer{i}", [B, N, D], F32).ap() for i in range(5)]
    q_parts = nc.dram_tensor("q_parts", [B * N // P, 2, D, P], F32).ap()
    k_parts = nc.dram_tensor("k_parts", [B, 2, D, N], F32).ap()
    v_heads = nc.dram_tensor("v_heads", [B, P, N // P * H * HV], F32).ap()
    heads_project(nc, "proj", x, q_parts, k_parts, v_heads, ln1_g, ln1_b, wq0, bq0, wk0, bk0, wv0, bv0, B, N)
    heads_attend(nc, "heads", x, mid[0], adj, q_parts, k_parts, v_heads, wo0, bo0, B, N)
    mlp_layer(nc, "mlp", mid[0], mid[1], ln2_g, ln2_b, w1, b1, w2, b2, B, N)
    direction_layer(nc, "dir", mid[1], mid[2], adj_turned, w_dir, b_dir, gamma1, beta1, B, N)
    attention_layer(nc, "fold", mid[2], mid[3], adj, wq2, wk2, wv2, wo2, None, None, bo2, gamma2, beta2,
                    float(D) ** -0.5, B, N)
    L, _, F = wq3.shape
    for k in range(L):
        attention_layer(nc, f"att{k}", mid[3 + k], out if k == L - 1 else mid[4 + k], adj, wq3[k], wk3[k], wc3[k], None,
                        bq3[k], bk3[k], None, gamma3[k], beta3[k], float(F) ** -0.5, B, N)


_INS = ["x", "adj", "adj_turned", "L0_gnn_ln1_g", "L0_gnn_ln1_b", "L0_gnn_ln2_g", "L0_gnn_ln2_b",
        "L0_gnn_wq", "L0_gnn_bq", "L0_gnn_wk", "L0_gnn_bk", "L0_gnn_wv", "L0_gnn_bv", "L0_gnn_wo", "L0_gnn_bo",
        "L0_gnn_w1", "L0_gnn_b1", "L0_gnn_w2", "L0_gnn_b2", "L1_gnn_W", "L1_gnn_b", "L1_gnn_gamma", "L1_gnn_beta",
        "L2_gnn_Wq", "L2_gnn_Wk", "L2_gnn_Wv", "L2_gnn_Wo", "L2_gnn_bo", "L2_gnn_gamma", "L2_gnn_beta",
        "L3_gnn_Wq", "L3_gnn_bq", "L3_gnn_Wk", "L3_gnn_bk", "L3_gnn_Wc", "L3_gnn_ln_g", "L3_gnn_ln_b"]


def kernel(**inputs):
    import numpy as _np
    import concourse.bacc as _bacc
    from concourse import mybir as _mybir
    from concourse.bass_utils import run_bass_kernel_spmd as _run

    data = dict(inputs)
    adj = _np.asarray(data["adj"])
    B, N, _ = adj.shape
    data["adj_turned"] = adj.reshape(B, N // 128, 128, N // 128, 128).transpose(0, 1, 4, 3, 2)
    for name in ("L2_gnn_Wq", "L2_gnn_Wk", "L2_gnn_Wv"):
        data[name] = _np.asarray(data[name]).T
    for name in ("L3_gnn_Wq", "L3_gnn_Wk", "L3_gnn_Wc"):
        data[name] = _np.asarray(data[name]).transpose(0, 2, 1)

    nc = _bacc.Bacc("TRN2", target_bir_lowering=False, num_devices=1)
    arrays, args = {}, []
    for name in _INS:
        a = _np.ascontiguousarray(data[name])
        arrays[f"in_{name}_dram"] = a
        args.append(nc.dram_tensor(f"in_{name}_dram", a.shape, _mybir.dt.from_np(a.dtype), kind="ExternalInput").ap())
    args.append(nc.dram_tensor("out_0_dram", data["x"].shape, _mybir.dt.float32, kind="ExternalOutput").ap())
    graph_net(nc, *args)
    r = _run(nc, [arrays], core_ids=[0])
    return r.results[0]["out_0_dram"]
```
